# Optimizing a Trainium2 kernel written in Bass

```python
import numpy as np
import jax
import jax.numpy as jnp

def _softmax(x, axis=-1):
    return jax.nn.softmax(x, axis=axis)

def _gelu(x):
    return jax.nn.gelu(x, approximate=True)

def _silu(x):
    return jax.nn.silu(x)

def _sigmoid(x):
    return jax.nn.sigmoid(x)

def _layernorm(x, axis=-1, eps=1e-05):
    m = jnp.mean(x, axis=axis, keepdims=True)
    v = jnp.var(x, axis=axis, keepdims=True)
    return (x - m) / jnp.sqrt(v + eps)

def _scatter_add(tgt, idx, src, axis=0):
    return tgt.at[idx].add(src)

def _segment_sum(src, seg, n):
    return jax.ops.segment_sum(src, seg, n)
kernel_name = 'mk_flamingo_gated_d2_seqx_r4_6d6212'

def setup_inputs(seed: int=0):
    np.random.seed(seed)
    _w = jnp.asarray

    def _rec_inputs():
        import jax
        import jax.numpy as jnp
        _rk = jax.random.key(seed)
        x = 7.22e-05 + 1 * jax.random.normal(jax.random.fold_in(_rk, 1), (32, 100, 256), jnp.float32)
        _lenS = 100 - jax.random.randint(jax.random.fold_in(_rk, 7), (32,), 0, max(1, 100 // 4) + 1, jnp.int32)
        _lenS2 = 361 - jax.random.randint(jax.random.fold_in(_rk, 8), (32,), 0, max(1, 361 // 4) + 1, jnp.int32)
        _ctx_1024P = jax.random.normal(jax.random.fold_in(_rk, 11), (32, 16, 256), jnp.float32)
        _ctx_1024c = jax.random.dirichlet(jax.random.fold_in(_rk, 511), 0.3 * jnp.ones((16,), jnp.float32), (32, 361))
        _ctx_1024t = jnp.einsum('bsk,bkd->bsd', _ctx_1024c, _ctx_1024P)
        _ctx_1024t = _ctx_1024t * jax.lax.rsqrt(jnp.mean(jnp.square(_ctx_1024t)) + 1e-12) * 0.953939
        ctx_1024 = 4.13588e-05 + 0.999923 * (_ctx_1024t + 0.3 * jax.random.normal(jax.random.fold_in(_rk, 611), (32, 361, 256), jnp.float32))
        _g = jax.random.normal(jax.random.fold_in(_rk, 9001), (2, 2), jnp.float32)
        _g = jnp.sign(_g) * jnp.maximum(jnp.abs(_g), 1.0) + (_g == 0) * 1.0
        g_xattn = _g[0]
        g_ffn = _g[1]
        return (x, ctx_1024, g_xattn, g_ffn)
    x, ctx_1024, g_xattn, g_ffn = _rec_inputs()

    def _L0_xattn_setup():
        import jax, jax.numpy as jnp
        import numpy as np
        DIM = 256
        HEADS = 16
        HEAD_DIM = DIM // HEADS
        key = jax.random.key(seed)
        ks = jax.random.split(key, 11)
        B, Sq, Skv = (4, 512, 512)
        s = 1.0 / np.sqrt(DIM)
        return {'query': jax.random.normal(ks[0], (B, Sq, DIM), jnp.float32), 'key': jax.random.normal(ks[1], (B, Skv, DIM), jnp.float32), 'value': jax.random.normal(ks[2], (B, Skv, DIM), jnp.float32), 'Wq': jax.random.normal(ks[3], (DIM, DIM), jnp.float32) * s, 'bq': jnp.zeros((DIM,), jnp.float32), 'Wk': jax.random.normal(ks[4], (DIM, DIM), jnp.float32) * s, 'bk': jnp.zeros((DIM,), jnp.float32), 'Wv': jax.random.normal(ks[5], (DIM, DIM), jnp.float32) * s, 'bv': jnp.zeros((DIM,), jnp.float32), 'Wo': jax.random.normal(ks[6], (DIM, DIM), jnp.float32) * s, 'bo': jnp.zeros((DIM,), jnp.float32)}
    _L0_xattn_all = _L0_xattn_setup()
    _L0_xattn_in = {k: v for k, v in _L0_xattn_all.items() if k in ('Wq', 'bq', 'Wk', 'bk', 'Wv', 'bv', 'Wo', 'bo')}
    del _L0_xattn_all

    def _L0_ffn_setup():
        import jax, jax.numpy as jnp
        import numpy as np
        E, D, TOP_K = (8, 128, 2)
        EPS_NORM, EPS_COS = (1e-12, 1e-08)

        def _l2norm(v, eps):
            return v / jnp.maximum(jnp.linalg.norm(v, axis=-1, keepdims=True), eps)

        def _mlp(x, gw, uw, dw):
            return jax.nn.silu(x @ gw.T) * (x @ uw.T) @ dw.T
        key = jax.random.key(seed)
        ks = jax.random.split(key, 12)
        B, S, H, F_ = (2, 512, 256, 512)
        G = E * D
        w = lambda k, shp: jax.random.normal(k, shp, dtype=jnp.float32) * 0.02
        return {'hidden_states': jax.random.normal(ks[0], (B, S, H), dtype=jnp.float32), 'gru_w_ih': w(ks[1], (3 * G, H)), 'gru_w_hh': w(ks[2], (3 * G, G)), 'expr_w': w(ks[3], (G, H)), 'ctx_w': w(ks[4], (G, H)), 'ctx_b': jnp.zeros((G,), dtype=jnp.float32), 'gate_w': w(ks[5], (E, F_, H)), 'up_w': w(ks[6], (E, F_, H)), 'down_w': w(ks[7], (E, H, F_)), 'shared_gate_w': w(ks[8], (F_, H)), 'shared_up_w': w(ks[9], (F_, H)), 'shared_down_w': w(ks[10], (H, F_))}
    _L0_ffn_all = _L0_ffn_setup()
    _L0_ffn_in = {k: v for k, v in _L0_ffn_all.items() if k in ('gru_w_ih', 'gru_w_hh', 'expr_w', 'ctx_w', 'ctx_b', 'gate_w', 'up_w', 'down_w', 'shared_gate_w', 'shared_up_w', 'shared_down_w')}
    del _L0_ffn_all

    def _L1_xattn_setup():
        import jax, jax.numpy as jnp
        import numpy as np
        from jax import lax
        BIG = jnp.float32(1e+30)

        def _pairwise_euclidean(a, b):
            aa = jnp.sum(a * a, axis=-1)[:, None]
            bb = jnp.sum(b * b, axis=-1)[None, :]
            ab = a @ b.T
            return jnp.sqrt(jnp.maximum(aa + bb - 2.0 * ab, 0.0))

        def _dtw_cost(D):
            row0 = jnp.cumsum(D[0])

            def row_step(prev_row, d_row):
                first = d_row[0] + prev_row[0]

                def col_step(left, inp):
                    d_ij, up, diag = inp
                    r = d_ij + jnp.minimum(jnp.minimum(up, left), diag)
                    return (r, r)
                _, rest = lax.scan(col_step, first, (d_row[1:], prev_row[1:], prev_row[:-1]))
                row = jnp.concatenate([first[None], rest])
                return (row, row)
            _, rows = lax.scan(row_step, row0, D[1:])
            return jnp.concatenate([row0[None], rows], axis=0)

        def _backtrack(R, T1, T2):
            L = T1 + T2 - 1

            def step(carry, _):
                i, j, done = carry
                valid = jnp.logical_not(done)
                cd = jnp.where((i > 0) & (j > 0), R[jnp.maximum(i - 1, 0), jnp.maximum(j - 1, 0)], BIG)
                cu = jnp.where(i > 0, R[jnp.maximum(i - 1, 0), j], BIG)
                cl = jnp.where(j > 0, R[i, jnp.maximum(j - 1, 0)], BIG)
                choice = jnp.argmin(jnp.stack([cd, cu, cl]))
                ni = jnp.where(choice <= 1, i - 1, i)
                nj = jnp.where((choice == 0) | (choice == 2), j - 1, j)
                at_origin = (i == 0) & (j == 0)
                ni = jnp.where(at_origin, 0, ni)
                nj = jnp.where(at_origin, 0, nj)
                return ((ni, nj, done | at_origin), (i, j, valid))
            init = (jnp.int32(T1 - 1), jnp.int32(T2 - 1), jnp.bool_(False))
            _, (i_idx, j_idx, valid) = lax.scan(step, init, None, length=L)
            return (i_idx, j_idx, valid)

        def _align_one(small, large):
            T_small, d = small.shape
            T_large = large.shape[0]
            D = _pairwise_euclidean(small, large)
            R = _dtw_cost(D)
            i_idx, j_idx, valid = _backtrack(R, T_small, T_large)
            contrib = small[i_idx] * valid[:, None].astype(small.dtype)
            expanded = jnp.zeros((T_large, d), dtype=small.dtype).at[j_idx].add(contrib)
            return expanded
        key = jax.random.key(seed)
        k1, k2 = jax.random.split(key)
        teacher = jax.random.normal(k1, (16, 100, 256), dtype=jnp.float32)
        student = jax.random.normal(k2, (16, 150, 256), dtype=jnp.float32)
        return {'teacher_features': teacher, 'student_features': student}
    _L1_xattn_all = _L1_xattn_setup()
    _L1_xattn_in = {k: v for k, v in _L1_xattn_all.items() if k in ()}
    del _L1_xattn_all

    def _L1_ffn_setup():
        import jax, jax.numpy as jnp
        import numpy as np
        MIN_EXPERT_CAPACITY = 4
        CAPACITY_FACTOR = 1.0

        def _moe_forward(x, router_w, w1, b1, w2, b2):
            B, S, D = x.shape
            E = router_w.shape[1]
            G = 1
            T = B * S
            C = max(int(round(CAPACITY_FACTOR * T / E)), MIN_EXPERT_CAPACITY)
            xt = x.reshape(G, T, D)
            logits = jnp.einsum('gtd,de->gte', xt, router_w)
            probs = jax.nn.softmax(logits, axis=-1)
            gate = jnp.max(probs, axis=-1)
            idx = jnp.argmax(probs, axis=-1)
            emask = jax.nn.one_hot(idx, E, dtype=x.dtype)
            pos = jnp.cumsum(emask, axis=1) * emask - 1.0
            pos = pos.astype(jnp.int32)
            slot = jax.nn.one_hot(pos, C, dtype=x.dtype)
            dispatch = emask[..., None] * slot
            combine = dispatch * gate[..., None, None]
            expert_inputs = jnp.einsum('gtd,gtec->gecd', xt, dispatch)
            h = jax.nn.relu(jnp.einsum('gecd,edf->gecf', expert_inputs, w1) + b1[None, :, None, :])
            expert_outputs = jnp.einsum('gecf,efd->gecd', h, w2) + b2[None, :, None, :]
            out = jnp.einsum('gecd,gtec->gtd', expert_outputs, combine)
            return out.reshape(B, S, D)
        key = jax.random.key(seed)
        k0, k1, k2, k3 = jax.random.split(key, 4)
        B, S, D, E, F = (4, 512, 256, 8, 1024)
        x = jax.random.normal(k0, (B, S, D), dtype=jnp.float32)
        router_w = jax.random.normal(k1, (D, E), dtype=jnp.float32) * D ** (-0.5)
        w1 = jax.random.normal(k2, (E, D, F), dtype=jnp.float32) * D ** (-0.5)
        b1 = jnp.zeros((E, F), dtype=jnp.float32)
        w2 = jax.random.normal(k3, (E, F, D), dtype=jnp.float32) * F ** (-0.5)
        b2 = jnp.zeros((E, D), dtype=jnp.float32)
        return {'x': x, 'router_w': router_w, 'w1': w1, 'b1': b1, 'w2': w2, 'b2': b2}
    _L1_ffn_all = _L1_ffn_setup()
    _L1_ffn_in = {k: v for k, v in _L1_ffn_all.items() if k in ('router_w', 'w1', 'b1', 'w2', 'b2')}
    del _L1_ffn_all
    return {'x': x, 'ctx_1024': ctx_1024, 'g_xattn': g_xattn, 'g_ffn': g_ffn, 'L0_xattn_Wq': _L0_xattn_in['Wq'], 'L0_xattn_bq': _L0_xattn_in['bq'], 'L0_xattn_Wk': _L0_xattn_in['Wk'], 'L0_xattn_bk': _L0_xattn_in['bk'], 'L0_xattn_Wv': _L0_xattn_in['Wv'], 'L0_xattn_bv': _L0_xattn_in['bv'], 'L0_xattn_Wo': _L0_xattn_in['Wo'], 'L0_xattn_bo': _L0_xattn_in['bo'], 'L0_ffn_gru_w_ih': _L0_ffn_in['gru_w_ih'], 'L0_ffn_gru_w_hh': _L0_ffn_in['gru_w_hh'], 'L0_ffn_expr_w': _L0_ffn_in['expr_w'], 'L0_ffn_ctx_w': _L0_ffn_in['ctx_w'], 'L0_ffn_ctx_b': _L0_ffn_in['ctx_b'], 'L0_ffn_gate_w': _L0_ffn_in['gate_w'], 'L0_ffn_up_w': _L0_ffn_in['up_w'], 'L0_ffn_down_w': _L0_ffn_in['down_w'], 'L0_ffn_shared_gate_w': _L0_ffn_in['shared_gate_w'], 'L0_ffn_shared_up_w': _L0_ffn_in['shared_up_w'], 'L0_ffn_shared_down_w': _L0_ffn_in['shared_down_w'], 'L1_ffn_router_w': _L1_ffn_in['router_w'], 'L1_ffn_w1': _L1_ffn_in['w1'], 'L1_ffn_b1': _L1_ffn_in['b1'], 'L1_ffn_w2': _L1_ffn_in['w2'], 'L1_ffn_b2': _L1_ffn_in['b2']}

def reference(x, ctx_1024, g_xattn, g_ffn, L0_xattn_Wq, L0_xattn_bq, L0_xattn_Wk, L0_xattn_bk, L0_xattn_Wv, L0_xattn_bv, L0_xattn_Wo, L0_xattn_bo, L0_ffn_gru_w_ih, L0_ffn_gru_w_hh, L0_ffn_expr_w, L0_ffn_ctx_w, L0_ffn_ctx_b, L0_ffn_gate_w, L0_ffn_up_w, L0_ffn_down_w, L0_ffn_shared_gate_w, L0_ffn_shared_up_w, L0_ffn_shared_down_w, L1_ffn_router_w, L1_ffn_w1, L1_ffn_b1, L1_ffn_w2, L1_ffn_b2):
    import jax
    import jax.numpy as jnp

    def _L0_xattn_ref(query, key, value, Wq, bq, Wk, bk, Wv, bv, Wo, bo):
        import jax, jax.numpy as jnp
        import numpy as np
        DIM = 256
        HEADS = 16
        HEAD_DIM = DIM // HEADS
        B = query.shape[0]
        scale = HEAD_DIM ** (-0.5)
        q = (query @ Wq.T + bq).reshape(B, -1, HEADS, HEAD_DIM)
        k = (key @ Wk.T + bk).reshape(B, -1, HEADS, HEAD_DIM)
        v = (value @ Wv.T + bv).reshape(B, -1, HEADS, HEAD_DIM)
        scores = jnp.einsum('bqhd,bkhd->bhqk', q, k) * scale
        attn = jax.nn.softmax(scores, axis=-1)
        out = jnp.einsum('bhqk,bkhd->bqhd', attn, v).reshape(B, -1, DIM)
        return out @ Wo.T + bo

    def _L0_ffn_ref(hidden_states, gru_w_ih, gru_w_hh, expr_w, ctx_w, ctx_b, gate_w, up_w, down_w, shared_gate_w, shared_up_w, shared_down_w):
        import jax, jax.numpy as jnp
        import numpy as np
        E, D, TOP_K = (8, 128, 2)
        EPS_NORM, EPS_COS = (1e-12, 1e-08)

        def _l2norm(v, eps):
            return v / jnp.maximum(jnp.linalg.norm(v, axis=-1, keepdims=True), eps)

        def _mlp(x, gw, uw, dw):
            return jax.nn.silu(x @ gw.T) * (x @ uw.T) @ dw.T
        B, S, H = hidden_states.shape
        h0 = hidden_states.mean(axis=1) @ ctx_w.T + ctx_b
        xw = hidden_states @ gru_w_ih.T

        def step(h, xw_t):
            hw = h @ gru_w_hh.T
            xr, xz, xn = jnp.split(xw_t, 3, axis=-1)
            hr, hz, hnn = jnp.split(hw, 3, axis=-1)
            r = jax.nn.sigmoid(xr + hr)
            z = jax.nn.sigmoid(xz + hz)
            n = jnp.tanh(xn + r * hnn)
            h_new = (1.0 - z) * n + z * h
            return (h_new, h_new)
        _, hs = jax.lax.scan(step, h0, jnp.swapaxes(xw, 0, 1))
        routing = jnp.swapaxes(hs, 0, 1).reshape(B, S, E, D)
        routing = _l2norm(routing, EPS_NORM)
        expr = (hidden_states @ expr_w.T).reshape(B, S, E, D)
        gram = jnp.einsum('bsed,bsfd->bsef', routing, routing)
        diff = gram - jnp.eye(E, dtype=routing.dtype)
        diff_n = _l2norm(diff, EPS_NORM)
        penalty = jnp.mean(jnp.sum(diff_n ** 2, axis=(-2, -1)))
        num = jnp.sum(expr * routing, axis=-1)
        den = jnp.maximum(jnp.linalg.norm(expr, axis=-1), EPS_COS) * jnp.maximum(jnp.linalg.norm(routing, axis=-1), EPS_COS)
        cos_dist = 1.0 - num / den
        scores = (cos_dist * (1.0 + penalty)).reshape(B * S, E)
        top_v, top_i = jax.lax.top_k(scores, TOP_K)
        mult = jax.nn.softmax(top_v, axis=-1)
        onehot = jax.nn.one_hot(top_i, E, dtype=mult.dtype)
        cw = jnp.einsum('tk,tke->te', mult, onehot)
        xf = hidden_states.reshape(B * S, H)
        out = jnp.zeros_like(xf)
        for e in range(E):
            out = out + cw[:, e:e + 1] * _mlp(xf, gate_w[e], up_w[e], down_w[e])
        moe = out.reshape(B, S, H)
        shared = jax.lax.stop_gradient(_mlp(hidden_states, shared_gate_w, shared_up_w, shared_down_w))
        return moe + shared

    def _L1_xattn_ref(teacher_features, student_features):
        import jax, jax.numpy as jnp
        import numpy as np
        from jax import lax
        BIG = jnp.float32(1e+30)

        def _pairwise_euclidean(a, b):
            aa = jnp.sum(a * a, axis=-1)[:, None]
            bb = jnp.sum(b * b, axis=-1)[None, :]
            ab = a @ b.T
            return jnp.sqrt(jnp.maximum(aa + bb - 2.0 * ab, 0.0))

        def _dtw_cost(D):
            row0 = jnp.cumsum(D[0])

            def row_step(prev_row, d_row):
                first = d_row[0] + prev_row[0]

                def col_step(left, inp):
                    d_ij, up, diag = inp
                    r = d_ij + jnp.minimum(jnp.minimum(up, left), diag)
                    return (r, r)
                _, rest = lax.scan(col_step, first, (d_row[1:], prev_row[1:], prev_row[:-1]))
                row = jnp.concatenate([first[None], rest])
                return (row, row)
            _, rows = lax.scan(row_step, row0, D[1:])
            return jnp.concatenate([row0[None], rows], axis=0)

        def _backtrack(R, T1, T2):
            L = T1 + T2 - 1

            def step(carry, _):
                i, j, done = carry
                valid = jnp.logical_not(done)
                cd = jnp.where((i > 0) & (j > 0), R[jnp.maximum(i - 1, 0), jnp.maximum(j - 1, 0)], BIG)
                cu = jnp.where(i > 0, R[jnp.maximum(i - 1, 0), j], BIG)
                cl = jnp.where(j > 0, R[i, jnp.maximum(j - 1, 0)], BIG)
                choice = jnp.argmin(jnp.stack([cd, cu, cl]))
                ni = jnp.where(choice <= 1, i - 1, i)
                nj = jnp.where((choice == 0) | (choice == 2), j - 1, j)
                at_origin = (i == 0) & (j == 0)
                ni = jnp.where(at_origin, 0, ni)
                nj = jnp.where(at_origin, 0, nj)
                return ((ni, nj, done | at_origin), (i, j, valid))
            init = (jnp.int32(T1 - 1), jnp.int32(T2 - 1), jnp.bool_(False))
            _, (i_idx, j_idx, valid) = lax.scan(step, init, None, length=L)
            return (i_idx, j_idx, valid)

        def _align_one(small, large):
            T_small, d = small.shape
            T_large = large.shape[0]
            D = _pairwise_euclidean(small, large)
            R = _dtw_cost(D)
            i_idx, j_idx, valid = _backtrack(R, T_small, T_large)
            contrib = small[i_idx] * valid[:, None].astype(small.dtype)
            expanded = jnp.zeros((T_large, d), dtype=small.dtype).at[j_idx].add(contrib)
            return expanded
        return jax.vmap(_align_one)(teacher_features, student_features)

    def _L1_ffn_ref(x, router_w, w1, b1, w2, b2):
        import jax, jax.numpy as jnp
        import numpy as np
        MIN_EXPERT_CAPACITY = 4
        CAPACITY_FACTOR = 1.0

        def _moe_forward(x, router_w, w1, b1, w2, b2):
            B, S, D = x.shape
            E = router_w.shape[1]
            G = 1
            T = B * S
            C = max(int(round(CAPACITY_FACTOR * T / E)), MIN_EXPERT_CAPACITY)
            xt = x.reshape(G, T, D)
            logits = jnp.einsum('gtd,de->gte', xt, router_w)
            probs = jax.nn.softmax(logits, axis=-1)
            gate = jnp.max(probs, axis=-1)
            idx = jnp.argmax(probs, axis=-1)
            emask = jax.nn.one_hot(idx, E, dtype=x.dtype)
            pos = jnp.cumsum(emask, axis=1) * emask - 1.0
            pos = pos.astype(jnp.int32)
            slot = jax.nn.one_hot(pos, C, dtype=x.dtype)
            dispatch = emask[..., None] * slot
            combine = dispatch * gate[..., None, None]
            expert_inputs = jnp.einsum('gtd,gtec->gecd', xt, dispatch)
            h = jax.nn.relu(jnp.einsum('gecd,edf->gecf', expert_inputs, w1) + b1[None, :, None, :])
            expert_outputs = jnp.einsum('gecf,efd->gecd', h, w2) + b2[None, :, None, :]
            out = jnp.einsum('gecd,gtec->gtd', expert_outputs, combine)
            return out.reshape(B, S, D)
        return _moe_forward(x, router_w, w1, b1, w2, b2)
    x = x + jnp.tanh(g_xattn[0]) * _L0_xattn_ref(_layernorm(x, axis=-1), ctx_1024, ctx_1024, L0_xattn_Wq, L0_xattn_bq, L0_xattn_Wk, L0_xattn_bk, L0_xattn_Wv, L0_xattn_bv, L0_xattn_Wo, L0_xattn_bo)
    x = x + jnp.tanh(g_ffn[0]) * _L0_ffn_ref(_layernorm(x, axis=-1), L0_ffn_gru_w_ih, L0_ffn_gru_w_hh, L0_ffn_expr_w, L0_ffn_ctx_w, L0_ffn_ctx_b, L0_ffn_gate_w, L0_ffn_up_w, L0_ffn_down_w, L0_ffn_shared_gate_w, L0_ffn_shared_up_w, L0_ffn_shared_down_w)
    x = x + jnp.tanh(g_xattn[1]) * _L1_xattn_ref(ctx_1024, _layernorm(x, axis=-1))
    x = x + jnp.tanh(g_ffn[1]) * _L1_ffn_ref(_layernorm(x, axis=-1), L1_ffn_router_w, L1_ffn_w1, L1_ffn_b1, L1_ffn_w2, L1_ffn_b2)
    return x

_drawn_inputs = setup_inputs


def setup_inputs(seed=0):
    import zlib

    import numpy as np

    out = dict(_drawn_inputs(seed))
    spreads = {'g_ffn': (-1.0, 0.6),
     'L0_xattn_bq': (0.0, 0.1),
     'L0_xattn_bk': (0.0, 2.0),
     'L0_xattn_bv': (0.0, 0.389),
     'L0_xattn_bo': (0.0, 0.1),
     'L0_ffn_ctx_b': (0.0, 0.8),
     'L1_ffn_b1': (0.0, 2.0),
     'L1_ffn_b2': (0.0, 0.8)}
    factors = {'L0_ffn_gru_w_hh': 4.238, 'L0_ffn_ctx_w': 8.0, 'L0_ffn_down_w': 2.976}
    for name, (base, spread) in spreads.items():
        noise = np.random.default_rng([zlib.crc32(name.encode()), seed]).standard_normal(out[name].shape)
        drawn = base * np.exp(spread * noise) if base else spread * noise
        out[name] = jnp.asarray(drawn.astype(out[name].dtype))
    for name, factor in factors.items():
        out[name] = (out[name] * factor).astype(out[name].dtype)
    return out
```

```python
from contextlib import ExitStack

import concourse.bass as bass
from concourse import mybir

F32 = mybir.dt.float32
BF16 = mybir.dt.bfloat16
I32 = mybir.dt.int32
U32 = mybir.dt.uint32
ALU = mybir.AluOpType
ACT = mybir.ActivationFunctionType
AX = mybir.AxisListType

P = 128
B, S, DIM = 32, 100, 256
KV, KC = 361, 121
KVP = 3 * KC
KLAST = KV - 2 * KC
KT = DIM // P
HEADS, HD = 16, 16
HG = HEADS // 4
LN_EPS = 1e-5


class Chain:

    def __init__(self, engine, semaphore, start=0):
        self.engine, self.semaphore, self.value = engine, semaphore, start

    def step(self, instruction):
        self.value = self.value + 1
        instruction.then_inc(self.semaphore, 1)
        self.engine.wait_ge(self.semaphore, self.value)


def repeat(engine, count, turn_of):
    turn_of(0)
    with engine.Fori(1, count) as i:
        turn_of(i)


def row_statistics(nc, stage, rows, mean, rstd):
    with ExitStack() as ctx:
        GROUP = 8
        stats = ctx.enter_context(nc.sbuf_tensor(f"stats_{stage}", [S, GROUP, 6], F32))
        mean_var = ctx.enter_context(nc.sbuf_tensor(f"mean_var_{stage}", [S, GROUP, 2], F32))
        stats_done = ctx.enter_context(nc.semaphore(f"stats_done_{stage}"))
        aggregated = ctx.enter_context(nc.semaphore(f"aggregated_{stage}"))
        taken = ctx.enter_context(nc.semaphore(f"taken_{stage}"))
        root_ready = ctx.enter_context(nc.semaphore(f"root_ready_{stage}"))
        block = ctx.enter_context(nc.Block())

        @block.vector
        def _(dve):
            for g in range(B // GROUP):
                for u in range(GROUP):
                    nc.vector.bn_stats(stats[:, u, :], rows[:, GROUP * g + u, :]).then_inc(stats_done, 1)
                dve.wait_ge(taken, 2 * g)
                for u in range(GROUP):
                    dve.wait_ge(stats_done, GROUP * g + u + 1)
                    nc.vector.bn_aggr(mean_var[:, u, :], stats[:, u, :]).then_inc(aggregated, 1)
                dve.wait_ge(aggregated, GROUP * g + GROUP)
                group = slice(GROUP * g, GROUP * g + GROUP)
                nc.vector.tensor_copy(mean[:, group], mean_var[:, :, 0]).then_inc(taken, 1)
                nc.vector.tensor_scalar(rstd[:, group], mean_var[:, :, 1], LN_EPS, None, ALU.add).then_inc(taken, 1)
            dve.wait_ge(taken, 2 * (B // GROUP) - 1)
            dve.wait_ge(root_ready, 1)
            nc.vector.reciprocal(rstd, rstd).then_inc(aggregated, 1)
            dve.wait_ge(aggregated, B + 1)

        @block.scalar
        def _(act):
            act.wait_ge(taken, 2 * (B // GROUP))
            nc.scalar.activation(rstd, rstd, ACT.Sqrt).then_inc(root_ready, 1)


def normalize(nc, out, rows, mean, rstd, b):
    return nc.vector.tensor_scalar(out, rows, mean[:, bass.ds(b, 1)], rstd[:, bass.ds(b, 1)], ALU.subtract, ALU.mult)


def load_rows(nc, stage, rows, source):
    with ExitStack() as ctx:
        rows_in = ctx.enter_context(nc.semaphore(f"rows_in_{stage}"))
        block = ctx.enter_context(nc.Block())

        @block.sync
        def _(sp):
            for n in range(4):
                some = slice(n * B // 4, (n + 1) * B // 4)
                sp.dma_start(rows[:, some, :], source[some].rearrange("b s d -> s b d")).then_inc(rows_in, 16)
            sp.wait_ge(rows_in, 4 * 16)


def normalized_rows_out(nc, rows, mean, rstd, h_rows, hT, ident):
    with ExitStack() as ctx:
        h = [ctx.enter_context(nc.sbuf_tensor(f"h{u}", [S, DIM], F32)) for u in range(2)]
        turned = [ctx.enter_context(nc.psum_tensor(f"turned{u}", [P, 512], F32)) for u in range(2)]
        h_ready = ctx.enter_context(nc.semaphore("h_ready"))
        h_stored = [ctx.enter_context(nc.semaphore(f"h_stored{u}")) for u in range(2)]
        h_turned = ctx.enter_context(nc.semaphore("h_turned"))
        hT_ready = ctx.enter_context(nc.semaphore("hT_ready"))
        block = ctx.enter_context(nc.Block())

        @block.vector
        def _(dve):
            def turn_of(i):
                for u in range(2):
                    b = 2 * i + u
                    dve.wait_ge(h_stored[u], 16 * i)
                    dve.wait_ge(h_turned, 2 * i)
                    normalize(nc, h[u][:], rows[:, bass.ds(b, 1), :].rearrange("p a n -> p (a n)"), mean, rstd, b).then_inc(h_ready, 1)

            repeat(dve, B // 2, turn_of)

        @block.tensor
        def _(pe):
            def turn_of(i):
                for u in range(2):
                    b = 2 * i + u
                    pe.wait_ge(h_ready, b + 1)
                    pe.wait_ge(hT_ready, 2 * i)
                    for k in range(KT):
                        last = nc.tensor.transpose(turned[u][:, k * S:(k + 1) * S], h[u][:, k * P:(k + 1) * P], ident[0:S, 0:S])
                    last.then_inc(h_turned, 1)

            repeat(pe, B // 2, turn_of)

        @block.scalar
        def _(act):
            def turn_of(i):
                for u in range(2):
                    b = 2 * i + u
                    act.wait_ge(h_turned, b + 1)
                    nc.scalar.copy(hT[:, :, bass.ds(b, 1), :].rearrange("p k a s -> p k (a s)"),
                                   turned[u][:, 0:KT * S].rearrange("p (k s) -> p k s", k=KT)).then_inc(hT_ready, 1)

            repeat(act, B // 2, turn_of)
            act.wait_ge(hT_ready, B)

        @block.sync
        def _(sp):
            def turn_of(i):
                for u in range(2):
                    b = 2 * i + u
                    sp.wait_ge(h_ready, b + 1)
                    sp.dma_start(h_rows[bass.ds(b, 1)].rearrange("a s d -> (a s) d"), h[u][:]).then_inc(h_stored[u], 16)

            repeat(sp, B // 2, turn_of)
            for u in range(2):
                sp.wait_ge(h_stored[u], 16 * (B // 2))


def constants(nc, ident, neg_ident, one_row):
    with ExitStack() as ctx:
        filled = ctx.enter_context(nc.semaphore("const_filled"))
        block = ctx.enter_context(nc.Block())

        @block.gpsimd
        def _(pool):
            nc.gpsimd.memset(ident[:, :], 0.0).then_inc(filled, 1)
            nc.gpsimd.memset(neg_ident[:, :], 0.0).then_inc(filled, 1)
            nc.gpsimd.memset(one_row[:, :], 1.0).then_inc(filled, 1)
            pool.wait_ge(filled, 3)
            nc.gpsimd.affine_select(out=ident[:, :], in_=ident[:, :], compare_op=ALU.not_equal, fill=1.0,
                                    base=0, pattern=[[-1, P]], channel_multiplier=1).then_inc(filled, 1)
            nc.gpsimd.affine_select(out=neg_ident[:, :], in_=neg_ident[:, :], compare_op=ALU.not_equal,
                                    fill=-1.0, base=0, pattern=[[-1, P]], channel_multiplier=1).then_inc(filled, 1)
            pool.wait_ge(filled, 5)


def pipelined(engine, count, turn_of):
    turn_of(0, 0, True, False)
    with engine.Fori(1, count // 2) as i:
        turn_of(2 * i - 1, 1, False, False)
        turn_of(2 * i, 0, False, False)
    turn_of(count - 1, (count - 1) % 2, False, True)


def attention(nc, rows, mean, rstd, ctxT, wqT, wkT, bqk, wvT, bv, woT, bo, g_xattn, x1, ident, neg_ident,
              whh, whhT, whh_in, to_clear, cleared_rows):
    with ExitStack() as ctx:
        def sb(name, shape, dt=F32):
            return ctx.enter_context(nc.sbuf_tensor("att_" + name, shape, dt))

        def ps(name):
            return ctx.enter_context(nc.psum_tensor("att_" + name, [P, 512], F32))

        def sem(name):
            return ctx.enter_context(nc.semaphore("att_" + name))

        PAIRS = HEADS // 2
        wq = sb("wq", [P, KT, HG * P])
        wk = sb("wk", [P, KT, HG * P])
        wv = sb("wv", [P, KT, DIM])
        wo = sb("wo", [P, KT, DIM])
        bq_bk = sb("bq_bk", [P, 2, HG])
        bv_all = sb("bv_all", [P, DIM])
        bo_gated = sb("bo_gated", [P, DIM])
        gate = sb("gate", [P, 2])
        c_in = [sb(f"c_in{u}", [P, KT, KVP]) for u in range(2)]
        xn = sb("xn", [S, DIM])
        xnT = sb("xnT", [P, KT, S])
        qT = sb("qT", [P, HG, S])
        qaT = sb("qaT", [P, HG, S])
        kT = [sb(f"kT{u}", [P, HG, KVP]) for u in range(2)]
        v = sb("v", [KC, 3, HEADS, 32])
        zero_rows = sb("zero_rows", [P, max(words for _, words in to_clear)])
        neg_max = sb("neg_max", [S, HG, 4, 32])
        probs = [sb(f"probs{u}", [KC, 4, 3 * S]) for u in range(2)]
        att = sb("att", [P, HG, S])
        inverse = sb("inverse", [S, HEADS])
        attn = sb("attn", [S, HEADS, HD])
        attnT = sb("attnT", [P, KT, S])

        proj = ps("proj")
        misc = ps("misc")
        keys = ps("keys")
        outs = ps("outs")
        score = [ctx.enter_context(nc.psum_tensor(f"score{u}", [P, 2, 512], F32)) for u in range(2)]

        weights_in = sem("weights_in")
        ctx_arrived = [sem(f"ctx_arrived{u}") for u in range(2)]
        stored = sem("x1_stored")
        gate_ready, cleared, bias_ready = sem("gate_ready"), sem("cleared"), sem("bias_ready")
        xn_ready, bias_added = sem("xn_ready"), sem("bias_added")
        xnT_psum, xnT_ready = sem("xnT_psum"), sem("xnT_ready")
        q_psum, q_ready = sem("q_psum"), sem("q_ready")
        k_psum, k_ready = sem("k_psum"), sem("k_ready")
        v_psum, v_ready = sem("v_psum"), sem("v_ready")
        s_psum, max_ready = sem("s_psum"), sem("max_ready")
        nm_psum, qa_ready = sem("nm_psum"), sem("qa_ready")
        t_psum, p_ready = sem("t_psum"), sem("p_ready")
        o_psum, att_ready = sem("o_psum"), sem("att_ready")
        back_psum, inverse_ready, attn_ready = sem("back_psum"), sem("inverse_ready"), sem("attn_ready")
        attnT_psum, attnT_ready = sem("attnT_psum"), sem("attnT_ready")
        y_psum, x1_ready = sem("y_psum"), sem("x1_ready")
        block = ctx.enter_context(nc.Block())

        def rows_of(b):
            return rows[:, bass.ds(b, 1), :].rearrange("p a n -> p (a n)")

        @block.sync
        def _(sp):
            for dst, src in ((wq[:], wqT), (wk[:], wkT), (wv[:], wvT), (wo[:], woT), (bq_bk[:], bqk),
                             (bv_all[:], bv.partition_broadcast(P)), (bo_gated[:], bo.partition_broadcast(P)),
                             (gate[:, 0:2], g_xattn.partition_broadcast(P))):
                sp.dma_start(dst, src).then_inc(weights_in, 16)

            def turn_of(i):
                for u in range(2):
                    b = 2 * i + u
                    if not isinstance(i, int):
                        sp.wait_ge(v_ready, 3 * b - 3)
                    sp.dma_start(c_in[u][:], ctxT[bass.ds(b, 1)].rearrange("a p k n -> (a p) k n")).then_inc(ctx_arrived[u], 16)

            repeat(sp, B // 2, turn_of)

        @block.gpsimd
        def _(pool):
            nc.gpsimd.memset(v[:], 0.0).then_inc(cleared, 1)
            nc.gpsimd.memset(neg_max[:], 0.0).then_inc(cleared, 1)
            nc.gpsimd.memset(zero_rows[:], 0.0).then_inc(cleared, 1)
            pool.wait_ge(cleared, 3)
            nc.gpsimd.memset(v[:, :, :, HD:HD + 1], 1.0).then_inc(cleared, 1)
            pool.wait_ge(weights_in, 8 * 16)
            for k in range(whh.shape[1]):
                pool.dma_start(whh[:, k, :], whhT[:, k, :]).then_inc(whh_in, 16)
            for dram, words in to_clear:
                pool.dma_start(dram, zero_rows[:, 0:words]).then_inc(cleared_rows, 16)
            pool.wait_ge(bias_ready, 1)

            def store(b):
                pool.wait_ge(x1_ready, b + 1)
                pool.dma_start(x1[bass.ds(b, 1)].rearrange("a s d -> (a s) d"), rows_of(b)).then_inc(stored, 16)

            def turn_of(b, u, first, last):
                pool.wait_ge(xn_ready, b + 1)
                nc.gpsimd.tensor_tensor(rows_of(b), rows_of(b), bo_gated[0:S, :], ALU.add).then_inc(bias_added, 1)
                if not first:
                    store(b - 1)

            pipelined(pool, B, turn_of)
            store(B - 1)
            pool.wait_ge(stored, 16 * B)
            pool.wait_ge(cleared_rows, 16 * len(to_clear))

        @block.scalar
        def _(act):
            def keys_out(b, u, c):
                act.wait_ge(k_psum, HG * b + c + 1)
                nc.scalar.activation(kT[u][:, c, :], keys[:, 0:KVP], ACT.Identity,
                                     bias=bq_bk[:, 1, c:c + 1]).then_inc(k_ready, 1)

            def xnT_out(b):
                act.wait_ge(xnT_psum, b + 1)
                nc.scalar.copy(xnT[:].rearrange("p k s -> p (k s)"), misc[:, 0:KT * S]).then_inc(xnT_ready, 1)

            def finish_before(b):
                act.wait_ge(o_psum, b + 1)
                nc.scalar.copy(att[:].rearrange("p c s -> p (c s)"), outs[:, 0:HG * S]).then_inc(att_ready, 1)
                act.wait_ge(attnT_psum, b + 1)
                nc.scalar.copy(attnT[:].rearrange("p k s -> p (k s)"), misc[:, 0:KT * S]).then_inc(attnT_ready, 1)

            act.wait_ge(weights_in, 8 * 16)
            nc.scalar.activation(gate[:, 0:1], gate[:, 0:1], ACT.Tanh).then_inc(gate_ready, 1)
            xnT_out(0)
            for c in range(HG):
                keys_out(0, 0, c)

            def turn_of(b, u, first, last):
                if not first:
                    finish_before(b - 1)
                if not last:
                    xnT_out(b + 1)
                    keys_out(b + 1, 1 - u, 0)
                for c in range(HG):
                    for pair in range(2):
                        act.wait_ge(t_psum, PAIRS * b + 2 * c + pair + 1)
                        nc.scalar.activation(probs[c % 2][:, 2 * pair:2 * pair + 2, :], score[pair][0:KC, :, 0:3 * S],
                                             ACT.Exp, scale=HD ** -0.5).then_inc(p_ready, 1)
                    if c + 1 < HG and not last:
                        keys_out(b + 1, 1 - u, c + 1)

            pipelined(act, B, turn_of)
            finish_before(B - 1)

        @block.vector
        def _(dve):
            def normalized(b):
                normalize(nc, xn[:], rows_of(b), mean, rstd, b).then_inc(xn_ready, 1)

            def queries_out(b):
                dve.wait_ge(q_psum, b + 1)
                nc.vector.tensor_tensor(qT[:], proj[:, 0:HG * S].rearrange("p (c s) -> p c s", c=HG),
                                        bq_bk[:, 0, :].unsqueeze(2).to_broadcast([P, HG, S]), ALU.add).then_inc(q_ready, 1)

            def divide(b):
                dve.wait_ge(back_psum, b + 1)
                heads = misc[0:S, :].rearrange("p (h j) -> p h j", h=HEADS)
                nc.vector.reciprocal(inverse[:], heads[:, :, HD]).then_inc(inverse_ready, 1)
                dve.wait_ge(inverse_ready, b + 1)
                nc.vector.tensor_tensor(attn[:], heads[:, :, 0:HD], inverse[:].unsqueeze(2).to_broadcast([S, HEADS, HD]),
                                        ALU.mult).then_inc(attn_ready, 1)

            def add_output(b):
                dve.wait_ge(bias_added, b + 1)
                dve.wait_ge(y_psum, b + 1)
                nc.vector.scalar_tensor_tensor(rows_of(b), proj[0:S, 0:DIM], gate[0:S, 0:1], rows_of(b),
                                               ALU.mult, ALU.add).then_inc(x1_ready, 1)

            normalized(0)
            dve.wait_ge(gate_ready, 1)
            nc.vector.tensor_scalar(bo_gated[:], bo_gated[:], gate[:, 0:1], None, ALU.mult).then_inc(bias_ready, 1)
            dve.wait_ge(cleared, 4)
            queries_out(0)

            def turn_of(b, u, first, last):
                for c in range(HG):
                    for pair in range(2):
                        dve.wait_ge(s_psum, PAIRS * b + 2 * c + pair + 1)
                        nc.vector.tensor_reduce(neg_max[:, c, 2 * pair:2 * pair + 2, HD:HD + 1].rearrange("p i o -> p (i o)"),
                                                score[pair][0:S, :, 0:KV], AX.X, ALU.max).then_inc(max_ready, 1)
                    if c < 3:
                        dve.wait_ge(v_psum, 3 * b + c + 1)
                        nc.vector.tensor_tensor(v[:, c, :, 0:HD], proj[0:KC, 0:DIM].rearrange("p (h d) -> p h d", h=HEADS),
                                                bv_all[0:KC, :].rearrange("p (h d) -> p h d", h=HEADS), ALU.add).then_inc(v_ready, 1)
                    if c == 0 and not first:
                        divide(b - 1)
                    if c == 1 and not last:
                        dve.wait_ge(xnT_psum, b + 1)
                        normalized(b + 1)
                dve.wait_ge(nm_psum, b + 1)
                nc.vector.tensor_tensor(qaT[:].rearrange("p c s -> p (c s)"), qT[:].rearrange("p c s -> p (c s)"),
                                        outs[:, 0:HG * S], ALU.add).then_inc(qa_ready, 1)
                if not first:
                    add_output(b - 1)
                if not last:
                    queries_out(b + 1)

            pipelined(dve, B, turn_of)
            divide(B - 1)
            add_output(B - 1)
            dve.wait_ge(x1_ready, B)

        @block.tensor
        def _(pe):
            def turn_x(b):
                pe.wait_ge(xn_ready, b + 1)
                for k in range(KT):
                    done = nc.tensor.transpose(misc[:, k * S:(k + 1) * S], xn[:, k * P:(k + 1) * P], ident[0:S, 0:S])
                done.then_inc(xnT_psum, 1)

            def project_keys(b, u, c, free):
                if free:
                    pe.wait_ge(k_ready, HG * b + c)
                for k in range(KT):
                    done = nc.tensor.matmul(keys[:, 0:KVP], wk[:, k, c * P:(c + 1) * P], c_in[u][:, k, :],
                                            start=(k == 0), stop=(k == KT - 1))
                done.then_inc(k_psum, 1)

            def project_queries(b, free):
                pe.wait_ge(xnT_ready, b + 1)
                if free:
                    pe.wait_ge(x1_ready, b - 1)
                for c in range(HG):
                    for k in range(KT):
                        done = nc.tensor.matmul(proj[:, c * S:(c + 1) * S], wq[:, k, c * P:(c + 1) * P], xnT[:, k, :],
                                                start=(k == 0), stop=(k == KT - 1))
                done.then_inc(q_psum, 1)

            def project_values(b, u, c):
                if c:
                    pe.wait_ge(v_ready, 3 * b + c)
                for k in range(KT):
                    done = nc.tensor.matmul(proj[0:KC, 0:DIM], c_in[u][:, k, c * KC:(c + 1) * KC], wv[:, k, :],
                                            start=(k == 0), stop=(k == KT - 1))
                done.then_inc(v_psum, 1)

            def scores(b, u, h):
                c, pair = divmod(h, 2)
                if h >= 2:
                    pe.wait_ge(max_ready, PAIRS * b + h - 1)
                for r in range(2):
                    at = slice(64 * pair + 32 * r, 64 * pair + 32 * r + 32)
                    done = nc.tensor.matmul(score[pair][0:S, r, 0:KV], qT[at, c, :], kT[u][at, c, 0:KV], start=True, stop=True)
                done.then_inc(s_psum, 1)

            def shifted_scores(b, u, h):
                c, pair = divmod(h, 2)
                if h >= 2:
                    pe.wait_ge(p_ready, PAIRS * b + h - 1)
                for m in range(3):
                    for r in range(2):
                        at = slice(64 * pair + 32 * r, 64 * pair + 32 * r + 32)
                        done = nc.tensor.matmul(score[pair][0:KC, r, m * S:(m + 1) * S], kT[u][at, c, m * KC:(m + 1) * KC],
                                                qaT[at, c, :], start=True, stop=True)
                done.then_inc(t_psum, 1)

            def outputs(b, c):
                pe.wait_ge(p_ready, PAIRS * b + 2 * c + 2)
                for m in range(3):
                    n = KC if m < 2 else KLAST
                    for r in range(4):
                        done = nc.tensor.matmul(outs[32 * r:32 * r + 32, c * S:(c + 1) * S], v[0:n, m, 4 * c + r, :],
                                                probs[c % 2][0:n, r, m * S:(m + 1) * S], start=(m == 0), stop=(m == 2))
                return done

            def turn_back(b):
                pe.wait_ge(att_ready, b + 1)
                for c in range(HG):
                    done = nc.tensor.transpose(misc[0:S, c * P:(c + 1) * P], att[:, c, :], ident[:, :])
                done.then_inc(back_psum, 1)

            def turn_attn(b):
                pe.wait_ge(attn_ready, b + 1)
                for k in range(KT):
                    done = nc.tensor.transpose(misc[:, k * S:(k + 1) * S],
                                               attn[:].rearrange("p h d -> p (h d)")[:, k * P:(k + 1) * P], ident[0:S, 0:S])
                done.then_inc(attnT_psum, 1)

            def project_output(b):
                pe.wait_ge(attnT_ready, b + 1)
                for k in range(KT):
                    done = nc.tensor.matmul(proj[0:S, 0:DIM], attnT[:, k, :], wo[:, k, :], start=(k == 0), stop=(k == KT - 1))
                done.then_inc(y_psum, 1)

            pe.wait_ge(weights_in, 8 * 16)
            turn_x(0)
            pe.wait_ge(ctx_arrived[0], 16)
            for c in range(HG):
                project_keys(0, 0, c, c > 0)
            project_queries(0, False)

            def turn_of(b, u, first, last):
                pe.wait_ge(q_ready, b + 1)
                pe.wait_ge(k_ready, HG * b + HG)
                if not first:
                    pe.wait_ge(p_ready, PAIRS * b)
                scores(b, u, 0)
                scores(b, u, 1)
                project_values(b, u, 0)
                if not first:
                    turn_back(b - 1)
                scores(b, u, 2)
                scores(b, u, 3)
                project_values(b, u, 1)
                if not first:
                    turn_attn(b - 1)
                scores(b, u, 4)
                scores(b, u, 5)
                project_values(b, u, 2)
                scores(b, u, 6)
                scores(b, u, 7)
                pe.wait_ge(v_ready, 3 * b + 3)
                if not first:
                    project_output(b - 1)
                if not last:
                    turn_x(b + 1)
                pe.wait_ge(max_ready, PAIRS * b + PAIRS)
                for c in range(HG):
                    done = nc.tensor.matmul(outs[:, c * S:(c + 1) * S], neg_max[:, c, :, :].rearrange("p i j -> p (i j)"),
                                            neg_ident[0:S, 0:S], start=True, stop=True)
                done.then_inc(nm_psum, 1)
                if not last:
                    if u:
                        pe.wait_ge(ctx_arrived[0], 8 * b + 24)
                    elif first:
                        pe.wait_ge(ctx_arrived[1], 16)
                    else:
                        pe.wait_ge(ctx_arrived[1], 8 * b + 16)
                    project_keys(b + 1, 1 - u, 0, True)
                pe.wait_ge(qa_ready, b + 1)
                shifted_scores(b, u, 0)
                shifted_scores(b, u, 1)
                for c in range(HG):
                    if not last:
                        if c + 1 < HG:
                            project_keys(b + 1, 1 - u, c + 1, True)
                        else:
                            project_queries(b + 1, not first)
                    if c + 1 < HG:
                        shifted_scores(b, u, 2 * c + 2)
                        shifted_scores(b, u, 2 * c + 3)
                    done = outputs(b, c)
                done.then_inc(o_psum, 1)

            pipelined(pe, B, turn_of)
            turn_back(B - 1)
            turn_attn(B - 1)
            project_output(B - 1)
            pe.wait_ge(x1_ready, B)


GD = 1024
EXPERTS, RD = 8, 128
GQ = GD // 4
GC = GD // P
STEPS = 4
TILES = S // STEPS
SHIFTS = ((0, 3), (1, 2), (4, 5, 6, 7))
ROWS = [sum(EXPERTS - s for s in g) for g in SHIFTS] + [2 * EXPERTS]
NSTAT = sum(ROWS)


def gru(nc, whh, whh_in, wihT, hT, wcT, ctx_b, weT, states, stat, ident):
    with ExitStack() as ctx:
        def sb(name, shape, dt=F32):
            return ctx.enter_context(nc.sbuf_tensor("gru_" + name, shape, dt))

        def ps(name):
            return ctx.enter_context(nc.psum_tensor("gru_" + name, [P, 512], F32))

        def sem(name):
            return ctx.enter_context(nc.semaphore("gru_" + name))

        wih = sb("wih", [P, KT, 3 * GD])
        we = sb("we", [P, KT, GD])
        xt = [sb(f"xt{u}", [P, KT, STEPS, B]) for u in range(2)]
        h = [sb(f"state{u}", [P, GQ]) for u in range(2)]
        stateT = [sb(f"stateT{t}", [P, P]) for t in range(2)]
        rz = sb("rz", [P, 2, GQ])
        one_z = sb("one_z", [P, GQ])
        zh = sb("zh", [P, GQ])
        cand = sb("cand", [P, GQ])
        cand_n = sb("cand_n", [P, GQ])
        routed = sb("routed", [P, EXPERTS, RD])
        expr = sb("expr", [P, EXPERTS, RD])
        prod = sb("prod", [P, max(ROWS), RD])
        x_mean = sb("x_mean", [P, KT, B])

        ps_rz, ps_n, ps_x = ps("ps_rz"), ps("ps_n"), ps("ps_x")
        ps_t = [ps("ps_t0"), ps("ps_t1")]
        ps_e = [ps("ps_e0"), ps("ps_e1")]

        small_in, inputs_in = sem("small_in"), sem("inputs_in")
        mean_ready, h0_psum = sem("mean_ready"), sem("h0_psum")
        xt_ready, gates_ready, rz_done, n_done = sem("xt_ready"), sem("gates_ready"), sem("rz_done"), sem("n_done")
        cand_ready, tanh_ready, h_ready = sem("cand_ready"), sem("tanh_ready"), sem("state_ready")
        turned, stateT_ready = sem("state_turned"), [sem("stateT0_ready"), sem("stateT1_ready")]
        stored = [sem("state_stored0"), sem("state_stored1")]
        e_done, e_copied = sem("e_done"), sem("e_copied")
        routed_in, prod_ready, prod_used = sem("routed_in"), sem("prod_ready"), sem("prod_used")
        dve_own = sem("gru_dve_own")

        with ExitStack() as first:
            wc = first.enter_context(nc.sbuf_tensor("wc", [P, KT, GD], F32))
            cb = first.enter_context(nc.sbuf_tensor("cb", [P, GQ], F32))
            block = first.enter_context(nc.Block())

            @block.sync
            def _(sp):
                sp.dma_start(wc[:], wcT).then_inc(small_in, 16)
                for q in range(4):
                    sp.dma_start(cb[32 * q:32 * q + 32, :], ctx_b[q * GQ:(q + 1) * GQ].partition_broadcast(32)).then_inc(small_in, 16)
                sp.dma_start(wih[:], wihT).then_inc(inputs_in, 16)
                sp.dma_start(we[:], weT).then_inc(inputs_in, 16)
                sp.wait_ge(small_in, 5 * 16)
                sp.wait_ge(inputs_in, 2 * 16)

            @block.vector
            def _(dve):
                nc.vector.tensor_reduce(x_mean[:], hT[:], AX.X, ALU.add).then_inc(dve_own, 1)
                dve.wait_ge(dve_own, 1)
                nc.vector.tensor_scalar(x_mean[:], x_mean[:], 1.0 / S, None, ALU.mult).then_inc(mean_ready, 1)
                dve.wait_ge(small_in, 5 * 16)
                dve.wait_ge(h0_psum, 1)
                nc.vector.tensor_tensor(h[0][:], ps_n[:, 0:GQ], cb[:], ALU.add).then_inc(h_ready, 1)
                dve.wait_ge(h_ready, 1)

            @block.tensor
            def _(pe):
                pe.wait_ge(small_in, 5 * 16)
                pe.wait_ge(mean_ready, 1)
                for q in range(4):
                    for k in range(KT):
                        last = nc.tensor.matmul(ps_n[32 * q:32 * q + 32, 0:GQ], x_mean[:, k, :], wc[:, k, q * GQ:(q + 1) * GQ],
                                                start=(k == 0), stop=(k == KT - 1))
                last.then_inc(h0_psum, 1)

        block = ctx.enter_context(nc.Block())

        def quarter(q):
            return slice(32 * q, 32 * q + 32)

        def rz_columns(w, k, q):
            return w[:, k, 0:2 * GD].rearrange("p (g n) -> p g n", g=2)[:, :, q * GQ:(q + 1) * GQ]

        def n_columns(w, k, q):
            return w[:, k, 2 * GD + q * GQ:2 * GD + (q + 1) * GQ]

        @block.sync
        def _(sp):
            def turn_of(it):
                for j in range(STEPS):
                    u = (j + 1) % 2
                    sp.wait_ge(h_ready, STEPS * it + j + 2)
                    sp.dma_start(states[bass.ds(it, 1), j].rearrange("a b (q n) -> (a q) b n", q=4), h[u][:]).then_inc(stored[u], 16)
                for u in range(2):
                    sp.wait_ge(stored[u], 16 * 2 * it + 32)
                sp.wait_ge(prod_ready, 4 * it)
                sp.dma_start(routed[:].rearrange("p e d -> p (e d)"),
                             states[bass.ds(it, 1)].rearrange("a j b n -> (a j b) n")).then_inc(routed_in, 16)

            repeat(sp, TILES, turn_of)

        @block.gpsimd
        def _(pool):
            def take_inputs(it, u):
                nc.gpsimd.tensor_copy(xt[u][:], hT[:, :, :, bass.ds(STEPS * it, STEPS)].rearrange("p k b j -> p k j b")).then_inc(xt_ready, 1)

            def products(it):
                pool.wait_ge(routed_in, 16 * it + 16)
                pool.wait_ge(e_copied, 2 * it + 2)
                groups = [[(routed[:, 0:EXPERTS - s, :], routed[:, s:EXPERTS, :]) for s in g] for g in SHIFTS]
                groups.insert(0, [(expr[:], routed[:]), (expr[:], expr[:])])
                for n, group in enumerate(groups):
                    pool.wait_ge(prod_used, 4 * it + n)
                    row = 0
                    for a, b in group:
                        rows = a.shape[1]
                        last = nc.gpsimd.tensor_tensor(prod[:, row:row + rows, :], a, b, ALU.mult)
                        row += rows
                    last.then_inc(prod_ready, 1)

            take_inputs(0, 0)
            def turn_of(i):
                for u in range(2):
                    it = 2 * i + u
                    pool.wait_ge(gates_ready, 2 * STEPS * it)
                    pool.wait_ge(e_done, 2 * it)
                    take_inputs(it + 1, 1 - u)
                    products(it)

            repeat(pool, TILES // 2, turn_of)
            products(TILES - 1)
            pool.wait_ge(prod_ready, 4 * TILES)

        def sum_group(dve, it, n):
            at = sum((ROWS[-1:] + ROWS[:-1])[:n])
            rows = (ROWS[-1:] + ROWS[:-1])[n]
            dve.wait_ge(prod_ready, 4 * it + n + 1)
            nc.vector.tensor_reduce(stat[:, bass.ds(it, 1), at:at + rows].rearrange("p a n -> p (a n)"),
                                    prod[:, 0:rows, :], AX.X, ALU.add).then_inc(prod_used, 1)

        @block.vector
        def _(dve):
            def steps(it, first):
                for j in range(STEPS):
                    t = STEPS * it + j
                    old, new = h[j % 2], h[(j + 1) % 2]
                    dve.wait_ge(turned, 2 * t + 1)
                    nc.vector.tensor_copy(stateT[0][:], ps_t[0][:, 0:P]).then_inc(stateT_ready[0], 1)
                    if not first:
                        sum_group(dve, it - 1, j)
                    dve.wait_ge(gates_ready, 2 * t + 1)
                    nc.vector.tensor_tensor(zh[:], rz[:, 1, :], old[:], ALU.mult).then_inc(dve_own, 1)
                    dve.wait_ge(n_done, t + 1)
                    nc.vector.tensor_tensor(cand[:], rz[:, 0, :], ps_n[:, 0:GQ], ALU.mult).then_inc(dve_own, 1)
                    dve.wait_ge(dve_own, 3 * t + 3)
                    nc.vector.tensor_tensor(cand[:], cand[:], ps_x[:, 0:GQ], ALU.add).then_inc(cand_ready, 1)
                    dve.wait_ge(gates_ready, 2 * t + 2)
                    dve.wait_ge(tanh_ready, t + 1)
                    nc.vector.tensor_tensor(cand_n[:], cand_n[:], one_z[:], ALU.mult).then_inc(dve_own, 1)
                    dve.wait_ge(dve_own, 3 * t + 4)
                    dve.wait_ge(stored[(j + 1) % 2], 16 * (2 * it + j // 2))
                    nc.vector.tensor_tensor(new[:], cand_n[:], zh[:], ALU.add).then_inc(h_ready, 1)

            steps(0, True)
            with dve.Fori(1, TILES) as it:
                steps(it, False)
            for n in range(4):
                sum_group(dve, TILES - 1, n)
            dve.wait_ge(prod_used, 4 * TILES)

        @block.scalar
        def _(act):
            def turn_of(it):
                for j in range(STEPS):
                    t = STEPS * it + j
                    act.wait_ge(turned, 2 * t + 2)
                    nc.scalar.copy(stateT[1][:], ps_t[1][:, 0:P]).then_inc(stateT_ready[1], 1)
                    if j >= 2:
                        act.wait_ge(e_done, 2 * it + 2)
                        act.wait_ge(prod_ready, 4 * it)
                        nc.scalar.copy(expr[:].rearrange("p e d -> p (e d)")[:, (j - 2) * 512:(j - 1) * 512], ps_e[j - 2][:, :]).then_inc(e_copied, 1)
                    act.wait_ge(rz_done, t + 1)
                    nc.scalar.activation(rz[:].rearrange("p g n -> p (g n)"), ps_rz[:, :], ACT.Sigmoid).then_inc(gates_ready, 1)
                    nc.scalar.activation(one_z[:], ps_rz[:, GQ:2 * GQ], ACT.Sigmoid, scale=-1.0).then_inc(gates_ready, 1)
                    act.wait_ge(cand_ready, t + 1)
                    nc.scalar.activation(cand_n[:], cand[:], ACT.Tanh).then_inc(tanh_ready, 1)

            repeat(act, TILES, turn_of)

        @block.tensor
        def _(pe):
            pe.wait_ge(whh_in, 16 * GC)

            def steps(it, u):
                pe.wait_ge(xt_ready, it + 1)
                for j in range(STEPS):
                    t = STEPS * it + j
                    pe.wait_ge(gates_ready, 2 * t)
                    for k in range(KT):
                        for q in range(4):
                            nc.tensor.matmul(ps_rz[quarter(q), :], xt[u][:, k, j, :], rz_columns(wih, k, q),
                                             start=(k == 0), stop=False)
                    pe.wait_ge(cand_ready, t)
                    for k in range(KT):
                        for q in range(4):
                            nc.tensor.matmul(ps_x[quarter(q), 0:GQ], xt[u][:, k, j, :], n_columns(wih, k, q),
                                             start=(k == 0), stop=(k == KT - 1))
                    if j < 2:
                        pe.wait_ge(e_copied, 2 * it)
                        for k in range(KT):
                            last = nc.tensor.matmul(ps_e[j][:, :], xt[u][:, k, :, :].rearrange("p j b -> p (j b)"),
                                                    we[:, k, j * 512:(j + 1) * 512], start=(k == 0), stop=(k == KT - 1))
                        last.then_inc(e_done, 1)
                    pe.wait_ge(h_ready, t + 1)
                    for half in range(2):
                        nc.tensor.transpose(ps_t[half][:, 0:P], h[j % 2][:, half * P:(half + 1) * P], ident[:, :]).then_inc(turned, 1)
                    for half in range(2):
                        pe.wait_ge(stateT_ready[half], t + 1)
                    for c in range(GC):
                        for q in range(4):
                            last = nc.tensor.matmul(ps_rz[quarter(q), :], stateT[c % 2][:, quarter(c // 2)], rz_columns(whh, c, q),
                                                    start=False, stop=(c == GC - 1))
                    last.then_inc(rz_done, 1)
                    for c in range(GC):
                        for q in range(4):
                            last = nc.tensor.matmul(ps_n[quarter(q), 0:GQ], stateT[c % 2][:, quarter(c // 2)], n_columns(whh, c, q),
                                                    start=(c == 0), stop=(c == GC - 1))
                    last.then_inc(n_done, 1)

            def turn_of(i):
                for u in range(2):
                    steps(2 * i + u, u)

            repeat(pe, TILES // 2, turn_of)
            steps(TILES - 1, 0)


FF = 512
TOKENS = B * S
TT = TOKENS // P
SLOT_TILES = (2 * TOKENS + EXPERTS * (P - 1)) // P
MOE_TILES = TT + SLOT_TILES
FC = FF // P
TINY_NORM, TINY_COS = 1e-12, 1e-8
HUGE = 3.0e38


def routing(nc, stat, weight, slot, tile_expert, iota_e, below, ones, g_ffn, gate, gu, guT, dn, dnT, weights_in):
    with ExitStack() as ctx:
        def sb(name, shape, dt=F32):
            return ctx.enter_context(nc.sbuf_tensor("route_" + name, shape, dt))

        def sem(name):
            return ctx.enter_context(nc.semaphore("route_" + name))

        inv = sb("inv", [P, TILES, EXPERTS])
        pair = sb("pair", [P, TILES, EXPERTS])
        row2 = sb("row2", [P, TILES, EXPERTS])
        root = sb("root", [P, TILES, EXPERTS])
        en = sb("en", [P, TILES, EXPERTS])
        score = sb("score", [P, TILES, EXPERTS])
        work = sb("work", [P, TILES, EXPERTS])
        hot = [sb(f"hot{k}", [P, TILES, EXPERTS]) for k in range(2)]
        chosen = sb("chosen", [P, TILES, EXPERTS])
        best = [sb(f"best{k}", [P, TILES]) for k in range(2)]
        index = sb("index", [P, TILES])
        ratio = sb("ratio", [P, TILES])
        share = sb("share", [P, TILES])
        pen = sb("pen", [P, 1])
        total = sb("total", [P, EXPERTS, TILES])
        upto = sb("upto", [P, EXPERTS, TILES])
        zeros = sb("zeros_r", [P, TILES])
        row_of = sb("row_of", [P, TILES, EXPERTS])
        steps_i = sb("steps_i", [P, EXPERTS, TILES], I32)
        steps_f = sb("steps_f", [P, EXPERTS, TILES])
        need = sb("need", [P, EXPERTS])
        end = sb("end", [P, EXPERTS])
        base = sb("base", [P, EXPERTS])
        slot_f = sb("slot_f", [P, TILES])
        tile_i = sb("tile_i", [1, MOE_TILES, EXPERTS], I32)
        tile_f = sb("tile_f", [1, MOE_TILES, EXPERTS])
        tile_e = sb("tile_e", [1, MOE_TILES])
        ps_pen = ctx.enter_context(nc.psum_tensor("ps_pen", [P, 512], F32))
        ps_rank = ctx.enter_context(nc.psum_tensor("ps_rank", [P, 512], F32))
        ps_total = ctx.enter_context(nc.psum_tensor("ps_total", [P, 512], F32))

        own, filled = sem("route_own"), sem("route_filled")
        root_in, root_out, exp_in, exp_out = sem("root_in"), sem("root_out"), sem("exp_in"), sem("exp_out")
        pen_in, pen_out, chosen_ready, ranked = sem("pen_in"), sem("pen_out"), sem("chosen_ready"), sem("ranked")
        gate_in, gate_ready = sem("ffn_gate_in"), sem("ffn_gate_ready")
        block = ctx.enter_context(nc.Block())

        @block.sync
        def _(sp):
            sp.dma_start(gate[:, :], g_ffn.partition_broadcast(P)).then_inc(gate_in, 16)
            for e in range(EXPERTS + 1):
                sp.dma_start(gu[:, e], guT[:, e]).then_inc(weights_in, 16)
                sp.dma_start(dn[:, e], dnT[:, e]).then_inc(weights_in, 16)
            sp.wait_ge(gate_in, 16)

        @block.gpsimd
        def _(pool):
            nc.gpsimd.iota(steps_i[:], pattern=[[0, EXPERTS], [P, TILES]], base=0, channel_multiplier=0).then_inc(filled, 1)
            nc.gpsimd.iota(tile_i[:], pattern=[[1, MOE_TILES], [0, EXPERTS]], base=-TT, channel_multiplier=0).then_inc(filled, 1)
            nc.gpsimd.memset(zeros[:], 0.0).then_inc(filled, 1)
            pool.wait_ge(filled, 3)
            nc.gpsimd.tensor_copy(steps_f[:], steps_i[:]).then_inc(filled, 1)
            nc.gpsimd.tensor_copy(tile_f[:], tile_i[:]).then_inc(filled, 1)

        @block.scalar
        def _(act):
            act.wait_ge(gate_in, 16)
            nc.scalar.activation(gate[:, :], gate[:, :], ACT.Tanh).then_inc(gate_ready, 1)
            act.wait_ge(gate_ready, 1)
            for n, (a, b) in enumerate(((inv, stat[:, :, 16:24]), (en, stat[:, :, 8:16]), (root, root), (work, row2))):
                act.wait_ge(root_in, n + 1)
                nc.scalar.activation(a[:], b if n < 2 else b[:], ACT.Sqrt).then_inc(root_out, 1)
            act.wait_ge(exp_in, 1)
            nc.scalar.activation(ratio[:], ratio[:], ACT.Exp).then_inc(exp_out, 1)

        @block.tensor
        def _(pe):
            pe.wait_ge(pen_in, 1)
            nc.tensor.matmul(ps_pen[:, 0:1], ones[:, :], pen[:, :], start=True, stop=True).then_inc(pen_out, 1)
            pe.wait_ge(chosen_ready, 1)
            flat = chosen[:].rearrange("p t e -> p (t e)")
            nc.tensor.matmul(ps_rank[:, 0:TILES * EXPERTS], below[:, :], flat, start=True, stop=True).then_inc(ranked, 1)
            nc.tensor.matmul(ps_total[:, 0:TILES * EXPERTS], ones[:, :], flat, start=True, stop=True).then_inc(ranked, 1)

        @block.vector
        def _(dve):
            v = nc.vector
            chain = Chain(dve, own)

            def every(a):
                return a[:].unsqueeze(2).to_broadcast([P, TILES, EXPERTS])

            v.tensor_copy(pen[:], stat[:, 0, 0:1]).then_inc(root_in, 2)
            dve.wait_ge(root_out, 2)
            chain.step(v.tensor_scalar(inv[:], inv[:], TINY_NORM, None, ALU.max))
            chain.step(v.reciprocal(inv[:], inv[:]))
            chain.step(v.tensor_tensor(root[:], stat[:, :, 16:24], inv[:], ALU.mult))
            chain.step(v.tensor_tensor(root[:], root[:], inv[:], ALU.mult))
            chain.step(v.tensor_scalar(row2[:], root[:], -1.0, None, ALU.add))
            v.tensor_tensor(row2[:], row2[:], row2[:], ALU.mult).then_inc(root_in, 1)
            dve.wait_ge(root_in, 3)
            at = 16
            for group in SHIFTS:
                for s in group:
                    n = EXPERTS - s
                    if s:
                        p = pair[:, :, 0:n]
                        chain.step(v.tensor_tensor(p, stat[:, :, at:at + n], inv[:, :, 0:n], ALU.mult))
                        chain.step(v.tensor_tensor(p, p, inv[:, :, s:EXPERTS], ALU.mult))
                        chain.step(v.tensor_tensor(p, p, p, ALU.mult))
                        chain.step(v.tensor_tensor(row2[:, :, 0:n], row2[:, :, 0:n], p, ALU.add))
                        chain.step(v.tensor_tensor(row2[:, :, s:EXPERTS], row2[:, :, s:EXPERTS], p, ALU.add))
                    at += n
            v.tensor_scalar(pen[:], pen[:], 0.0, None, ALU.mult).then_inc(root_in, 1)
            dve.wait_ge(root_out, 3)
            chain.step(v.tensor_scalar(root[:], root[:], TINY_COS, None, ALU.max))
            chain.step(v.tensor_scalar(en[:], en[:], TINY_COS, None, ALU.max))
            chain.step(v.tensor_tensor(en[:], en[:], root[:], ALU.mult))
            chain.step(v.reciprocal(en[:], en[:]))
            chain.step(v.tensor_tensor(score[:], stat[:, :, 0:8], inv[:], ALU.mult))
            chain.step(v.tensor_tensor(score[:], score[:], en[:], ALU.mult))
            chain.step(v.tensor_scalar(score[:], score[:], -1.0, 1.0, ALU.mult, ALU.add))
            dve.wait_ge(root_out, 4)
            chain.step(v.tensor_scalar(work[:], work[:], TINY_NORM, None, ALU.max))
            chain.step(v.reciprocal(work[:], work[:]))
            chain.step(v.tensor_tensor(row2[:], row2[:], work[:], ALU.mult))
            chain.step(v.tensor_tensor(row2[:], row2[:], work[:], ALU.mult))
            v.tensor_reduce(pen[:], row2[:], AX.XY, ALU.add).then_inc(pen_in, 1)
            dve.wait_ge(pen_out, 1)
            chain.step(v.tensor_scalar(pen[:], ps_pen[:, 0:1], 1.0 / TOKENS, 1.0, ALU.mult, ALU.add))
            chain.step(v.tensor_scalar(score[:], score[:], pen[:, 0:1], None, ALU.mult))
            for k in range(2):
                chain.step(v.tensor_reduce(best[k][:], score[:], AX.X, ALU.max))
                chain.step(v.tensor_tensor(work[:], score[:], every(best[k]), ALU.is_lt))
                chain.step(v.scalar_tensor_tensor(work[:], work[:], 2.0 * EXPERTS, iota_e[:], ALU.mult, ALU.add))
                chain.step(v.tensor_reduce(index[:], work[:], AX.X, ALU.min))
                chain.step(v.tensor_tensor(hot[k][:], iota_e[:], every(index), ALU.is_equal))
                if k == 0:
                    chain.step(v.scalar_tensor_tensor(score[:], hot[0][:], -HUGE, score[:], ALU.mult, ALU.add))
            v.tensor_tensor(chosen[:], hot[0][:], hot[1][:], ALU.add).then_inc(chosen_ready, 1)
            v.tensor_tensor(ratio[:], best[1][:], best[0][:], ALU.subtract).then_inc(exp_in, 1)
            dve.wait_ge(exp_out, 1)
            chain.step(v.tensor_scalar(share[:], ratio[:], 1.0, None, ALU.add))
            chain.step(v.reciprocal(weight[:, :, 0], share[:]))
            chain.step(v.tensor_tensor(weight[:, :, 1], weight[:, :, 0], ratio[:], ALU.mult))
            dve.wait_ge(ranked, 2)
            dve.wait_ge(filled, 5)
            chain.step(v.tensor_copy(total[:], ps_total[:, 0:TILES * EXPERTS].rearrange("p (t e) -> p e t", e=EXPERTS)))
            for e in range(EXPERTS):
                chain.step(v.tensor_tensor_scan(upto[:, e, :], zeros[:], total[:, e, :], 0.0, ALU.add, ALU.add))
            chain.step(v.tensor_tensor(steps_f[:], steps_f[:], upto[:, :, TILES - 1:TILES].to_broadcast([P, EXPERTS, TILES]), ALU.is_lt))
            chain.step(v.tensor_reduce(need[:], steps_f[:], AX.X, ALU.add))
            chain.step(v.tensor_tensor_scan(end[:], zeros[:, 0:EXPERTS], need[:], 0.0, ALU.add, ALU.add))
            chain.step(v.tensor_tensor(base[:], end[:], need[:], ALU.subtract))
            chain.step(v.tensor_scalar(base[:], base[:], float(P), float(TOKENS - 1), ALU.mult, ALU.add))
            chain.step(v.tensor_tensor(upto[:], upto[:], total[:], ALU.subtract))
            chain.step(v.tensor_tensor(upto[:], upto[:], base[:].unsqueeze(2).to_broadcast([P, EXPERTS, TILES]), ALU.add))
            chain.step(v.tensor_tensor(row_of[:], ps_rank[:, 0:TILES * EXPERTS].rearrange("p (t e) -> p t e", e=EXPERTS),
                                       upto[:].rearrange("p e t -> p t e"), ALU.add))
            for k in range(2):
                chain.step(v.tensor_tensor(work[:], hot[k][:], row_of[:], ALU.mult))
                chain.step(v.tensor_reduce(slot_f[:], work[:], AX.X, ALU.add))
                chain.step(v.tensor_copy(slot[:, :, k], slot_f[:]))
            chain.step(v.tensor_tensor(tile_f[:], tile_f[:], end[0:1, :].unsqueeze(1).to_broadcast([1, MOE_TILES, EXPERTS]), ALU.is_ge))
            chain.step(v.tensor_reduce(tile_e[:], tile_f[:], AX.X, ALU.add))
            chain.step(v.tensor_scalar(tile_e[:], tile_e[:], float(EXPERTS - 1), None, ALU.min))
            chain.step(v.memset(tile_e[:, 0:TT], float(EXPERTS)))
            chain.step(v.tensor_copy(tile_expert[:], tile_e[:]))


def scatter_rows(nc, h_rows, moe_in, slot):
    with ExitStack() as ctx:
        h_all = ctx.enter_context(nc.sbuf_tensor("h_all", [P, TILES, DIM], F32))
        h_in = ctx.enter_context(nc.semaphore("h_in"))
        scattered = ctx.enter_context(nc.semaphore("scattered"))
        block = ctx.enter_context(nc.Block())
        h_view = h_rows.rearrange("b (t j) d -> t j b d", j=STEPS)

        @block.sync
        def _(sp):
            def turn_of(it):
                for j in range(STEPS):
                    sp.dma_start(h_all[32 * j:32 * j + 32, bass.ds(it, 1), :].rearrange("p a n -> p (a n)"),
                                 h_view[bass.ds(it, 1), j].rearrange("a b d -> (a b) d")).then_inc(h_in, 16)

            repeat(sp, TILES, turn_of)

        @block.gpsimd
        def _(pool):
            pool.wait_ge(h_in, 16 * STEPS * TILES)
            for it in range(TILES):
                for k in range(2):
                    nc.gpsimd.indirect_dma_start(moe_in, bass.IndirectOffsetOnAxis(ap=slot[:, it, k:k + 1], axis=0),
                                                 h_all[:, it, :], None).then_inc(scattered, 16)
            pool.wait_ge(scattered, 16 * 2 * TILES)


def expert_tiles(nc, moe_in, moe_out, gu, dn, tile_expert, weights_in, ident):
    with ExitStack() as ctx:
        def sb(name, shape, dt=F32):
            return ctx.enter_context(nc.sbuf_tensor("moe_" + name, shape, dt))

        def ps(name):
            return ctx.enter_context(nc.psum_tensor("moe_" + name, [P, 512], F32))

        def sem(name):
            return ctx.enter_context(nc.semaphore("moe_" + name))

        xs = [sb(f"xs{u}", [P, DIM]) for u in range(2)]
        xT = [sb(f"xT{u}", [P, KT, P]) for u in range(2)]
        act_g = [sb(f"act_g{u}", [P, FF]) for u in range(2)]
        mid = [sb(f"mid{u}", [P, FF]) for u in range(2)]
        midT = [sb(f"midT{u}", [P, FC, P]) for u in range(2)]
        y = [sb(f"moe_y{u}", [P, DIM]) for u in range(2)]
        ps_x, ps_m, ps_y = ps("moe_ps_x"), ps("moe_ps_m"), ps("moe_ps_y")
        ps_g = [ps(f"moe_ps_g{u}") for u in range(2)]
        ps_u = [ps(f"moe_ps_u{u}") for u in range(2)]
        xs_in, x_turned, xT_ready = [sem("xs_in0"), sem("xs_in1")], sem("x_turned"), sem("xT_ready")
        g_done, u_done, act_ready, mid_ready = sem("g_done"), sem("u_done"), sem("act_ready"), sem("mid_ready")
        m_turned, midT_ready, y_done, y_ready = sem("m_turned"), sem("midT_ready"), sem("y_done"), sem("y_ready")
        y_stored = [sem("y_stored0"), sem("y_stored1")]
        block = ctx.enter_context(nc.Block())

        def rows(dram, n):
            return dram.rearrange("(t p) d -> t p d", p=P)[bass.ds(n, 1)].rearrange("a p d -> (a p) d")

        @block.sync
        def _(sp):
            def turn_of(i):
                for u in range(2):
                    sp.wait_ge(x_turned, 2 * i)
                    sp.dma_start(xs[u][:], rows(moe_in, 2 * i + u)).then_inc(xs_in[u], 16)

            repeat(sp, MOE_TILES // 2, turn_of)

        @block.gpsimd
        def _(pool):
            def turn_of(i):
                for u in range(2):
                    pool.wait_ge(y_ready, 2 * i + u + 1)
                    pool.dma_start(rows(moe_out, 2 * i + u), y[u][:]).then_inc(y_stored[u], 16)

            repeat(pool, MOE_TILES // 2, turn_of)
            for u in range(2):
                pool.wait_ge(y_stored[u], 16 * (MOE_TILES // 2))

        @block.scalar
        def _(act):
            def take_x(n, u):
                act.wait_ge(x_turned, n + 1)
                nc.scalar.copy(xT[u][:].rearrange("p k n -> p (k n)"), ps_x[:, 0:KT * P]).then_inc(xT_ready, 1)

            take_x(0, 0)
            def two_tiles(i, more):
                for u in range(2):
                    n = 2 * i + u
                    act.wait_ge(g_done, n + 1)
                    act.wait_ge(mid_ready, 2 * i)
                    nc.scalar.activation(act_g[u][:], ps_g[u][:, :], ACT.Silu).then_inc(act_ready, 1)
                    if u == 0 or more:
                        take_x(n + 1, 1 - u)
                    act.wait_ge(y_done, n + 1)
                    act.wait_ge(y_stored[u], 16 * i)
                    nc.scalar.copy(y[u][:], ps_y[:, 0:DIM]).then_inc(y_ready, 1)

            def turn_of(i):
                two_tiles(i, True)

            repeat(act, MOE_TILES // 2 - 1, turn_of)
            two_tiles(MOE_TILES // 2 - 1, False)

        @block.vector
        def _(dve):
            def turn_of(i):
                for u in range(2):
                    n = 2 * i + u
                    dve.wait_ge(act_ready, n + 1)
                    dve.wait_ge(u_done, n + 1)
                    dve.wait_ge(m_turned, 2 * i)
                    nc.vector.tensor_tensor(mid[u][:], act_g[u][:], ps_u[u][:, :], ALU.mult).then_inc(mid_ready, 1)
                    dve.wait_ge(m_turned, n + 1)
                    nc.vector.tensor_copy(midT[u][:].rearrange("p k n -> p (k n)"), ps_m[:, :]).then_inc(midT_ready, 1)

            repeat(dve, MOE_TILES // 2, turn_of)

        @block.tensor
        def _(pe):
            expert = tile_expert

            def turn(n_half, n, u):
                pe.wait_ge(xs_in[u], 16 * n_half + 16)
                pe.wait_ge(xT_ready, n)
                for k in range(KT):
                    last = nc.tensor.transpose(ps_x[:, k * P:(k + 1) * P], xs[u][:, k * P:(k + 1) * P], ident[:, :])
                last.then_inc(x_turned, 1)

            def up(psum, half, e, u):
                for k in range(KT):
                    last = nc.tensor.matmul(psum[:, :], xT[u][:, k, :],
                                            gu[:, bass.ds(e, 1), k, half * FF:(half + 1) * FF].rearrange("p a n -> p (a n)"),
                                            start=(k == 0), stop=(k == KT - 1))
                return last

            pe.wait_ge(weights_in, 16 * 2 * (EXPERTS + 1))
            turn(0, 0, 0)
            def two_tiles(i, more):
                for u in range(2):
                    n = 2 * i + u
                    e = nc.tensor.value_load(expert[0:1, bass.ds(n, 1)], min_val=0, max_val=EXPERTS)
                    pe.wait_ge(xT_ready, n + 1)
                    pe.wait_ge(act_ready, 2 * i)
                    up(ps_g[u], 0, e, u).then_inc(g_done, 1)
                    pe.wait_ge(mid_ready, 2 * i)
                    up(ps_u[u], 1, e, u).then_inc(u_done, 1)
                    if u == 0:
                        turn(i, n + 1, 1)
                    elif more:
                        turn(i + 1, n + 1, 0)
                    pe.wait_ge(mid_ready, n + 1)
                    pe.wait_ge(midT_ready, n)
                    for c in range(FC):
                        last = nc.tensor.transpose(ps_m[:, c * P:(c + 1) * P], mid[u][:, c * P:(c + 1) * P], ident[:, :])
                    last.then_inc(m_turned, 1)
                    pe.wait_ge(midT_ready, n + 1)
                    pe.wait_ge(y_ready, n)
                    for c in range(FC):
                        last = nc.tensor.matmul(ps_y[:, 0:DIM], midT[u][:, c, :],
                                                dn[:, bass.ds(e, 1), c, :].rearrange("p a n -> p (a n)"),
                                                start=(c == 0), stop=(c == FC - 1))
                    last.then_inc(y_done, 1)

            def turn_of(i):
                two_tiles(i, True)

            repeat(pe, MOE_TILES // 2 - 1, turn_of)
            two_tiles(MOE_TILES // 2 - 1, False)


def combine(nc, moe_out, x1, weight, slot, gate, x2):
    with ExitStack() as ctx:
        def sb(name, shape, dt=F32):
            return ctx.enter_context(nc.sbuf_tensor("mix_" + name, shape, dt))

        def sem(name):
            return ctx.enter_context(nc.semaphore("mix_" + name))

        N = 5
        pair = [[sb(f"pair{k}_{u}", [P, DIM]) for k in range(2)] for u in range(N)]
        shared = [sb(f"shared{u}", [P, DIM]) for u in range(N)]
        x = [sb(f"x_c{u}", [P, DIM]) for u in range(N)]
        rows_in = [sem(f"c_rows_in{u}") for u in range(N)]
        pair_in = [sem(f"c_pair_in{u}") for u in range(N)]
        own, x2_ready = sem("combine_own"), sem("x2_ready")
        x2_stored = [sem(f"x2_stored{u}") for u in range(N)]
        block = ctx.enter_context(nc.Block())
        x1_view = x1.rearrange("b (t j) d -> t j b d", j=STEPS)
        x2_view = x2.rearrange("b (t j) d -> t j b d", j=STEPS)
        shared_view = moe_out[0:TOKENS].rearrange("(b t j) d -> t j b d", b=B, j=STEPS)

        @block.sync
        def _(sp):
            for it in range(TILES):
                u = it % N
                if it >= N:
                    sp.wait_ge(x2_stored[u], 16 * STEPS * (it // N))
                for j in range(STEPS):
                    sp.dma_start(x[u][32 * j:32 * j + 32, :], x1_view[it, j]).then_inc(rows_in[u], 16)
                    sp.dma_start(shared[u][32 * j:32 * j + 32, :], shared_view[it, j]).then_inc(rows_in[u], 16)

        @block.gpsimd
        def _(pool):
            for it in range(TILES):
                u = it % N
                if it >= N:
                    pool.wait_ge(x2_ready, it - N + 1)
                for k in range(2):
                    nc.gpsimd.indirect_dma_start(pair[u][k][:], None, moe_out,
                                                 bass.IndirectOffsetOnAxis(ap=slot[:, it, k:k + 1], axis=0)).then_inc(pair_in[u], 16)

        @block.vector
        def _(dve):
            chain = Chain(dve, own)
            for it in range(TILES):
                u = it % N
                dve.wait_ge(rows_in[u], 16 * 2 * STEPS * (it // N + 1))
                dve.wait_ge(pair_in[u], 32 * (it // N + 1))
                for k in range(2):
                    chain.step(nc.vector.scalar_tensor_tensor(shared[u][:], pair[u][k][:], weight[:, it, k:k + 1], shared[u][:],
                                                              ALU.mult, ALU.add))
                nc.vector.scalar_tensor_tensor(x[u][:], shared[u][:], gate[:, 0:1], x[u][:], ALU.mult, ALU.add).then_inc(x2_ready, 1)

        @block.scalar
        def _(act):
            for it in range(TILES):
                u = it % N
                act.wait_ge(x2_ready, it + 1)
                for j in range(STEPS):
                    act.dma_start(x2_view[it, j], x[u][32 * j:32 * j + 32, :]).then_inc(x2_stored[u], 16)
            for u in range(N):
                act.wait_ge(x2_stored[u], 16 * STEPS * len(range(u, TILES, N)))


BANDS = 4
BAND = -(-KV // BANDS)
LAST_BAND = KV - (BANDS - 1) * BAND
DSTEPS = S + BANDS - 1
FAR = 1.0e30


def band(r):
    return slice(B * r, B * r + B)


def distances(nc, rows, mean, rstd, ctxT, table, ones, ident):
    with ExitStack() as ctx:
        def sb(name, shape, dt=F32):
            return ctx.enter_context(nc.sbuf_tensor("dist_" + name, shape, dt))

        def sem(name):
            return ctx.enter_context(nc.semaphore("dist_" + name))

        c_in = [sb(f"d_ctx{u}", [P, KT, KVP]) for u in range(2)]
        square = [sb(f"d_square{u}", [P, KT, KV]) for u in range(2)]
        xn = [sb(f"d_xn{u}", [S, DIM]) for u in range(2)]
        xx = [sb(f"d_xx{u}", [S, DIM]) for u in range(2)]
        norm = [sb(f"d_norm{u}", [S, 1]) for u in range(2)]
        xT = [sb(f"d_xT{u}", [P, KT, S]) for u in range(2)]
        dist = [sb(f"d_dist{u}", [S, KV]) for u in range(2)]
        ps_x = [ctx.enter_context(nc.psum_tensor(f"d_ps_x{u}", [P, 512], F32)) for u in range(2)]
        ps_d = [ctx.enter_context(nc.psum_tensor(f"d_ps_d{u}", [P, 512], F32)) for u in range(2)]
        ctx_in = [sem("d_ctx_in0"), sem("d_ctx_in1")]
        squared, xn_ready, turned, xT_ready = sem("d_squared"), sem("d_xn_ready"), sem("d_turned"), sem("d_xT_ready")
        norm_ready, summed, square_ready, dist_ready = sem("d_norm_ready"), sem("d_summed"), sem("d_square_ready"), sem("d_dist_ready")
        placed = [sem("d_placed0"), sem("d_placed1")]
        cleared = sem("d_cleared")
        block = ctx.enter_context(nc.Block())

        @block.sync
        def _(sp):
            sp.wait_ge(cleared, 1)
            for b in range(B + 2):
                if b < B:
                    if b >= 2:
                        sp.wait_ge(summed, b - 1)
                        sp.wait_ge(squared, b - 1)
                    sp.dma_start(c_in[b % 2][:], ctxT[b]).then_inc(ctx_in[b % 2], 16)
                if b >= 2:
                    sp.wait_ge(dist_ready, b - 1)
                    for r in range(BANDS):
                        n = BAND if r < BANDS - 1 else LAST_BAND
                        sp.dma_start(table[B * r + b - 2:B * r + b - 1, r:r + S, 0:n],
                                     dist[b % 2][:, r * BAND:r * BAND + n]).then_inc(placed[b % 2], 16)
            for u in range(2):
                sp.wait_ge(placed[u], 16 * BANDS * (B // 2))

        @block.gpsimd
        def _(pool):
            nc.gpsimd.memset(table[:], FAR).then_inc(cleared, 1)
            def turn_of(i):
                for u in range(2):
                    pool.wait_ge(ctx_in[u], 16 * i + 16)
                    pool.wait_ge(summed, 2 * i)
                    nc.gpsimd.tensor_tensor(square[u][:], c_in[u][:, :, 0:KV], c_in[u][:, :, 0:KV], ALU.mult).then_inc(squared, 1)

            repeat(pool, B // 2, turn_of)

        @block.vector
        def _(dve):
            def turn_of(i):
                for u in range(2):
                    b = 2 * i + u
                    dve.wait_ge(turned, 2 * i)
                    dve.wait_ge(norm_ready, 2 * i)
                    normalize(nc, xn[u][:], rows[:, bass.ds(b, 1), :].rearrange("p a n -> p (a n)"), mean, rstd, b).then_inc(xn_ready, 1)
                    dve.wait_ge(turned, b + 1)
                    nc.vector.tensor_scalar(xT[u][:].rearrange("p k s -> p (k s)"), ps_x[u][:, 0:KT * S], -2.0, None, ALU.mult).then_inc(xT_ready, 1)
                    dve.wait_ge(summed, b + 1)
                    dve.wait_ge(norm_ready, b + 1)
                    dve.wait_ge(placed[u], 16 * BANDS * i)
                    nc.vector.tensor_scalar(dist[u][:], ps_d[u][0:S, 0:KV], norm[u][:, 0:1], 0.0, ALU.add, ALU.max).then_inc(square_ready, 1)

            repeat(dve, B // 2, turn_of)

        @block.scalar
        def _(act):
            def turn_of(i):
                for u in range(2):
                    b = 2 * i + u
                    act.wait_ge(xn_ready, b + 1)
                    act.wait_ge(square_ready, 2 * i)
                    nc.scalar.activation(xx[u][:], xn[u][:], ACT.Square, accum_out=norm[u][:, 0:1]).then_inc(norm_ready, 1)
                    act.wait_ge(square_ready, b + 1)
                    nc.scalar.activation(dist[u][:], dist[u][:], ACT.Sqrt).then_inc(dist_ready, 1)

            repeat(act, B // 2, turn_of)

        @block.tensor
        def _(pe):
            def turn_of(i):
                for u in range(2):
                    b = 2 * i + u
                    pe.wait_ge(xn_ready, b + 1)
                    pe.wait_ge(xT_ready, 2 * i)
                    for k in range(KT):
                        last = nc.tensor.transpose(ps_x[u][:, k * S:(k + 1) * S], xn[u][:, k * P:(k + 1) * P], ident[0:S, 0:S])
                    last.then_inc(turned, 1)
                    pe.wait_ge(squared, b + 1)
                    pe.wait_ge(square_ready, 2 * i)
                    for k in range(KT):
                        nc.tensor.matmul(ps_d[u][0:S, 0:KV], ones[:, 0:S], square[u][:, k, :], start=(k == 0), stop=False)
                    pe.wait_ge(xT_ready, b + 1)
                    pe.wait_ge(ctx_in[u], 16 * i + 16)
                    for k in range(KT):
                        last = nc.tensor.matmul(ps_d[u][0:S, 0:KV], xT[u][:, k, :], c_in[u][:, k, 0:KV], start=False, stop=(k == KT - 1))
                    last.then_inc(summed, 1)

            repeat(pe, B // 2, turn_of)


def align(nc, table, on_path, ident):
    with ExitStack() as ctx:
        def sb(name, shape, dt=F32):
            return ctx.enter_context(nc.sbuf_tensor("align_" + name, shape, dt))

        def sem(name):
            return ctx.enter_context(nc.semaphore("align_" + name))

        cost = sb("cost", [P, DSTEPS + 2, BAND + 1])
        least = sb("least", [P, BAND])
        back = sb("back", [P, 2, DSTEPS + 1, BAND + 1], BF16)
        up = sb("up", [P, DSTEPS + 1, BAND + 1], BF16)
        path_words = (DSTEPS + 1) * (BAND + 1)
        path = table[:].rearrange("p s n -> p (s n)").bitcast(BF16)[:, 0:path_words].rearrange("p (s n) -> p s n", n=BAND + 1)
        moved = sb("moved", [P, 2, BAND + 1], BF16)
        entry = sb("entry", [P, BAND], BF16)
        ident16 = sb("ident16", [P, P], BF16)
        ps_p = [ctx.enter_context(nc.psum_tensor(f"ps_p{u}", [P, 512], BF16)) for u in range(2)]
        set_up, own, edge = sem("a_set_up"), sem("align_own"), sem("align_edge")
        path_ready, path_turned, path_kept = sem("path_ready"), sem("path_turned"), sem("path_kept")
        block = ctx.enter_context(nc.Block())
        TURN = 3

        @block.gpsimd
        def _(pool):
            nc.gpsimd.memset(cost[:], FAR).then_inc(set_up, 1)
            pool.wait_ge(set_up, 1)
            nc.gpsimd.memset(cost[0:B, 0:1, 0:1], 0.0).then_inc(set_up, 1)
            nc.gpsimd.memset(back[:], 0.0).then_inc(set_up, 1)
            nc.gpsimd.memset(up[:], 0.0).then_inc(set_up, 1)
            nc.gpsimd.tensor_copy(ident16[:], ident[:]).then_inc(set_up, 1)
            pool.wait_ge(set_up, 5)
            nc.gpsimd.memset(back[:, 1, 0:1, :], 1.0).then_inc(set_up, 1)

        @block.vector
        def _(dve):
            v = nc.vector
            dve.wait_ge(set_up, 6)
            OWN, EDGE = 2, BANDS - 1

            def forward(s):
                dve.wait_ge(edge, EDGE * s)
                here, after = cost[:, bass.ds(s, 1), :], cost[:, bass.ds(s + 1, 1), :]
                v.tensor_tensor(least[:].unsqueeze(1), here[:, :, 0:BAND], here[:, :, 1:BAND + 1], ALU.min).then_inc(own, 1)
                dve.wait_ge(own, OWN * s + 1)
                v.tensor_tensor_scan(after[:, :, 1:BAND + 1].rearrange("p a n -> p (a n)"), least[:],
                                     table[:, bass.ds(s, 1), :].rearrange("p a n -> p (a n)"),
                                     after[:, :, 0:1].rearrange("p a n -> p (a n)"), ALU.min, ALU.add).then_inc(own, 1)
                dve.wait_ge(own, OWN * s + 2)
                for r in range(1, BANDS):
                    v.tensor_copy(cost[band(r), bass.ds(s + 2, 1), 0:1], after[band(r - 1), :, BAND:BAND + 1]).then_inc(edge, 1)

            assert DSTEPS % 3 == 1
            def turn_of(i):
                for u in range(3):
                    forward(3 * i + u)

            repeat(dve, DSTEPS // 3, turn_of)
            forward(DSTEPS - 1)
            dve.wait_ge(edge, EDGE * DSTEPS)
            chain = Chain(dve, own, OWN * DSTEPS)
            before, at = cost[:, 0:DSTEPS, :], cost[:, 1:DSTEPS + 1, :]
            diagonal, above, left = before[:, :, 0:BAND], at[:, :, 0:BAND], before[:, :, 1:BAND + 1]
            is_diagonal, is_left, is_up = (m[:, 1:DSTEPS + 1, 1:BAND + 1][:, ::-1, ::-1] for m in (back[:, 0], back[:, 1], up))
            chain.step(v.tensor_tensor(table[:], above, left, ALU.min))
            chain.step(v.tensor_tensor(is_diagonal, diagonal, table[:], ALU.is_le))
            chain.step(v.tensor_tensor(is_up, above, left, ALU.is_le))
            chain.step(v.tensor_tensor(is_up, is_up, is_diagonal, ALU.is_gt))
            chain.step(v.tensor_tensor(is_left, is_up, is_diagonal, ALU.is_equal))
            for r in range(BANDS - 1):
                chain.step(v.tensor_copy(back[band(r), 0, 2:DSTEPS + 1, 0:1], back[band(r + 1), 0, 1:DSTEPS, BAND:BAND + 1]))
                chain.step(v.tensor_copy(up[band(r), 2:DSTEPS + 1, 0:1], up[band(r + 1), 1:DSTEPS, BAND:BAND + 1]))
            chain.step(v.memset(path[:, :, 0:1], 0.0))
            chain.step(v.memset(path[:, 0:1, :], 0.0))
            chain.step(v.memset(path[band(BANDS - 1), 0:1, BAND - LAST_BAND + 1:BAND - LAST_BAND + 2], 1.0))
            own_before = OWN * DSTEPS + 8 + 2 * (BANDS - 1)

            def backward(n, more=True):
                ahead, here = path[:, bass.ds(n, 1), :], path[:, bass.ds(n + 1, 1), :]
                dve.wait_ge(edge, EDGE * (n + DSTEPS))
                v.tensor_tensor(moved[:], ahead.to_broadcast([P, 2, BAND + 1]),
                                back[:, :, bass.ds(n, 1), :].rearrange("p k a n -> p k (a n)"), ALU.mult).then_inc(own, 1)
                dve.wait_ge(own, own_before + OWN * n + 1)
                v.tensor_tensor(entry[:], moved[:, 0, 0:BAND], moved[:, 1, 1:BAND + 1], ALU.add).then_inc(own, 1)
                dve.wait_ge(own, own_before + OWN * n + 2)
                v.tensor_tensor_scan(here[:, :, 1:BAND + 1].rearrange("p a n -> p (a n)"),
                                     up[:, bass.ds(n + 1, 1), 0:BAND].rearrange("p a n -> p (a n)"), entry[:],
                                     here[:, :, 0:1].rearrange("p a n -> p (a n)"), ALU.mult, ALU.add).then_inc(path_ready, 1)
                dve.wait_ge(path_ready, n + 1)
                if more:
                    for r in range(BANDS - 1):
                        v.tensor_copy(path[band(r), bass.ds(n + 2, 1), 0:1], here[band(r + 1), :, BAND:BAND + 1]).then_inc(edge, 1)

            def turn_of(i):
                for u in range(3):
                    backward(3 * i + u)

            repeat(dve, DSTEPS // 3, turn_of)
            backward(DSTEPS - 1, more=False)

        @block.tensor
        def _(pe):
            pe.wait_ge(set_up, 6)

            def turn_of(i):
                for u in range(2):
                    n = 2 * i + u
                    pe.wait_ge(path_ready, n + 1)
                    pe.wait_ge(path_kept, 2 * i)
                    nc.tensor.matmul(ps_p[u][0:BAND, 0:P], path[:, bass.ds(n + 1, 1), 1:BAND + 1].rearrange("p a n -> p (a n)"),
                                     ident16[:, :], is_transpose=True, start=True, stop=True).then_inc(path_turned, 1)

            repeat(pe, DSTEPS // 2, turn_of)
            pe.wait_ge(path_ready, DSTEPS)
            pe.wait_ge(path_kept, DSTEPS - 1)
            nc.tensor.transpose(ps_p[0][0:BAND, 0:P], path[:, DSTEPS, 1:BAND + 1], ident16[:, :]).then_inc(path_turned, 1)

        @block.scalar
        def _(act):
            def turn_of(i):
                for u in range(2):
                    n = 2 * i + u
                    act.wait_ge(path_turned, n + 1)
                    nc.scalar.copy(on_path[:, bass.ds(DSTEPS - 1 - n, 1), :].rearrange("p a n -> p (a n)"), ps_p[u][0:BAND, 0:P]).then_inc(path_kept, 1)

            repeat(act, DSTEPS // 2, turn_of)
            act.wait_ge(path_turned, DSTEPS)
            nc.scalar.copy(on_path[:, 0, :], ps_p[0][0:BAND, 0:P]).then_inc(path_kept, 1)
            act.wait_ge(path_kept, DSTEPS)


def add_aligned(nc, rows, ctx_rows, on_path, g_xattn, gate):
    with ExitStack() as ctx:
        def sb(name, shape, dt=F32):
            return ctx.enter_context(nc.sbuf_tensor("add_" + name, shape, dt))

        def sem(name):
            return ctx.enter_context(nc.semaphore("add_" + name))

        c_rows = [sb(f"e_ctx{u}", [BAND, BANDS, DIM]) for u in range(2)]
        pick = [sb(f"pick{u}", [BAND, BANDS, S]) for u in range(2)]
        ps_e = [ctx.enter_context(nc.psum_tensor(f"e_ps{u}", [P, 512], F32)) for u in range(2)]
        ctx_in = [sem("e_ctx_in0"), sem("e_ctx_in1")]
        gate_in, gate_ready, pick_ready, summed, added = sem("e_gate_in"), sem("e_gate_ready"), sem("pick_ready"), sem("e_summed"), sem("e_added")
        block = ctx.enter_context(nc.Block())

        @block.sync
        def _(sp):
            sp.dma_start(gate[:, :], g_xattn.partition_broadcast(P)).then_inc(gate_in, 16)
            def turn_of(i):
                for u in range(2):
                    b = 2 * i + u
                    sp.wait_ge(summed, 2 * i)
                    sp.dma_start(c_rows[u][:], ctx_rows[bass.ds(b, 1)].rearrange("a n r d -> (a n) r d")).then_inc(ctx_in[u], 16)

            repeat(sp, B // 2, turn_of)

        @block.scalar
        def _(act):
            act.wait_ge(gate_in, 16)
            nc.scalar.activation(gate[:, :], gate[:, :], ACT.Tanh).then_inc(gate_ready, 1)
            def turn_of(i):
                for u in range(2):
                    b = 2 * i + u
                    act.wait_ge(summed, 2 * i)
                    for r in range(BANDS):
                        nc.scalar.copy(pick[u][:, r, :], on_path[:, r:r + S, bass.ds(B * r + b, 1)].rearrange("p s a -> p (s a)")).then_inc(pick_ready, 1)

            repeat(act, B // 2, turn_of)

        @block.tensor
        def _(pe):
            def turn_of(i):
                for u in range(2):
                    b = 2 * i + u
                    pe.wait_ge(pick_ready, BANDS * b + BANDS)
                    pe.wait_ge(ctx_in[u], 16 * i + 16)
                    pe.wait_ge(added, 2 * i)
                    for r in range(BANDS):
                        last = nc.tensor.matmul(ps_e[u][0:S, 0:DIM], pick[u][:, r, :], c_rows[u][:, r, :],
                                                start=(r == 0), stop=(r == BANDS - 1))
                    last.then_inc(summed, 1)

            repeat(pe, B // 2, turn_of)

        @block.vector
        def _(dve):
            dve.wait_ge(gate_ready, 1)
            def turn_of(i):
                for u in range(2):
                    b = 2 * i + u
                    dve.wait_ge(summed, b + 1)
                    x_b = rows[:, bass.ds(b, 1), :].rearrange("p a n -> p (a n)")
                    nc.vector.scalar_tensor_tensor(x_b, ps_e[u][0:S, 0:DIM], gate[0:S, 1:2], x_b, ALU.mult, ALU.add).then_inc(added, 1)

            repeat(dve, B // 2, turn_of)
            dve.wait_ge(added, B)


F2 = 1024
F2C = F2 // P
CAPACITY = TOKENS // EXPERTS
CT = CAPACITY // S


def route_once(nc, rows, mean, rstd, router, below, ones, ident, iota_s, xn_all, slot_put, slot_get, keep_gate, gate):
    with ExitStack() as ctx:
        def sb(name, shape, dt=F32):
            return ctx.enter_context(nc.sbuf_tensor("once_" + name, shape, dt))

        def sem(name):
            return ctx.enter_context(nc.semaphore("once_" + name))

        x_now = [sb(f"r_x{u}", [S, DIM]) for u in range(2)]
        kept = sem("r_kept")
        wr = sb("wr", [P, KT, EXPERTS])
        xT = [sb(f"r_xT{u}", [P, KT, S]) for u in range(2)]
        logit = sb("logit", [S, B, EXPERTS])
        work = sb("r_work", [S, B, EXPERTS])
        hot = sb("r_hot", [S, B, EXPERTS])
        best = sb("r_best", [S, B])
        index = sb("r_index", [S, B])
        total = sb("r_total", [S, EXPERTS, B])
        upto = sb("r_upto", [S, EXPERTS, B])
        zeros = sb("r_zeros", [S, B])
        place = sb("r_place", [S, B])
        inside = sb("r_inside", [S, B])
        beyond = sb("r_beyond", [S, B])
        token_i = sb("token_i", [S, B], I32)
        token = sb("token", [S, B])
        ps_x = [ctx.enter_context(nc.psum_tensor(f"r_ps_x{u}", [P, 512], F32)) for u in range(2)]
        ps_l = [ctx.enter_context(nc.psum_tensor(f"r_ps_l{u}", [P, 512], F32)) for u in range(2)]
        ps_rank = ctx.enter_context(nc.psum_tensor("r_ps_rank", [P, 512], F32))
        ps_total = ctx.enter_context(nc.psum_tensor("r_ps_total", [P, 512], F32))
        router_in, filled = sem("router_in"), sem("r_filled")
        xn_ready, turned, xT_ready, scored, logit_ready = sem("r_xn_ready"), sem("r_turned"), sem("r_xT_ready"), sem("scored"), sem("logit_ready")
        exp_in, exp_out, hot_ready, ranked, own = sem("r_exp_in"), sem("r_exp_out"), sem("r_hot_ready"), sem("r_ranked"), sem("r_own")
        block = ctx.enter_context(nc.Block())

        @block.sync
        def _(sp):
            sp.dma_start(wr[:], router).then_inc(router_in, 16)
            sp.wait_ge(router_in, 16)

        @block.gpsimd
        def _(pool):
            nc.gpsimd.iota(token_i[:], pattern=[[S, B]], base=TOKENS, channel_multiplier=1).then_inc(filled, 1)
            nc.gpsimd.memset(zeros[:], 0.0).then_inc(filled, 1)
            pool.wait_ge(filled, 2)
            nc.gpsimd.tensor_copy(token[:], token_i[:]).then_inc(filled, 1)

        @block.tensor
        def _(pe):
            pe.wait_ge(router_in, 16)
            def turn_of(i):
                for u in range(2):
                    b = 2 * i + u
                    pe.wait_ge(xn_ready, b + 1)
                    pe.wait_ge(xT_ready, 2 * i)
                    for k in range(KT):
                        last = nc.tensor.transpose(ps_x[u][:, k * S:(k + 1) * S], x_now[u][:, k * P:(k + 1) * P], ident[0:S, 0:S])
                    last.then_inc(turned, 1)
                    pe.wait_ge(xT_ready, b + 1)
                    pe.wait_ge(logit_ready, 2 * i)
                    for k in range(KT):
                        last = nc.tensor.matmul(ps_l[u][0:S, 0:EXPERTS], xT[u][:, k, :], wr[:, k, :], start=(k == 0), stop=(k == KT - 1))
                    last.then_inc(scored, 1)

            repeat(pe, B // 2, turn_of)
            pe.wait_ge(hot_ready, 1)
            flat = hot[:].rearrange("p b e -> p (b e)")
            nc.tensor.matmul(ps_rank[0:S, 0:B * EXPERTS], below[0:S, 0:S], flat, start=True, stop=True).then_inc(ranked, 1)
            nc.tensor.matmul(ps_total[0:S, 0:B * EXPERTS], ones[0:S, 0:S], flat, start=True, stop=True).then_inc(ranked, 1)

        @block.scalar
        def _(act):
            def turn_of(i):
                for u in range(2):
                    b = 2 * i + u
                    act.wait_ge(xn_ready, b + 1)
                    nc.scalar.copy(xn_all[:, bass.ds(b, 1), :].rearrange("p a n -> p (a n)"), x_now[u][:]).then_inc(kept, 1)
                    act.wait_ge(turned, b + 1)
                    nc.scalar.copy(xT[u][:].rearrange("p k s -> p (k s)"), ps_x[u][:, 0:KT * S]).then_inc(xT_ready, 1)

            repeat(act, B // 2, turn_of)
            act.wait_ge(exp_in, 1)
            nc.scalar.activation(logit[:], logit[:], ACT.Exp).then_inc(exp_out, 1)
            act.wait_ge(kept, B)

        @block.vector
        def _(dve):
            v = nc.vector
            chain = Chain(dve, own)
            def turn_of(i):
                for u in range(2):
                    b = 2 * i + u
                    dve.wait_ge(turned, 2 * i)
                    dve.wait_ge(kept, 2 * i)
                    normalize(nc, x_now[u][:], rows[:, bass.ds(b, 1), :].rearrange("p a n -> p (a n)"), mean, rstd, b).then_inc(xn_ready, 1)
                    dve.wait_ge(scored, b + 1)
                    v.tensor_copy(logit[:, bass.ds(b, 1), :].rearrange("p a n -> p (a n)"), ps_l[u][0:S, 0:EXPERTS]).then_inc(logit_ready, 1)

            repeat(dve, B // 2, turn_of)
            dve.wait_ge(logit_ready, B)

            def every(a):
                return a[:].unsqueeze(2).to_broadcast([S, B, EXPERTS])

            chain.step(v.tensor_reduce(best[:], logit[:], AX.X, ALU.max))
            v.tensor_tensor(logit[:], logit[:], every(best), ALU.subtract).then_inc(exp_in, 1)
            dve.wait_ge(exp_out, 1)
            chain.step(v.tensor_reduce(inside[:], logit[:], AX.X, ALU.add))
            chain.step(v.reciprocal(keep_gate[:], inside[:]))
            chain.step(v.tensor_scalar(keep_gate[:], keep_gate[:], gate[0:S, 1:2], None, ALU.mult))
            chain.step(v.tensor_reduce(best[:], logit[:], AX.X, ALU.max))
            chain.step(v.tensor_tensor(work[:], logit[:], every(best), ALU.is_lt))
            chain.step(v.scalar_tensor_tensor(work[:], work[:], 2.0 * EXPERTS, iota_s[:], ALU.mult, ALU.add))
            chain.step(v.tensor_reduce(index[:], work[:], AX.X, ALU.min))
            v.tensor_tensor(hot[:], iota_s[:], every(index), ALU.is_equal).then_inc(hot_ready, 1)
            dve.wait_ge(ranked, 2)
            dve.wait_ge(filled, 3)
            chain.step(v.tensor_copy(total[:], ps_total[0:S, 0:B * EXPERTS].rearrange("p (b e) -> p e b", e=EXPERTS)))
            for e in range(EXPERTS):
                chain.step(v.tensor_tensor_scan(upto[:, e, :], zeros[:], total[:, e, :], 0.0, ALU.add, ALU.add))
            chain.step(v.tensor_tensor(upto[:], upto[:], total[:], ALU.subtract))
            chain.step(v.tensor_tensor(work[:], ps_rank[0:S, 0:B * EXPERTS].rearrange("p (b e) -> p b e", e=EXPERTS),
                                       upto[:].rearrange("p e b -> p b e"), ALU.add))
            chain.step(v.tensor_tensor(work[:], work[:], hot[:], ALU.mult))
            chain.step(v.tensor_reduce(place[:], work[:], AX.X, ALU.add))
            chain.step(v.tensor_scalar(inside[:], place[:], float(CAPACITY), None, ALU.is_le))
            chain.step(v.tensor_tensor(keep_gate[:], keep_gate[:], inside[:], ALU.mult))
            chain.step(v.scalar_tensor_tensor(place[:], index[:], float(CAPACITY), place[:], ALU.mult, ALU.add))
            chain.step(v.tensor_scalar(place[:], place[:], -1.0, None, ALU.add))
            chain.step(v.tensor_tensor(place[:], place[:], inside[:], ALU.mult))
            chain.step(v.tensor_copy(slot_get[:], place[:]))
            chain.step(v.tensor_scalar(beyond[:], inside[:], -1.0, 1.0, ALU.mult, ALU.add))
            chain.step(v.tensor_tensor(beyond[:], beyond[:], token[:], ALU.mult))
            chain.step(v.tensor_tensor(place[:], place[:], beyond[:], ALU.add))
            chain.step(v.tensor_copy(slot_put[:], place[:]))


def dispatch(nc, xn_all, slot_put, buffer):
    with ExitStack() as ctx:
        put = ctx.enter_context(nc.semaphore("dispatched"))
        block = ctx.enter_context(nc.Block())

        @block.gpsimd
        def _(pool):
            for b in range(B):
                nc.gpsimd.indirect_dma_start(buffer, bass.IndirectOffsetOnAxis(ap=slot_put[:, b:b + 1], axis=0),
                                             xn_all[:, b, :], None).then_inc(put, 16)
            pool.wait_ge(put, 16 * B)


def capacity_experts(nc, buffer, result, w1, b1, w2, b2, ident):
    with ExitStack() as ctx:
        def sb(name, shape, dt=F32):
            return ctx.enter_context(nc.sbuf_tensor("cap_" + name, shape, dt))

        def ps(name):
            return ctx.enter_context(nc.psum_tensor("cap_" + name, [P, 512], F32))

        def sem(name):
            return ctx.enter_context(nc.semaphore("cap_" + name))

        w1_sb = [sb(f"w1_{u}", [P, KT, F2]) for u in range(2)]
        w2_sb = [sb(f"w2_{u}", [P, F2C, DIM]) for u in range(2)]
        b2_sb = [sb(f"b2_{u}", [S, DIM]) for u in range(2)]
        b1_sb = sb("b1_sb", [P, EXPERTS, F2C])
        x = [sb(f"f_x{u}", [S, CT, DIM]) for u in range(2)]
        xT = sb("f_xT", [P, KT, CAPACITY])
        mid = sb("f_mid", [P, F2C, CAPACITY])
        y = [sb(f"f_y{u}", [S, CT, DIM]) for u in range(2)]
        ps_x = [ps(f"f_ps_x{u}") for u in range(KT)]
        ps_m = [ps(f"f_ps_m{u}") for u in range(2)]
        ps_y = [ps(f"f_ps_y{u}") for u in range(2)]
        bias_in = sem("f_bias_in")
        loaded, stored = [sem("f_loaded0"), sem("f_loaded1")], [sem("f_stored0"), sem("f_stored1")]
        turned, xT_ready, m_done, mid_ready, y_done, y_ready = (sem("f_turned"), sem("f_xT_ready"), sem("f_m_done"),
                                                               sem("f_mid_ready"), sem("f_y_done"), sem("f_y_ready"))
        block = ctx.enter_context(nc.Block())

        def one(dram, e):
            return dram[bass.ds(e, 1)]

        @block.sync
        def _(sp):
            sp.dma_start(b1_sb[:], b1).then_inc(bias_in, 16)
            def turn_of(i):
                for u in range(2):
                    e = 2 * i + u
                    sp.wait_ge(y_ready, CT * 2 * i)
                    sp.dma_start(x[u][:], buffer[bass.ds(e * CAPACITY, CAPACITY), :].rearrange("(c s) d -> s c d", s=S)).then_inc(loaded[u], 16)
                    sp.dma_start(w1_sb[u][:], one(w1, e).rearrange("a p k n -> (a p) k n")).then_inc(loaded[u], 16)
                    sp.dma_start(w2_sb[u][:], one(w2, e).rearrange("a p k n -> (a p) k n")).then_inc(loaded[u], 16)
                    sp.dma_start(b2_sb[u][:], one(b2, e).rearrange("a n -> (a n)").partition_broadcast(S)).then_inc(loaded[u], 16)

            repeat(sp, EXPERTS // 2, turn_of)
            sp.wait_ge(bias_in, 16)

        @block.gpsimd
        def _(pool):
            def turn_of(i):
                for u in range(2):
                    e = 2 * i + u
                    pool.wait_ge(y_ready, CT * e + CT)
                    pool.dma_start(result[bass.ds(e * CAPACITY, CAPACITY), :].rearrange("(c s) d -> s c d", s=S), y[u][:]).then_inc(stored[u], 16)

            repeat(pool, EXPERTS // 2, turn_of)
            for u in range(2):
                pool.wait_ge(stored[u], 16 * (EXPERTS // 2))

        @block.tensor
        def _(pe):
            def turn_of(i):
                for u in range(2):
                    e = 2 * i + u
                    pe.wait_ge(loaded[u], 64 * i + 64)
                    pe.wait_ge(xT_ready, KT * e)
                    for k in range(KT):
                        for c in range(CT):
                            last = nc.tensor.transpose(ps_x[k][:, c * S:(c + 1) * S], x[u][:, c, k * P:(k + 1) * P], ident[0:S, 0:S])
                        last.then_inc(turned, 1)
                    pe.wait_ge(xT_ready, KT * e + KT)
                    for f in range(F2C):
                        n = F2C * e + f
                        if f >= 2:
                            pe.wait_ge(mid_ready, n - 1)
                        else:
                            pe.wait_ge(mid_ready, F2C * e)
                        for k in range(KT):
                            last = nc.tensor.matmul(ps_m[f % 2][:, 0:CAPACITY], w1_sb[u][:, k, f * P:(f + 1) * P], xT[:, k, :],
                                                    start=(k == 0), stop=(k == KT - 1))
                        last.then_inc(m_done, 1)
                    pe.wait_ge(mid_ready, F2C * e + F2C)
                    for c in range(CT):
                        if c >= 2:
                            pe.wait_ge(y_ready, CT * e + c - 1)
                        else:
                            pe.wait_ge(y_ready, CT * e)
                        for f in range(F2C):
                            last = nc.tensor.matmul(ps_y[c % 2][0:S, 0:DIM], mid[:, f, c * S:(c + 1) * S], w2_sb[u][:, f, :],
                                                    start=(f == 0), stop=(f == F2C - 1))
                        last.then_inc(y_done, 1)

            repeat(pe, EXPERTS // 2, turn_of)

        @block.scalar
        def _(act):
            act.wait_ge(bias_in, 16)
            def turn_of(i):
                for u in range(2):
                    e = 2 * i + u
                    act.wait_ge(y_done, CT * e)
                    for f in range(F2C):
                        act.wait_ge(m_done, F2C * e + f + 1)
                        nc.scalar.activation(mid[:, f, :], ps_m[f % 2][:, 0:CAPACITY], ACT.Relu,
                                             bias=b1_sb[:, bass.ds(e, 1), f:f + 1].rearrange("p a n -> p (a n)")).then_inc(mid_ready, 1)

            repeat(act, EXPERTS // 2, turn_of)

        @block.vector
        def _(dve):
            def turn_of(i):
                for u in range(2):
                    e = 2 * i + u
                    dve.wait_ge(m_done, F2C * e)
                    for k in range(KT):
                        dve.wait_ge(turned, KT * e + k + 1)
                        nc.vector.tensor_copy(xT[:, k, :], ps_x[k][:, 0:CAPACITY]).then_inc(xT_ready, 1)
                    dve.wait_ge(stored[u], 16 * i)
                    dve.wait_ge(loaded[u], 64 * i + 64)
                    for c in range(CT):
                        dve.wait_ge(y_done, CT * e + c + 1)
                        nc.vector.tensor_tensor(y[u][:, c, :], ps_y[c % 2][0:S, 0:DIM], b2_sb[u][:], ALU.add).then_inc(y_ready, 1)

            repeat(dve, EXPERTS // 2, turn_of)


def finish(nc, rows, result, slot_get, keep_gate, out):
    with ExitStack() as ctx:
        N = 8
        got = [ctx.enter_context(nc.sbuf_tensor(f"got{u}", [S, DIM], F32)) for u in range(N)]
        got_in = [ctx.enter_context(nc.semaphore(f"got_in{u}")) for u in range(N)]
        out_ready = ctx.enter_context(nc.semaphore("out_ready"))
        out_stored = ctx.enter_context(nc.semaphore("out_stored"))
        block = ctx.enter_context(nc.Block())

        @block.gpsimd
        def _(pool):
            for b in range(B):
                if b >= N:
                    pool.wait_ge(out_ready, b - N + 1)
                nc.gpsimd.indirect_dma_start(got[b % N][:], None, result,
                                             bass.IndirectOffsetOnAxis(ap=slot_get[:, b:b + 1], axis=0)).then_inc(got_in[b % N], 16)

        @block.vector
        def _(dve):
            for b in range(B):
                dve.wait_ge(got_in[b % N], 16 * (b // N + 1))
                nc.vector.scalar_tensor_tensor(rows[:, b, :], got[b % N][:], keep_gate[:, b:b + 1], rows[:, b, :],
                                               ALU.mult, ALU.add).then_inc(out_ready, 1)

        @block.sync
        def _(sp):
            def turn_of(b):
                sp.wait_ge(out_ready, b + 1)
                sp.dma_start(out[bass.ds(b, 1)].rearrange("a s d -> (a s) d"),
                             rows[:, bass.ds(b, 1), :].rearrange("p a n -> p (a n)")).then_inc(out_stored, 16)

            repeat(sp, B, turn_of)
            sp.wait_ge(out_stored, 16 * B)


def constants_for_routing(nc, below, iota_e, iota_s):
    with ExitStack() as ctx:
        counted_e = ctx.enter_context(nc.sbuf_tensor("counted_e", [P, TILES, EXPERTS], I32))
        counted_s = ctx.enter_context(nc.sbuf_tensor("counted_s", [S, B, EXPERTS], I32))
        counted = ctx.enter_context(nc.semaphore("counted"))
        block = ctx.enter_context(nc.Block())

        @block.gpsimd
        def _(pool):
            nc.gpsimd.memset(below[:], 1.0).then_inc(counted, 1)
            nc.gpsimd.iota(counted_e[:], pattern=[[0, TILES], [1, EXPERTS]], base=0, channel_multiplier=0).then_inc(counted, 1)
            nc.gpsimd.iota(counted_s[:], pattern=[[0, B], [1, EXPERTS]], base=0, channel_multiplier=0).then_inc(counted, 1)
            pool.wait_ge(counted, 3)
            nc.gpsimd.affine_select(out=below[:], in_=below[:], compare_op=ALU.is_ge, fill=0.0, base=0,
                                    pattern=[[1, P]], channel_multiplier=-1).then_inc(counted, 1)
            nc.gpsimd.tensor_copy(iota_e[:], counted_e[:]).then_inc(counted, 1)
            nc.gpsimd.tensor_copy(iota_s[:], counted_s[:]).then_inc(counted, 1)
            pool.wait_ge(counted, 6)


def clear_semaphores(nc):
    numbers = sorted(nc.released_uncleared_semaphores)
    starts = [n for n in numbers if n - 1 not in numbers]
    with nc.Block() as block:

        @block.gpsimd
        def _(pool):
            for first in starts:
                stop = first
                while stop in numbers:
                    stop += 1
                pool.sem_clear(range(first, stop))


def build(nc, x, ctx_rows, ctxT, wqT, wkT, bqk, wvT, bv, woT, bo, g_xattn, g_ffn, whhT, wihT, wcT, ctx_b, weT, guT, dnT,
          router, w1, b1, w2, b2, out):
    def dram(name, shape):
        return nc.dram_tensor(name, shape, F32, kind="Internal").ap()

    x1 = dram("x1", (B, S, DIM))
    x2 = dram("x2", (B, S, DIM))
    states = dram("states", (TILES, STEPS, B, GD))
    moe_in = dram("moe_in", (MOE_TILES * P, DIM))
    moe_out = dram("moe_out", (MOE_TILES * P, DIM))
    buffer = dram("buffer", (2 * TOKENS, DIM))
    result = dram("result", (TOKENS, DIM))
    h_rows = moe_in[0:TOKENS].rearrange("(b s) d -> b s d", b=B)

    def pieces(rows, n):
        flat = rows.rearrange("r d -> (r d)").rearrange("(p c w) -> c p w", p=P, c=n)
        return [(flat[c], flat.shape[2]) for c in range(n)]

    to_clear = pieces(moe_in[TOKENS:MOE_TILES * P], 8) + pieces(buffer[0:TOKENS], 4)

    with ExitStack() as ctx:
        def sb(stack, name, shape, dt=F32, **more):
            return stack.enter_context(nc.sbuf_tensor(name, shape, dt, **more))

        ident = sb(ctx, "ident", [P, P])
        ones = sb(ctx, "ones", [P, P])
        gate = sb(ctx, "gate_ffn", [P, 2])
        gate_x = sb(ctx, "gate_x", [P, 2])
        below = sb(ctx, "below", [P, P])
        iota_e = sb(ctx, "iota_e", [P, TILES, EXPERTS])
        iota_s = sb(ctx, "iota_s", [S, B, EXPERTS])
        neg_ident = sb(ctx, "neg_ident", [P, P])
        whh_in = ctx.enter_context(nc.semaphore("whh_in"))
        cleared_rows = ctx.enter_context(nc.semaphore("cleared_rows"))
        experts_in = ctx.enter_context(nc.semaphore("experts_in"))
        constants(nc, ident, neg_ident, ones)
        constants_for_routing(nc, below, iota_e, iota_s)

        with ExitStack() as mixture:
            stat = sb(mixture, "stat", [P, TILES, NSTAT])
            with ExitStack() as recurrent:
                whh = sb(recurrent, "whh", [P, GC, 3 * GD])
                with ExitStack() as first:
                    rows = sb(first, "rows_x", [S, B, DIM], side="right")
                    mean = sb(first, "mean_x", [S, B], side="right")
                    rstd = sb(first, "rstd_x", [S, B], side="right")
                    load_rows(nc, "x", rows, x)
                    row_statistics(nc, "x", rows, mean[:], rstd[:])
                    attention(nc, rows, mean, rstd, ctxT, wqT, wkT, bqk, wvT, bv, woT, bo, g_xattn, x1, ident, neg_ident,
                              whh, whhT, whh_in, to_clear, cleared_rows)
                    row_statistics(nc, "x1", rows, mean[:], rstd[:])
                    hT = sb(recurrent, "hT", [P, KT, B, S])
                    normalized_rows_out(nc, rows, mean, rstd, h_rows, hT, ident)
                gru(nc, whh, whh_in, wihT, hT, wcT, ctx_b, weT, states, stat, ident)
            weight = sb(mixture, "weight", [P, TILES, 2])
            slot = sb(mixture, "slot", [P, TILES, 2], U32)
            tile_expert = sb(mixture, "tile_expert", [1, MOE_TILES], I32)
            with ExitStack() as experts:
                gu = sb(experts, "gu", [P, EXPERTS + 1, KT, 2 * FF])
                dn = sb(experts, "dn", [P, EXPERTS + 1, FC, DIM])
                routing(nc, stat, weight, slot, tile_expert, iota_e, below, ones, g_ffn, gate, gu, guT, dn, dnT, experts_in)
                scatter_rows(nc, h_rows, moe_in, slot)
                expert_tiles(nc, moe_in, moe_out, gu, dn, tile_expert, experts_in, ident)
            combine(nc, moe_out, x1, weight, slot, gate, x2)

        clear_semaphores(nc)
        rows = sb(ctx, "rows", [S, B, DIM])
        mean = sb(ctx, "mean", [S, B])
        rstd = sb(ctx, "rstd", [S, B])
        load_rows(nc, "x2", rows, x2)
        row_statistics(nc, "x2", rows, mean[:], rstd[:])
        with ExitStack() as alignment:
            on_path = sb(alignment, "on_path", [BAND, DSTEPS, P], BF16)
            with ExitStack() as tables:
                table = sb(tables, "table", [P, DSTEPS, BAND])
                distances(nc, rows, mean, rstd, ctxT, table, ones, ident)
                align(nc, table, on_path, ident)
            add_aligned(nc, rows, ctx_rows, on_path, g_xattn, gate_x)
        row_statistics(nc, "x3", rows, mean[:], rstd[:])
        with ExitStack() as last:
            xn_all = sb(last, "xn_all", [S, B, DIM])
            slot_put = sb(last, "slot_put", [S, B], U32)
            slot_get = sb(last, "slot_get", [S, B], U32)
            keep_gate = sb(last, "keep_gate", [S, B])
            route_once(nc, rows, mean, rstd, router, below, ones, ident, iota_s, xn_all, slot_put, slot_get, keep_gate, gate)
            dispatch(nc, xn_all, slot_put, buffer)
            capacity_experts(nc, buffer, result, w1, b1, w2, b2, ident)
            finish(nc, rows, result, slot_get, keep_gate, out)


def layouts(i):
    import numpy as np

    def tiles(w):
        return w.T.reshape(-1, P, w.shape[0]).transpose(1, 0, 2)

    def pad_heads(w):
        out = np.zeros((P, KT, HG, 4, 32), w.dtype)
        out[..., 0:HD] = w.reshape(HG, 4, HD, KT, P).transpose(4, 3, 0, 1, 2)
        return out.reshape(P, KT, HG * P)

    att, ffn, moe = "L0_xattn_", "L0_ffn_", "L1_ffn_"
    ctxT = np.zeros((B, P, KT, KVP), i["ctx_1024"].dtype)
    ctxT[..., 0:KV] = i["ctx_1024"].reshape(B, KV, KT, P).transpose(0, 3, 2, 1)
    ctx_rows = np.zeros((B, BANDS * BAND, DIM), i["ctx_1024"].dtype)
    ctx_rows[:, 0:KV] = i["ctx_1024"]
    ctx_rows = ctx_rows.reshape(B, BANDS, BAND, DIM)[:, :, ::-1].transpose(0, 2, 1, 3)
    bqk = np.zeros((4, 32, 2, HG), i[att + "bq"].dtype)
    bqk[:, 0:HD, 0, :] = i[att + "bq"].reshape(HG, 4, HD).transpose(1, 2, 0)
    bqk[:, 0:HD, 1, :] = i[att + "bk"].reshape(HG, 4, HD).transpose(1, 2, 0)
    bqk[:, HD, 1, :] = 1

    def with_shared(name):
        return np.concatenate([i[ffn + name], i[ffn + "shared_" + name][None]])

    gate_up = np.concatenate([with_shared("gate_w"), with_shared("up_w")], 1)
    return {
        "x": i["x"], "ctx_rows": ctx_rows, "ctxT": ctxT,
        "wqT": pad_heads(i[att + "Wq"]), "wkT": pad_heads(i[att + "Wk"]), "bqk": bqk.reshape(P, 2, HG),
        "wvT": tiles(i[att + "Wv"]), "bv": i[att + "bv"], "woT": tiles(i[att + "Wo"]), "bo": i[att + "bo"],
        "g_xattn": i["g_xattn"], "g_ffn": i["g_ffn"],
        "whhT": tiles(i[ffn + "gru_w_hh"]), "wihT": tiles(i[ffn + "gru_w_ih"]), "wcT": tiles(i[ffn + "ctx_w"]),
        "ctx_b": i[ffn + "ctx_b"], "weT": tiles(i[ffn + "expr_w"]),
        "guT": gate_up.reshape(EXPERTS + 1, 2 * FF, KT, P).transpose(3, 0, 2, 1),
        "dnT": with_shared("down_w").reshape(EXPERTS + 1, DIM, FC, P).transpose(3, 0, 2, 1),
        "router": i[moe + "router_w"].reshape(KT, P, EXPERTS).transpose(1, 0, 2),
        "w1": i[moe + "w1"].reshape(EXPERTS, KT, P, F2).transpose(0, 2, 1, 3),
        "b1": i[moe + "b1"].reshape(EXPERTS, F2C, P).transpose(2, 0, 1),
        "w2": i[moe + "w2"].reshape(EXPERTS, F2C, P, DIM).transpose(0, 2, 1, 3),
        "b2": i[moe + "b2"],
    }


def kernel(**inputs):
    import numpy as np
    import concourse.bacc as bacc
    from concourse.bass_utils import run_bass_kernel_spmd

    nc = bacc.Bacc("TRN2", target_bir_lowering=False, num_devices=1)
    arrays, args = {}, []
    for name, a in layouts({k: np.asarray(v) for k, v in inputs.items()}).items():
        a = np.ascontiguousarray(a)
        arrays[f"in_{name}"] = a
        args.append(nc.dram_tensor(f"in_{name}", a.shape, mybir.dt.from_np(a.dtype), kind="ExternalInput").ap())
    args.append(nc.dram_tensor("out_x", (B, S, DIM), F32, kind="ExternalOutput").ap())
    build(nc, *args)
    result = run_bass_kernel_spmd(nc, [arrays], core_ids=[0])
    return result.results[0]["out_x"]
```

```python
from contextlib import ExitStack

import concourse.bass as bass
from concourse import mybir

F32 = mybir.dt.float32
BF16 = mybir.dt.bfloat16
I32 = mybir.dt.int32
U32 = mybir.dt.uint32
ALU = mybir.AluOpType
ACT = mybir.ActivationFunctionType
AX = mybir.AxisListType

P = 128
B, S, DIM = 32, 100, 256
KV, KC = 361, 121
KVP = 3 * KC
KLAST = KV - 2 * KC
KT = DIM // P
HEADS, HD = 16, 16
HG = HEADS // 4
LN_EPS = 1e-5


class Chain:

    def __init__(self, engine, semaphore, start=0):
        self.engine, self.semaphore, self.value = engine, semaphore, start

    def step(self, instruction):
        self.value = self.value + 1
        instruction.then_inc(self.semaphore, 1)
        self.engine.wait_ge(self.semaphore, self.value)

    def together(self, *instructions):
        for instruction in instructions:
            instruction.then_inc(self.semaphore, 1)
        self.value = self.value + len(instructions)
        self.engine.wait_ge(self.semaphore, self.value)


def repeat(engine, count, turn_of):
    turn_of(0)
    with engine.Fori(1, count) as i:
        turn_of(i)


def reused(engine, semaphore, i, u, of, per=1):
    if not isinstance(i, int):
        engine.wait_ge(semaphore, per * (of * (i - 1) + u + 1))


def row_statistics(nc, stage, rows, mean, rstd):
    with ExitStack() as ctx:
        GROUP = 8
        stats = ctx.enter_context(nc.sbuf_tensor(f"stats_{stage}", [S, GROUP, 6], F32))
        mean_var = ctx.enter_context(nc.sbuf_tensor(f"mean_var_{stage}", [S, GROUP, 2], F32))
        stats_done = ctx.enter_context(nc.semaphore(f"stats_done_{stage}"))
        aggregated = ctx.enter_context(nc.semaphore(f"aggregated_{stage}"))
        taken = ctx.enter_context(nc.semaphore(f"taken_{stage}"))
        root_ready = ctx.enter_context(nc.semaphore(f"root_ready_{stage}"))
        block = ctx.enter_context(nc.Block())

        @block.vector
        def _(dve):
            for g in range(B // GROUP):
                for u in range(GROUP):
                    nc.vector.bn_stats(stats[:, u, :], rows[:, GROUP * g + u, :]).then_inc(stats_done, 1)
                dve.wait_ge(taken, 2 * g)
                for u in range(GROUP):
                    dve.wait_ge(stats_done, GROUP * g + u + 1)
                    nc.vector.bn_aggr(mean_var[:, u, :], stats[:, u, :]).then_inc(aggregated, 1)
                dve.wait_ge(aggregated, GROUP * g + GROUP)
                group = slice(GROUP * g, GROUP * g + GROUP)
                nc.vector.tensor_copy(mean[:, group], mean_var[:, :, 0]).then_inc(taken, 1)
                nc.vector.tensor_scalar(rstd[:, group], mean_var[:, :, 1], LN_EPS, None, ALU.add).then_inc(taken, 1)
            dve.wait_ge(taken, 2 * (B // GROUP) - 1)
            dve.wait_ge(root_ready, 1)
            nc.vector.reciprocal(rstd, rstd).then_inc(aggregated, 1)
            dve.wait_ge(aggregated, B + 1)

        @block.scalar
        def _(act):
            act.wait_ge(taken, 2 * (B // GROUP))
            nc.scalar.activation(rstd, rstd, ACT.Sqrt).then_inc(root_ready, 1)


def normalize(nc, out, rows, mean, rstd, b):
    return nc.vector.tensor_scalar(out, rows, mean[:, bass.ds(b, 1)], rstd[:, bass.ds(b, 1)], ALU.subtract, ALU.mult)


def load_rows(nc, stage, rows, source):
    with ExitStack() as ctx:
        rows_in = ctx.enter_context(nc.semaphore(f"rows_in_{stage}"))
        block = ctx.enter_context(nc.Block())

        @block.sync
        def _(sp):
            for n in range(4):
                some = slice(n * B // 4, (n + 1) * B // 4)
                sp.dma_start(rows[:, some, :], source[some].rearrange("b s d -> s b d")).then_inc(rows_in, 16)
            sp.wait_ge(rows_in, 4 * 16)


def normalized_rows_out(nc, rows, mean, rstd, h_rows, hT, ident):
    AT_ONCE = 4
    with ExitStack() as ctx:
        h = [ctx.enter_context(nc.sbuf_tensor(f"h{u}", [S, DIM], F32)) for u in range(AT_ONCE)]
        turned = [ctx.enter_context(nc.psum_tensor(f"turned{u}", [P, 512], F32)) for u in range(AT_ONCE)]
        h_ready = ctx.enter_context(nc.semaphore("h_ready"))
        h_stored = [ctx.enter_context(nc.semaphore(f"h_stored{u}")) for u in range(AT_ONCE)]
        h_turned = ctx.enter_context(nc.semaphore("h_turned"))
        hT_ready = ctx.enter_context(nc.semaphore("hT_ready"))
        block = ctx.enter_context(nc.Block())

        @block.vector
        def _(dve):
            def turn_of(i):
                for u in range(AT_ONCE):
                    b = AT_ONCE * i + u
                    dve.wait_ge(h_stored[u], 16 * i)
                    reused(dve, h_turned, i, u, AT_ONCE)
                    normalize(nc, h[u][:], rows[:, bass.ds(b, 1), :].rearrange("p a n -> p (a n)"), mean, rstd, b).then_inc(h_ready, 1)

            repeat(dve, B // AT_ONCE, turn_of)

        @block.tensor
        def _(pe):
            def turn_of(i):
                for u in range(AT_ONCE):
                    b = AT_ONCE * i + u
                    pe.wait_ge(h_ready, b + 1)
                    reused(pe, hT_ready, i, u, AT_ONCE)
                    for k in range(KT):
                        last = nc.tensor.transpose(turned[u][:, k * S:(k + 1) * S], h[u][:, k * P:(k + 1) * P], ident[0:S, 0:S])
                    last.then_inc(h_turned, 1)

            repeat(pe, B // AT_ONCE, turn_of)

        @block.scalar
        def _(act):
            def turn_of(i):
                for u in range(AT_ONCE):
                    b = AT_ONCE * i + u
                    act.wait_ge(h_turned, b + 1)
                    nc.scalar.copy(hT[:, :, bass.ds(b, 1), :].rearrange("p k a s -> p k (a s)"),
                                   turned[u][:, 0:KT * S].rearrange("p (k s) -> p k s", k=KT)).then_inc(hT_ready, 1)

            repeat(act, B // AT_ONCE, turn_of)
            act.wait_ge(hT_ready, B)

        @block.sync
        def _(sp):
            def turn_of(i):
                for u in range(AT_ONCE):
                    b = AT_ONCE * i + u
                    sp.wait_ge(h_ready, b + 1)
                    sp.dma_start(h_rows[bass.ds(b, 1)].rearrange("a s d -> (a s) d"), h[u][:]).then_inc(h_stored[u], 16)

            repeat(sp, B // AT_ONCE, turn_of)
            for u in range(AT_ONCE):
                sp.wait_ge(h_stored[u], 16 * (B // AT_ONCE))


def constants(nc, ident, neg_ident, one_row):
    with ExitStack() as ctx:
        filled = ctx.enter_context(nc.semaphore("const_filled"))
        block = ctx.enter_context(nc.Block())

        @block.gpsimd
        def _(pool):
            nc.gpsimd.memset(ident[:, :], 0.0).then_inc(filled, 1)
            nc.gpsimd.memset(neg_ident[:, :], 0.0).then_inc(filled, 1)
            nc.gpsimd.memset(one_row[:, :], 1.0).then_inc(filled, 1)
            pool.wait_ge(filled, 3)
            nc.gpsimd.affine_select(out=ident[:, :], in_=ident[:, :], compare_op=ALU.not_equal, fill=1.0,
                                    base=0, pattern=[[-1, P]], channel_multiplier=1).then_inc(filled, 1)
            nc.gpsimd.affine_select(out=neg_ident[:, :], in_=neg_ident[:, :], compare_op=ALU.not_equal,
                                    fill=-1.0, base=0, pattern=[[-1, P]], channel_multiplier=1).then_inc(filled, 1)
            pool.wait_ge(filled, 5)


def pipelined(engine, count, turn_of):
    turn_of(0, 0, True, False)
    with engine.Fori(1, count // 2) as i:
        turn_of(2 * i - 1, 1, False, False)
        turn_of(2 * i, 0, False, False)
    turn_of(count - 1, (count - 1) % 2, False, True)


def attention(nc, rows, mean, rstd, ctxT, wqT, wkT, bqk, wvT, bv, woT, bo, g_xattn, x1, ident, neg_ident,
              whh, whhT, whh_in, to_clear, cleared_rows):
    with ExitStack() as ctx:
        def sb(name, shape, dt=F32):
            return ctx.enter_context(nc.sbuf_tensor("att_" + name, shape, dt))

        def ps(name):
            return ctx.enter_context(nc.psum_tensor("att_" + name, [P, 512], F32))

        def sem(name):
            return ctx.enter_context(nc.semaphore("att_" + name))

        PAIRS = HEADS // 2
        wq = sb("wq", [P, KT, HG * P])
        wk = sb("wk", [P, KT, HG * P])
        wv = sb("wv", [P, KT, DIM])
        wo = sb("wo", [P, KT, DIM])
        bq_bk = sb("bq_bk", [P, 2, HG])
        bv_all = sb("bv_all", [P, DIM])
        bo_gated = sb("bo_gated", [P, DIM])
        gate = sb("gate", [P, 2])
        c_in = [sb(f"c_in{u}", [P, KT, KVP]) for u in range(2)]
        xn = sb("xn", [S, DIM])
        xnT = sb("xnT", [P, KT, S])
        qT = sb("qT", [P, HG, S])
        qaT = sb("qaT", [P, HG, S])
        kT = [sb(f"kT{u}", [P, HG, KVP]) for u in range(2)]
        v = sb("v", [KC, 3, HEADS, 32])
        zero_rows = sb("zero_rows", [P, max(words for _, words in to_clear)])
        neg_max = sb("neg_max", [S, HG, 4, 32])
        probs = [sb(f"probs{u}", [KC, 4, 3 * S]) for u in range(2)]
        att = sb("att", [P, HG, S])
        inverse = sb("inverse", [S, HEADS])
        attn = sb("attn", [S, HEADS, HD])
        attnT = sb("attnT", [P, KT, S])

        proj = ps("proj")
        misc = ps("misc")
        keys = ps("keys")
        outs = ps("outs")
        score = [ctx.enter_context(nc.psum_tensor(f"score{u}", [P, 2, 512], F32)) for u in range(2)]

        weights_in = sem("weights_in")
        ctx_arrived = [sem(f"ctx_arrived{u}") for u in range(2)]
        stored = sem("x1_stored")
        gate_ready, cleared, bias_ready = sem("gate_ready"), sem("cleared"), sem("bias_ready")
        xn_ready, bias_added = sem("xn_ready"), sem("bias_added")
        xnT_psum, xnT_ready = sem("xnT_psum"), sem("xnT_ready")
        q_psum, q_ready = sem("q_psum"), sem("q_ready")
        k_psum, k_ready = sem("k_psum"), sem("k_ready")
        v_psum, v_ready = sem("v_psum"), sem("v_ready")
        s_psum, max_ready = sem("s_psum"), sem("max_ready")
        nm_psum, qa_ready = sem("nm_psum"), sem("qa_ready")
        t_psum, p_ready = sem("t_psum"), sem("p_ready")
        o_psum, att_ready = sem("o_psum"), sem("att_ready")
        back_psum, inverse_ready, attn_ready = sem("back_psum"), sem("inverse_ready"), sem("attn_ready")
        attnT_psum, attnT_ready = sem("attnT_psum"), sem("attnT_ready")
        y_psum, x1_ready = sem("y_psum"), sem("x1_ready")
        block = ctx.enter_context(nc.Block())

        def rows_of(b):
            return rows[:, bass.ds(b, 1), :].rearrange("p a n -> p (a n)")

        @block.sync
        def _(sp):
            for dst, src in ((wq[:], wqT), (wk[:], wkT), (wv[:], wvT), (wo[:], woT), (bq_bk[:], bqk),
                             (bv_all[:], bv.partition_broadcast(P)), (bo_gated[:], bo.partition_broadcast(P)),
                             (gate[:, 0:2], g_xattn.partition_broadcast(P))):
                sp.dma_start(dst, src).then_inc(weights_in, 16)

            def turn_of(i):
                for u in range(2):
                    b = 2 * i + u
                    if not isinstance(i, int):
                        sp.wait_ge(v_ready, 3 * b - 3)
                    sp.dma_start(c_in[u][:], ctxT[bass.ds(b, 1)].rearrange("a p k n -> (a p) k n")).then_inc(ctx_arrived[u], 16)

            repeat(sp, B // 2, turn_of)

        @block.gpsimd
        def _(pool):
            nc.gpsimd.memset(v[:], 0.0).then_inc(cleared, 1)
            nc.gpsimd.memset(neg_max[:], 0.0).then_inc(cleared, 1)
            nc.gpsimd.memset(zero_rows[:], 0.0).then_inc(cleared, 1)
            pool.wait_ge(cleared, 3)
            nc.gpsimd.memset(v[:, :, :, HD:HD + 1], 1.0).then_inc(cleared, 1)
            pool.wait_ge(weights_in, 8 * 16)
            for k in range(whh.shape[1]):
                pool.dma_start(whh[:, k, :], whhT[:, k, :]).then_inc(whh_in, 16)
            for dram, words in to_clear:
                pool.dma_start(dram, zero_rows[:, 0:words]).then_inc(cleared_rows, 16)
            pool.wait_ge(bias_ready, 1)

            def store(b):
                pool.wait_ge(x1_ready, b + 1)
                pool.dma_start(x1[bass.ds(b, 1)].rearrange("a s d -> (a s) d"), rows_of(b)).then_inc(stored, 16)

            def turn_of(b, u, first, last):
                pool.wait_ge(xn_ready, b + 1)
                nc.gpsimd.tensor_tensor(rows_of(b), rows_of(b), bo_gated[0:S, :], ALU.add).then_inc(bias_added, 1)
                if not first:
                    store(b - 1)

            pipelined(pool, B, turn_of)
            store(B - 1)
            pool.wait_ge(stored, 16 * B)
            pool.wait_ge(cleared_rows, 16 * len(to_clear))

        @block.scalar
        def _(act):
            def keys_out(b, u, c):
                act.wait_ge(k_psum, HG * b + c + 1)
                nc.scalar.activation(kT[u][:, c, :], keys[:, 0:KVP], ACT.Identity,
                                     bias=bq_bk[:, 1, c:c + 1]).then_inc(k_ready, 1)

            def xnT_out(b):
                act.wait_ge(xnT_psum, b + 1)
                nc.scalar.copy(xnT[:].rearrange("p k s -> p (k s)"), misc[:, 0:KT * S]).then_inc(xnT_ready, 1)

            def finish_before(b):
                act.wait_ge(o_psum, b + 1)
                nc.scalar.copy(att[:].rearrange("p c s -> p (c s)"), outs[:, 0:HG * S]).then_inc(att_ready, 1)
                act.wait_ge(attnT_psum, b + 1)
                nc.scalar.copy(attnT[:].rearrange("p k s -> p (k s)"), misc[:, 0:KT * S]).then_inc(attnT_ready, 1)

            act.wait_ge(weights_in, 8 * 16)
            nc.scalar.activation(gate[:, 0:1], gate[:, 0:1], ACT.Tanh).then_inc(gate_ready, 1)
            xnT_out(0)
            for c in range(HG):
                keys_out(0, 0, c)

            def turn_of(b, u, first, last):
                if not first:
                    finish_before(b - 1)
                if not last:
                    xnT_out(b + 1)
                    keys_out(b + 1, 1 - u, 0)
                for c in range(HG):
                    for pair in range(2):
                        act.wait_ge(t_psum, PAIRS * b + 2 * c + pair + 1)
                        nc.scalar.activation(probs[c % 2][:, 2 * pair:2 * pair + 2, :], score[pair][0:KC, :, 0:3 * S],
                                             ACT.Exp, scale=HD ** -0.5).then_inc(p_ready, 1)
                    if c + 1 < HG and not last:
                        keys_out(b + 1, 1 - u, c + 1)

            pipelined(act, B, turn_of)
            finish_before(B - 1)

        @block.vector
        def _(dve):
            def normalized(b):
                normalize(nc, xn[:], rows_of(b), mean, rstd, b).then_inc(xn_ready, 1)

            def queries_out(b):
                dve.wait_ge(q_psum, b + 1)
                nc.vector.tensor_tensor(qT[:], proj[:, 0:HG * S].rearrange("p (c s) -> p c s", c=HG),
                                        bq_bk[:, 0, :].unsqueeze(2).to_broadcast([P, HG, S]), ALU.add).then_inc(q_ready, 1)

            def divide(b):
                dve.wait_ge(back_psum, b + 1)
                heads = misc[0:S, :].rearrange("p (h j) -> p h j", h=HEADS)
                nc.vector.reciprocal(inverse[:], heads[:, :, HD]).then_inc(inverse_ready, 1)
                dve.wait_ge(inverse_ready, b + 1)
                nc.vector.tensor_tensor(attn[:], heads[:, :, 0:HD], inverse[:].unsqueeze(2).to_broadcast([S, HEADS, HD]),
                                        ALU.mult).then_inc(attn_ready, 1)

            def add_output(b):
                dve.wait_ge(bias_added, b + 1)
                dve.wait_ge(y_psum, b + 1)
                nc.vector.scalar_tensor_tensor(rows_of(b), proj[0:S, 0:DIM], gate[0:S, 0:1], rows_of(b),
                                               ALU.mult, ALU.add).then_inc(x1_ready, 1)

            normalized(0)
            dve.wait_ge(gate_ready, 1)
            nc.vector.tensor_scalar(bo_gated[:], bo_gated[:], gate[:, 0:1], None, ALU.mult).then_inc(bias_ready, 1)
            dve.wait_ge(cleared, 4)
            queries_out(0)

            def turn_of(b, u, first, last):
                for c in range(HG):
                    for pair in range(2):
                        dve.wait_ge(s_psum, PAIRS * b + 2 * c + pair + 1)
                        nc.vector.tensor_reduce(neg_max[:, c, 2 * pair:2 * pair + 2, HD:HD + 1].rearrange("p i o -> p (i o)"),
                                                score[pair][0:S, :, 0:KV], AX.X, ALU.max).then_inc(max_ready, 1)
                    if c < 3:
                        dve.wait_ge(v_psum, 3 * b + c + 1)
                        nc.vector.tensor_tensor(v[:, c, :, 0:HD], proj[0:KC, 0:DIM].rearrange("p (h d) -> p h d", h=HEADS),
                                                bv_all[0:KC, :].rearrange("p (h d) -> p h d", h=HEADS), ALU.add).then_inc(v_ready, 1)
                    if c == 0 and not first:
                        divide(b - 1)
                    if c == 1 and not last:
                        dve.wait_ge(xnT_psum, b + 1)
                        normalized(b + 1)
                dve.wait_ge(nm_psum, b + 1)
                nc.vector.tensor_tensor(qaT[:].rearrange("p c s -> p (c s)"), qT[:].rearrange("p c s -> p (c s)"),
                                        outs[:, 0:HG * S], ALU.add).then_inc(qa_ready, 1)
                if not first:
                    add_output(b - 1)
                if not last:
                    queries_out(b + 1)

            pipelined(dve, B, turn_of)
            divide(B - 1)
            add_output(B - 1)
            dve.wait_ge(x1_ready, B)

        @block.tensor
        def _(pe):
            def turn_x(b):
                pe.wait_ge(xn_ready, b + 1)
                for k in range(KT):
                    done = nc.tensor.transpose(misc[:, k * S:(k + 1) * S], xn[:, k * P:(k + 1) * P], ident[0:S, 0:S])
                done.then_inc(xnT_psum, 1)

            def project_keys(b, u, c, free):
                if free:
                    pe.wait_ge(k_ready, HG * b + c)
                for k in range(KT):
                    done = nc.tensor.matmul(keys[:, 0:KVP], wk[:, k, c * P:(c + 1) * P], c_in[u][:, k, :],
                                            start=(k == 0), stop=(k == KT - 1))
                done.then_inc(k_psum, 1)

            def project_queries(b, free):
                pe.wait_ge(xnT_ready, b + 1)
                if free:
                    pe.wait_ge(x1_ready, b - 1)
                for c in range(HG):
                    for k in range(KT):
                        done = nc.tensor.matmul(proj[:, c * S:(c + 1) * S], wq[:, k, c * P:(c + 1) * P], xnT[:, k, :],
                                                start=(k == 0), stop=(k == KT - 1))
                done.then_inc(q_psum, 1)

            def project_values(b, u, c):
                if c:
                    pe.wait_ge(v_ready, 3 * b + c)
                for k in range(KT):
                    done = nc.tensor.matmul(proj[0:KC, 0:DIM], c_in[u][:, k, c * KC:(c + 1) * KC], wv[:, k, :],
                                            start=(k == 0), stop=(k == KT - 1))
                done.then_inc(v_psum, 1)

            def scores(b, u, h):
                c, pair = divmod(h, 2)
                if h >= 2:
                    pe.wait_ge(max_ready, PAIRS * b + h - 1)
                for r in range(2):
                    at = slice(64 * pair + 32 * r, 64 * pair + 32 * r + 32)
                    done = nc.tensor.matmul(score[pair][0:S, r, 0:KV], qT[at, c, :], kT[u][at, c, 0:KV], start=True, stop=True)
                done.then_inc(s_psum, 1)

            def shifted_scores(b, u, h):
                c, pair = divmod(h, 2)
                if h >= 2:
                    pe.wait_ge(p_ready, PAIRS * b + h - 1)
                for m in range(3):
                    for r in range(2):
                        at = slice(64 * pair + 32 * r, 64 * pair + 32 * r + 32)
                        done = nc.tensor.matmul(score[pair][0:KC, r, m * S:(m + 1) * S], kT[u][at, c, m * KC:(m + 1) * KC],
                                                qaT[at, c, :], start=True, stop=True)
                done.then_inc(t_psum, 1)

            def outputs(b, c):
                pe.wait_ge(p_ready, PAIRS * b + 2 * c + 2)
                for m in range(3):
                    n = KC if m < 2 else KLAST
                    for r in range(4):
                        done = nc.tensor.matmul(outs[32 * r:32 * r + 32, c * S:(c + 1) * S], v[0:n, m, 4 * c + r, :],
                                                probs[c % 2][0:n, r, m * S:(m + 1) * S], start=(m == 0), stop=(m == 2))
                return done

            def turn_back(b):
                pe.wait_ge(att_ready, b + 1)
                for c in range(HG):
                    done = nc.tensor.transpose(misc[0:S, c * P:(c + 1) * P], att[:, c, :], ident[:, :])
                done.then_inc(back_psum, 1)

            def turn_attn(b):
                pe.wait_ge(attn_ready, b + 1)
                for k in range(KT):
                    done = nc.tensor.transpose(misc[:, k * S:(k + 1) * S],
                                               attn[:].rearrange("p h d -> p (h d)")[:, k * P:(k + 1) * P], ident[0:S, 0:S])
                done.then_inc(attnT_psum, 1)

            def project_output(b):
                pe.wait_ge(attnT_ready, b + 1)
                for k in range(KT):
                    done = nc.tensor.matmul(proj[0:S, 0:DIM], attnT[:, k, :], wo[:, k, :], start=(k == 0), stop=(k == KT - 1))
                done.then_inc(y_psum, 1)

            pe.wait_ge(weights_in, 8 * 16)
            turn_x(0)
            pe.wait_ge(ctx_arrived[0], 16)
            for c in range(HG):
                project_keys(0, 0, c, c > 0)
            project_queries(0, False)

            def turn_of(b, u, first, last):
                pe.wait_ge(q_ready, b + 1)
                pe.wait_ge(k_ready, HG * b + HG)
                if not first:
                    pe.wait_ge(p_ready, PAIRS * b)
                scores(b, u, 0)
                scores(b, u, 1)
                project_values(b, u, 0)
                if not first:
                    turn_back(b - 1)
                scores(b, u, 2)
                scores(b, u, 3)
                project_values(b, u, 1)
                if not first:
                    turn_attn(b - 1)
                scores(b, u, 4)
                scores(b, u, 5)
                project_values(b, u, 2)
                scores(b, u, 6)
                scores(b, u, 7)
                pe.wait_ge(v_ready, 3 * b + 3)
                if not first:
                    project_output(b - 1)
                if not last:
                    turn_x(b + 1)
                pe.wait_ge(max_ready, PAIRS * b + PAIRS)
                for c in range(HG):
                    done = nc.tensor.matmul(outs[:, c * S:(c + 1) * S], neg_max[:, c, :, :].rearrange("p i j -> p (i j)"),
                                            neg_ident[0:S, 0:S], start=True, stop=True)
                done.then_inc(nm_psum, 1)
                if not last:
                    if u:
                        pe.wait_ge(ctx_arrived[0], 8 * b + 24)
                    elif first:
                        pe.wait_ge(ctx_arrived[1], 16)
                    else:
                        pe.wait_ge(ctx_arrived[1], 8 * b + 16)
                    project_keys(b + 1, 1 - u, 0, True)
                pe.wait_ge(qa_ready, b + 1)
                shifted_scores(b, u, 0)
                shifted_scores(b, u, 1)
                for c in range(HG):
                    if not last:
                        if c + 1 < HG:
                            project_keys(b + 1, 1 - u, c + 1, True)
                        else:
                            project_queries(b + 1, not first)
                    if c + 1 < HG:
                        shifted_scores(b, u, 2 * c + 2)
                        shifted_scores(b, u, 2 * c + 3)
                    done = outputs(b, c)
                done.then_inc(o_psum, 1)

            pipelined(pe, B, turn_of)
            turn_back(B - 1)
            turn_attn(B - 1)
            project_output(B - 1)
            pe.wait_ge(x1_ready, B)


GD = 1024
EXPERTS, RD = 8, 128
GQ = GD // 4
GC = GD // P
STEPS = 4
TILES = S // STEPS
SHIFTS = ((0, 3), (1, 2), (4, 5, 6, 7))
ROWS = [sum(EXPERTS - s for s in g) for g in SHIFTS] + [2 * EXPERTS]
NSTAT = sum(ROWS)


def gru(nc, whh, whh_in, wihT, hT, wcT, ctx_b, weT, states, stat, ident):
    with ExitStack() as ctx:
        def sb(name, shape, dt=F32):
            return ctx.enter_context(nc.sbuf_tensor("gru_" + name, shape, dt))

        def ps(name):
            return ctx.enter_context(nc.psum_tensor("gru_" + name, [P, 512], F32))

        def sem(name):
            return ctx.enter_context(nc.semaphore("gru_" + name))

        wih = sb("wih", [P, KT, 3 * GD])
        we = sb("we", [P, KT, GD])
        xt = [sb(f"xt{u}", [P, KT, STEPS, B]) for u in range(2)]
        h = [sb(f"state{u}", [P, GQ]) for u in range(2)]
        stateT = [sb(f"stateT{t}", [P, P]) for t in range(2)]
        rz = sb("rz", [P, 2, GQ])
        one_z = sb("one_z", [P, GQ])
        zh = sb("zh", [P, GQ])
        cand = sb("cand", [P, GQ])
        cand_n = sb("cand_n", [P, GQ])
        routed = sb("routed", [P, EXPERTS, RD])
        expr = sb("expr", [P, EXPERTS, RD])
        prod = sb("prod", [P, max(ROWS), RD])
        x_mean = sb("x_mean", [P, KT, B])

        ps_rz, ps_n, ps_x = ps("ps_rz"), ps("ps_n"), ps("ps_x")
        ps_t = [ps("ps_t0"), ps("ps_t1")]
        ps_e = [ps("ps_e0"), ps("ps_e1")]

        small_in, inputs_in = sem("small_in"), sem("inputs_in")
        mean_ready, h0_psum = sem("mean_ready"), sem("h0_psum")
        xt_ready, gates_ready, rz_done, n_done = sem("xt_ready"), sem("gates_ready"), sem("rz_done"), sem("n_done")
        cand_ready, tanh_ready, h_ready = sem("cand_ready"), sem("tanh_ready"), sem("state_ready")
        turned, stateT_ready = sem("state_turned"), [sem("stateT0_ready"), sem("stateT1_ready")]
        stored = [sem("state_stored0"), sem("state_stored1")]
        e_done, e_copied = sem("e_done"), sem("e_copied")
        routed_in, prod_ready, prod_used = sem("routed_in"), sem("prod_ready"), sem("prod_used")
        dve_own = sem("gru_dve_own")

        with ExitStack() as first:
            wc = first.enter_context(nc.sbuf_tensor("wc", [P, KT, GD], F32))
            cb = first.enter_context(nc.sbuf_tensor("cb", [P, GQ], F32))
            block = first.enter_context(nc.Block())

            @block.sync
            def _(sp):
                sp.dma_start(wc[:], wcT).then_inc(small_in, 16)
                for q in range(4):
                    sp.dma_start(cb[32 * q:32 * q + 32, :], ctx_b[q * GQ:(q + 1) * GQ].partition_broadcast(32)).then_inc(small_in, 16)
                sp.dma_start(wih[:], wihT).then_inc(inputs_in, 16)
                sp.dma_start(we[:], weT).then_inc(inputs_in, 16)
                sp.wait_ge(small_in, 5 * 16)
                sp.wait_ge(inputs_in, 2 * 16)

            @block.vector
            def _(dve):
                nc.vector.tensor_reduce(x_mean[:], hT[:], AX.X, ALU.add).then_inc(dve_own, 1)
                dve.wait_ge(dve_own, 1)
                nc.vector.tensor_scalar(x_mean[:], x_mean[:], 1.0 / S, None, ALU.mult).then_inc(mean_ready, 1)
                dve.wait_ge(small_in, 5 * 16)
                dve.wait_ge(h0_psum, 1)
                nc.vector.tensor_tensor(h[0][:], ps_n[:, 0:GQ], cb[:], ALU.add).then_inc(h_ready, 1)
                dve.wait_ge(h_ready, 1)

            @block.tensor
            def _(pe):
                pe.wait_ge(small_in, 5 * 16)
                pe.wait_ge(mean_ready, 1)
                for q in range(4):
                    for k in range(KT):
                        last = nc.tensor.matmul(ps_n[32 * q:32 * q + 32, 0:GQ], x_mean[:, k, :], wc[:, k, q * GQ:(q + 1) * GQ],
                                                start=(k == 0), stop=(k == KT - 1))
                last.then_inc(h0_psum, 1)

        block = ctx.enter_context(nc.Block())

        def quarter(q):
            return slice(32 * q, 32 * q + 32)

        def rz_columns(w, k, q):
            return w[:, k, 0:2 * GD].rearrange("p (g n) -> p g n", g=2)[:, :, q * GQ:(q + 1) * GQ]

        def n_columns(w, k, q):
            return w[:, k, 2 * GD + q * GQ:2 * GD + (q + 1) * GQ]

        @block.sync
        def _(sp):
            def turn_of(it):
                for j in range(STEPS):
                    u = (j + 1) % 2
                    sp.wait_ge(h_ready, STEPS * it + j + 2)
                    sp.dma_start(states[bass.ds(it, 1), j].rearrange("a b (q n) -> (a q) b n", q=4), h[u][:]).then_inc(stored[u], 16)
                for u in range(2):
                    sp.wait_ge(stored[u], 16 * 2 * it + 32)
                sp.wait_ge(prod_ready, 4 * it)
                sp.dma_start(routed[:].rearrange("p e d -> p (e d)"),
                             states[bass.ds(it, 1)].rearrange("a j b n -> (a j b) n")).then_inc(routed_in, 16)

            repeat(sp, TILES, turn_of)

        @block.gpsimd
        def _(pool):
            def take_inputs(it, u):
                nc.gpsimd.tensor_copy(xt[u][:], hT[:, :, :, bass.ds(STEPS * it, STEPS)].rearrange("p k b j -> p k j b")).then_inc(xt_ready, 1)

            def products(it):
                pool.wait_ge(routed_in, 16 * it + 16)
                pool.wait_ge(e_copied, 2 * it + 2)
                groups = [[(routed[:, 0:EXPERTS - s, :], routed[:, s:EXPERTS, :]) for s in g] for g in SHIFTS]
                groups.insert(0, [(expr[:], routed[:]), (expr[:], expr[:])])
                for n, group in enumerate(groups):
                    pool.wait_ge(prod_used, 4 * it + n)
                    row = 0
                    for a, b in group:
                        rows = a.shape[1]
                        last = nc.gpsimd.tensor_tensor(prod[:, row:row + rows, :], a, b, ALU.mult)
                        row += rows
                    last.then_inc(prod_ready, 1)

            take_inputs(0, 0)
            def turn_of(i):
                for u in range(2):
                    it = 2 * i + u
                    pool.wait_ge(gates_ready, 2 * STEPS * it)
                    pool.wait_ge(e_done, STEPS * it)
                    take_inputs(it + 1, 1 - u)
                    products(it)

            repeat(pool, TILES // 2, turn_of)
            products(TILES - 1)
            pool.wait_ge(prod_ready, 4 * TILES)

        def sum_group(dve, it, n):
            at = sum((ROWS[-1:] + ROWS[:-1])[:n])
            rows = (ROWS[-1:] + ROWS[:-1])[n]
            dve.wait_ge(prod_ready, 4 * it + n + 1)
            nc.vector.tensor_reduce(stat[:, bass.ds(it, 1), at:at + rows].rearrange("p a n -> p (a n)"),
                                    prod[:, 0:rows, :], AX.X, ALU.add).then_inc(prod_used, 1)

        @block.vector
        def _(dve):
            def steps(it, first):
                for j in range(STEPS):
                    t = STEPS * it + j
                    old, new = h[j % 2], h[(j + 1) % 2]
                    dve.wait_ge(turned, 2 * t + 1)
                    nc.vector.tensor_copy(stateT[0][:], ps_t[0][:, 0:P]).then_inc(stateT_ready[0], 1)
                    if not first:
                        sum_group(dve, it - 1, j)
                    dve.wait_ge(gates_ready, 2 * t + 1)
                    nc.vector.tensor_tensor(zh[:], rz[:, 1, :], old[:], ALU.mult).then_inc(dve_own, 1)
                    dve.wait_ge(n_done, t + 1)
                    nc.vector.tensor_tensor(cand[:], rz[:, 0, :], ps_n[:, 0:GQ], ALU.mult).then_inc(dve_own, 1)
                    dve.wait_ge(dve_own, 3 * t + 3)
                    nc.vector.tensor_tensor(cand[:], cand[:], ps_x[:, 0:GQ], ALU.add).then_inc(cand_ready, 1)
                    dve.wait_ge(gates_ready, 2 * t + 2)
                    dve.wait_ge(tanh_ready, t + 1)
                    nc.vector.tensor_tensor(cand_n[:], cand_n[:], one_z[:], ALU.mult).then_inc(dve_own, 1)
                    dve.wait_ge(dve_own, 3 * t + 4)
                    dve.wait_ge(stored[(j + 1) % 2], 16 * (2 * it + j // 2))
                    nc.vector.tensor_tensor(new[:], cand_n[:], zh[:], ALU.add).then_inc(h_ready, 1)

            steps(0, True)
            with dve.Fori(1, TILES) as it:
                steps(it, False)
            for n in range(4):
                sum_group(dve, TILES - 1, n)
            dve.wait_ge(prod_used, 4 * TILES)

        @block.scalar
        def _(act):
            def turn_of(it):
                for j in range(STEPS):
                    t = STEPS * it + j
                    act.wait_ge(turned, 2 * t + 2)
                    nc.scalar.copy(stateT[1][:], ps_t[1][:, 0:P]).then_inc(stateT_ready[1], 1)
                    if j >= 2:
                        act.wait_ge(e_done, STEPS * it + 2 * (j - 1))
                        act.wait_ge(prod_ready, 4 * it)
                        nc.scalar.copy(expr[:].rearrange("p e d -> p (e d)")[:, (j - 2) * 512:(j - 1) * 512], ps_e[j - 2][:, :]).then_inc(e_copied, 1)
                    act.wait_ge(rz_done, t + 1)
                    nc.scalar.activation(rz[:].rearrange("p g n -> p (g n)"), ps_rz[:, :], ACT.Sigmoid).then_inc(gates_ready, 1)
                    nc.scalar.activation(one_z[:], ps_rz[:, GQ:2 * GQ], ACT.Sigmoid, scale=-1.0).then_inc(gates_ready, 1)
                    act.wait_ge(cand_ready, t + 1)
                    nc.scalar.activation(cand_n[:], cand[:], ACT.Tanh).then_inc(tanh_ready, 1)

            repeat(act, TILES, turn_of)

        @block.tensor
        def _(pe):
            pe.wait_ge(whh_in, 16 * GC)

            def steps(it, u):
                pe.wait_ge(xt_ready, it + 1)
                for j in range(STEPS):
                    t = STEPS * it + j
                    pe.wait_ge(gates_ready, 2 * t)
                    for k in range(KT):
                        for q in range(4):
                            nc.tensor.matmul(ps_rz[quarter(q), :], xt[u][:, k, j, :], rz_columns(wih, k, q),
                                             start=(k == 0), stop=False)
                    pe.wait_ge(cand_ready, t)
                    for k in range(KT):
                        for q in range(4):
                            nc.tensor.matmul(ps_x[quarter(q), 0:GQ], xt[u][:, k, j, :], n_columns(wih, k, q),
                                             start=(k == 0), stop=(k == KT - 1))
                    pe.wait_ge(h_ready, t + 1)
                    for half in range(2):
                        nc.tensor.transpose(ps_t[half][:, 0:P], h[j % 2][:, half * P:(half + 1) * P], ident[:, :]).then_inc(turned, 1)
                    if j % 2 == 0:
                        pe.wait_ge(e_copied, 2 * it)
                    for k in range(KT):
                        last = nc.tensor.matmul(ps_e[j // 2][:, (j % 2) * GQ:(j % 2 + 1) * GQ], xt[u][:, k, :, :].rearrange("p j b -> p (j b)"),
                                                we[:, k, j * GQ:(j + 1) * GQ], start=(k == 0), stop=(k == KT - 1))
                    last.then_inc(e_done, 1)
                    for half in range(2):
                        pe.wait_ge(stateT_ready[half], t + 1)
                    for c in range(GC):
                        for q in range(4):
                            last = nc.tensor.matmul(ps_rz[quarter(q), :], stateT[c % 2][:, quarter(c // 2)], rz_columns(whh, c, q),
                                                    start=False, stop=(c == GC - 1))
                    last.then_inc(rz_done, 1)
                    for c in range(GC):
                        for q in range(4):
                            last = nc.tensor.matmul(ps_n[quarter(q), 0:GQ], stateT[c % 2][:, quarter(c // 2)], n_columns(whh, c, q),
                                                    start=(c == 0), stop=(c == GC - 1))
                    last.then_inc(n_done, 1)

            def turn_of(i):
                for u in range(2):
                    steps(2 * i + u, u)

            repeat(pe, TILES // 2, turn_of)
            steps(TILES - 1, 0)


FF = 512
TOKENS = B * S
TT = TOKENS // P
SLOT_TILES = (2 * TOKENS + EXPERTS * (P - 1)) // P
MOE_TILES = TT + SLOT_TILES
FC = FF // P
TINY_NORM, TINY_COS = 1e-12, 1e-8
HUGE = 3.0e38


def routing(nc, stat, weight, slot, tile_expert, iota_e, below, ones, g_ffn, gate, gu, guT, dn, dnT, shared_in,
            h_rows, h_all, h_in):
    with ExitStack() as ctx:
        def sb(name, shape, dt=F32):
            return ctx.enter_context(nc.sbuf_tensor("route_" + name, shape, dt))

        def sem(name):
            return ctx.enter_context(nc.semaphore("route_" + name))

        inv = sb("inv", [P, TILES, EXPERTS])
        pair = sb("pair", [P, EXPERTS, TILES, EXPERTS])
        row2_too = sb("row2_too", [P, TILES, EXPERTS])
        row2 = sb("row2", [P, TILES, EXPERTS])
        root = sb("root", [P, TILES, EXPERTS])
        en = sb("en", [P, TILES, EXPERTS])
        score = sb("score", [P, TILES, EXPERTS])
        work = sb("work", [P, TILES, EXPERTS])
        hot = [sb(f"hot{k}", [P, TILES, EXPERTS]) for k in range(2)]
        chosen = sb("chosen", [P, TILES, EXPERTS])
        best = [sb(f"best{k}", [P, TILES]) for k in range(2)]
        index = sb("index", [P, TILES])
        ratio = sb("ratio", [P, TILES])
        share = sb("share", [P, TILES])
        pen = sb("pen", [P, 1])
        total = sb("total", [P, EXPERTS, TILES])
        upto = sb("upto", [P, EXPERTS, TILES])
        zeros = sb("zeros_r", [P, TILES])
        row_of = sb("row_of", [P, TILES, EXPERTS])
        steps_i = sb("steps_i", [P, EXPERTS, TILES], I32)
        steps_f = sb("steps_f", [P, EXPERTS, TILES])
        need = sb("need", [P, EXPERTS])
        end = sb("end", [P, EXPERTS])
        base = sb("base", [P, EXPERTS])
        slot_f = sb("slot_f", [P, TILES])
        tile_i = sb("tile_i", [1, MOE_TILES, EXPERTS], I32)
        tile_f = sb("tile_f", [1, MOE_TILES, EXPERTS])
        tile_e = sb("tile_e", [1, MOE_TILES])
        ps_pen = ctx.enter_context(nc.psum_tensor("ps_pen", [P, 512], F32))
        ps_rank = ctx.enter_context(nc.psum_tensor("ps_rank", [P, 512], F32))
        ps_total = ctx.enter_context(nc.psum_tensor("ps_total", [P, 512], F32))

        own, filled = sem("route_own"), sem("route_filled")
        root_in, root_out, exp_in, exp_out = sem("root_in"), sem("root_out"), sem("exp_in"), sem("exp_out")
        pen_in, pen_out, chosen_ready, ranked = sem("pen_in"), sem("pen_out"), sem("chosen_ready"), sem("ranked")
        gate_in, gate_ready = sem("ffn_gate_in"), sem("ffn_gate_ready")
        block = ctx.enter_context(nc.Block())

        @block.sync
        def _(sp):
            sp.dma_start(gate[:, :], g_ffn.partition_broadcast(P)).then_inc(gate_in, 16)
            sp.dma_start(gu[:, EXPERTS], guT[:, EXPERTS]).then_inc(shared_in, 16)
            sp.dma_start(dn[:, EXPERTS], dnT[:, EXPERTS]).then_inc(shared_in, 16)
            h_view = h_rows.rearrange("b (t j) d -> j b t d", j=STEPS)
            for j in range(STEPS):
                sp.dma_start(h_all[32 * j:32 * j + 32, :, :], h_view[j]).then_inc(h_in, 16)
            sp.wait_ge(gate_in, 16)

        @block.gpsimd
        def _(pool):
            nc.gpsimd.iota(steps_i[:], pattern=[[0, EXPERTS], [P, TILES]], base=0, channel_multiplier=0).then_inc(filled, 1)
            nc.gpsimd.iota(tile_i[:], pattern=[[1, MOE_TILES], [0, EXPERTS]], base=-TT, channel_multiplier=0).then_inc(filled, 1)
            nc.gpsimd.memset(zeros[:], 0.0).then_inc(filled, 1)
            pool.wait_ge(filled, 3)
            nc.gpsimd.tensor_copy(steps_f[:], steps_i[:]).then_inc(filled, 1)
            nc.gpsimd.tensor_copy(tile_f[:], tile_i[:]).then_inc(filled, 1)

        @block.scalar
        def _(act):
            act.wait_ge(gate_in, 16)
            nc.scalar.activation(gate[:, :], gate[:, :], ACT.Tanh).then_inc(gate_ready, 1)
            act.wait_ge(gate_ready, 1)
            for n, (a, b) in enumerate(((inv, stat[:, :, 16:24]), (en, stat[:, :, 8:16]), (root, root), (work, row2))):
                act.wait_ge(root_in, n + 1)
                nc.scalar.activation(a[:], b if n < 2 else b[:], ACT.Sqrt).then_inc(root_out, 1)
            act.wait_ge(exp_in, 1)
            nc.scalar.activation(ratio[:], ratio[:], ACT.Exp).then_inc(exp_out, 1)

        @block.tensor
        def _(pe):
            pe.wait_ge(pen_in, 1)
            nc.tensor.matmul(ps_pen[:, 0:1], ones[:, :], pen[:, :], start=True, stop=True).then_inc(pen_out, 1)
            pe.wait_ge(chosen_ready, 1)
            flat = chosen[:].rearrange("p t e -> p (t e)")
            nc.tensor.matmul(ps_rank[:, 0:TILES * EXPERTS], below[:, :], flat, start=True, stop=True).then_inc(ranked, 1)
            nc.tensor.matmul(ps_total[:, 0:TILES * EXPERTS], ones[:, :], flat, start=True, stop=True).then_inc(ranked, 1)

        @block.vector
        def _(dve):
            v = nc.vector
            chain = Chain(dve, own)

            def every(a):
                return a[:].unsqueeze(2).to_broadcast([P, TILES, EXPERTS])

            v.tensor_copy(pen[:], stat[:, 0, 0:1]).then_inc(root_in, 2)
            dve.wait_ge(root_out, 2)
            chain.step(v.tensor_scalar(inv[:], inv[:], TINY_NORM, None, ALU.max))
            chain.step(v.reciprocal(inv[:], inv[:]))
            chain.step(v.tensor_tensor(root[:], stat[:, :, 16:24], inv[:], ALU.mult))
            chain.step(v.tensor_tensor(root[:], root[:], inv[:], ALU.mult))
            chain.step(v.tensor_scalar(row2[:], root[:], -1.0, None, ALU.add))
            v.tensor_tensor(row2[:], row2[:], row2[:], ALU.mult).then_inc(root_in, 1)
            dve.wait_ge(root_in, 3)
            at, pairs = 2 * EXPERTS, []
            for s in (s for group in SHIFTS for s in group):
                n = EXPERTS - s
                if s:
                    pairs.append((s, n, pair[:, s, :, 0:n], stat[:, :, at:at + n]))
                at += n
            chain.together(*[v.tensor_tensor(p, raw, inv[:, :, 0:n], ALU.mult) for s, n, p, raw in pairs],
                           v.memset(row2_too[:], 0.0))
            chain.together(*[v.tensor_tensor(p, p, inv[:, :, s:EXPERTS], ALU.mult) for s, n, p, raw in pairs])
            chain.together(*[v.tensor_tensor(p, p, p, ALU.mult) for s, n, p, raw in pairs])
            for s, n, p, raw in pairs:
                chain.together(v.tensor_tensor(row2[:, :, 0:n], row2[:, :, 0:n], p, ALU.add),
                               v.tensor_tensor(row2_too[:, :, s:EXPERTS], row2_too[:, :, s:EXPERTS], p, ALU.add))
            chain.step(v.tensor_tensor(row2[:], row2[:], row2_too[:], ALU.add))
            v.tensor_scalar(pen[:], pen[:], 0.0, None, ALU.mult).then_inc(root_in, 1)
            dve.wait_ge(root_out, 3)
            chain.together(v.tensor_scalar(root[:], root[:], TINY_COS, None, ALU.max),
                           v.tensor_scalar(en[:], en[:], TINY_COS, None, ALU.max),
                           v.tensor_tensor(score[:], stat[:, :, 0:EXPERTS], inv[:], ALU.mult))
            chain.step(v.tensor_tensor(en[:], en[:], root[:], ALU.mult))
            chain.step(v.reciprocal(en[:], en[:]))
            chain.step(v.tensor_tensor(score[:], score[:], en[:], ALU.mult))
            chain.step(v.tensor_scalar(score[:], score[:], -1.0, 1.0, ALU.mult, ALU.add))
            dve.wait_ge(root_out, 4)
            chain.step(v.tensor_scalar(work[:], work[:], TINY_NORM, None, ALU.max))
            chain.step(v.reciprocal(work[:], work[:]))
            chain.step(v.tensor_tensor(row2[:], row2[:], work[:], ALU.mult))
            chain.step(v.tensor_tensor(row2[:], row2[:], work[:], ALU.mult))
            v.tensor_reduce(pen[:], row2[:], AX.XY, ALU.add).then_inc(pen_in, 1)
            dve.wait_ge(pen_out, 1)
            chain.step(v.tensor_scalar(pen[:], ps_pen[:, 0:1], 1.0 / TOKENS, 1.0, ALU.mult, ALU.add))
            chain.step(v.tensor_scalar(score[:], score[:], pen[:, 0:1], None, ALU.mult))
            for k in range(2):
                chain.step(v.tensor_reduce(best[k][:], score[:], AX.X, ALU.max))
                chain.step(v.tensor_tensor(work[:], score[:], every(best[k]), ALU.is_lt))
                chain.step(v.scalar_tensor_tensor(work[:], work[:], 2.0 * EXPERTS, iota_e[:], ALU.mult, ALU.add))
                chain.step(v.tensor_reduce(index[:], work[:], AX.X, ALU.min))
                chain.step(v.tensor_tensor(hot[k][:], iota_e[:], every(index), ALU.is_equal))
                if k == 0:
                    chain.step(v.scalar_tensor_tensor(score[:], hot[0][:], -HUGE, score[:], ALU.mult, ALU.add))
            v.tensor_tensor(chosen[:], hot[0][:], hot[1][:], ALU.add).then_inc(chosen_ready, 1)
            v.tensor_tensor(ratio[:], best[1][:], best[0][:], ALU.subtract).then_inc(exp_in, 1)
            dve.wait_ge(exp_out, 1)
            chain.step(v.tensor_scalar(share[:], ratio[:], 1.0, None, ALU.add))
            chain.step(v.reciprocal(weight[:, :, 0], share[:]))
            chain.step(v.tensor_tensor(weight[:, :, 1], weight[:, :, 0], ratio[:], ALU.mult))
            dve.wait_ge(ranked, 2)
            dve.wait_ge(filled, 5)
            chain.step(v.tensor_copy(total[:], ps_total[:, 0:TILES * EXPERTS].rearrange("p (t e) -> p e t", e=EXPERTS)))
            chain.together(*[v.tensor_tensor_scan(upto[:, e, :], zeros[:], total[:, e, :], 0.0, ALU.add, ALU.add)
                             for e in range(EXPERTS)])
            chain.step(v.tensor_tensor(steps_f[:], steps_f[:], upto[:, :, TILES - 1:TILES].to_broadcast([P, EXPERTS, TILES]), ALU.is_lt))
            chain.step(v.tensor_reduce(need[:], steps_f[:], AX.X, ALU.add))
            chain.step(v.tensor_tensor_scan(end[:], zeros[:, 0:EXPERTS], need[:], 0.0, ALU.add, ALU.add))
            chain.step(v.tensor_tensor(base[:], end[:], need[:], ALU.subtract))
            chain.step(v.tensor_scalar(base[:], base[:], float(P), float(TOKENS - 1), ALU.mult, ALU.add))
            chain.step(v.tensor_tensor(upto[:], upto[:], total[:], ALU.subtract))
            chain.step(v.tensor_tensor(upto[:], upto[:], base[:].unsqueeze(2).to_broadcast([P, EXPERTS, TILES]), ALU.add))
            chain.step(v.tensor_tensor(row_of[:], ps_rank[:, 0:TILES * EXPERTS].rearrange("p (t e) -> p t e", e=EXPERTS),
                                       upto[:].rearrange("p e t -> p t e"), ALU.add))
            for k in range(2):
                chain.step(v.tensor_tensor(work[:], hot[k][:], row_of[:], ALU.mult))
                chain.step(v.tensor_reduce(slot_f[:], work[:], AX.X, ALU.add))
                chain.step(v.tensor_copy(slot[:, :, k], slot_f[:]))
            chain.step(v.tensor_tensor(tile_f[:], tile_f[:], end[0:1, :].unsqueeze(1).to_broadcast([1, MOE_TILES, EXPERTS]), ALU.is_ge))
            chain.step(v.tensor_reduce(tile_e[:], tile_f[:], AX.X, ALU.add))
            chain.step(v.tensor_scalar(tile_e[:], tile_e[:], float(EXPERTS - 1), None, ALU.min))
            chain.step(v.memset(tile_e[:, 0:TT], float(EXPERTS)))
            chain.step(v.tensor_copy(tile_expert[:], tile_e[:]))


def expert_tiles(nc, moe_in, moe_out, gu, guT, dn, dnT, tile_expert, shared_in, ident, slot, h_all, h_in):
    with ExitStack() as ctx:
        def sb(name, shape, dt=F32):
            return ctx.enter_context(nc.sbuf_tensor("moe_" + name, shape, dt))

        def ps(name):
            return ctx.enter_context(nc.psum_tensor("moe_" + name, [P, 512], F32))

        def sem(name):
            return ctx.enter_context(nc.semaphore("moe_" + name))

        xs = [sb(f"xs{u}", [P, DIM]) for u in range(2)]
        xT = [sb(f"xT{u}", [P, KT, P]) for u in range(2)]
        act_g = [sb(f"act_g{u}", [P, FF]) for u in range(2)]
        mid = [sb(f"mid{u}", [P, FF]) for u in range(2)]
        midT = sb("midT", [P, FC, P])
        y = [sb(f"y{u}", [P, DIM]) for u in range(2)]
        ps_x, ps_m, ps_y = ps("ps_x"), ps("ps_m"), ps("ps_y")
        ps_g = [ps(f"ps_g{u}") for u in range(2)]
        ps_u = [ps(f"ps_u{u}") for u in range(2)]
        scattered, experts_in = sem("scattered"), sem("experts_in")
        xs_in, x_turned, xT_ready = [sem("xs_in0"), sem("xs_in1")], sem("x_turned"), sem("xT_ready")
        g_done, u_done, act_ready, mid_ready = sem("g_done"), sem("u_done"), sem("act_ready"), sem("mid_ready")
        m_turned, midT_ready, y_done, y_ready = sem("m_turned"), sem("midT_ready"), sem("y_done"), sem("y_ready")
        y_stored = [sem("y_stored0"), sem("y_stored1")]
        block = ctx.enter_context(nc.Block())
        LAST = MOE_TILES - 1
        assert TT % 2 == 1 and MOE_TILES % 2 == 0

        def rows(dram, n):
            return dram.rearrange("(t p) d -> t p d", p=P)[bass.ds(n, 1)].rearrange("a p d -> (a p) d")

        @block.sync
        def _(sp):
            def load(n, u):
                sp.dma_start(xs[u][:], rows(moe_in, n)).then_inc(xs_in[u], 16)

            def store(n, u):
                sp.wait_ge(y_ready, n + 1)
                sp.dma_start(rows(moe_out, n), y[u][:]).then_inc(y_stored[u], 16)

            def turn_of(n, u):
                sp.wait_ge(x_turned, n + 1)
                load(n + 2, u)
                store(n - 1, 1 - u)

            load(0, 0)
            load(1, 1)
            sp.wait_ge(x_turned, 1)
            load(2, 0)
            with sp.Fori(1, EXPERTS + 1) as i:
                turn_of(2 * i - 1, 1)
                e = bass.ds(i - 1, 1)
                sp.dma_start(gu[:, e].rearrange("p a k n -> p (a k n)"), guT[:, e].rearrange("p a k n -> p (a k n)")).then_inc(experts_in, 16)
                sp.dma_start(dn[:, e].rearrange("p a k n -> p (a k n)"), dnT[:, e].rearrange("p a k n -> p (a k n)")).then_inc(experts_in, 16)
                turn_of(2 * i, 0)
            with sp.Fori(EXPERTS + 1, (TT - 1) // 2) as i:
                turn_of(2 * i - 1, 1)
                turn_of(2 * i, 0)
            sp.wait_ge(scattered, 16 * 2 * TILES)
            with sp.Fori((TT - 1) // 2, MOE_TILES // 2 - 1) as i:
                turn_of(2 * i - 1, 1)
                turn_of(2 * i, 0)
            turn_of(LAST - 2, 1)
            store(LAST - 2, 1)
            store(LAST - 1, 0)
            store(LAST, 1)
            for u in range(2):
                sp.wait_ge(y_stored[u], 16 * (MOE_TILES // 2))

        @block.gpsimd
        def _(pool):
            pool.wait_ge(h_in, 16 * STEPS)
            for it in range(TILES):
                for k in range(2):
                    nc.gpsimd.indirect_dma_start(moe_in, bass.IndirectOffsetOnAxis(ap=slot[:, it, k:k + 1], axis=0),
                                                 h_all[:, it, :], None).then_inc(scattered, 16)
            pool.wait_ge(scattered, 16 * 2 * TILES)

        @block.scalar
        def _(act):
            def take_x(n, u):
                act.wait_ge(x_turned, n + 1)
                nc.scalar.copy(xT[u][:].rearrange("p k n -> p (k n)"), ps_x[:, 0:KT * P]).then_inc(xT_ready, 1)

            def take_y(n, u, first):
                act.wait_ge(y_done, n + 1)
                if not first:
                    act.wait_ge(y_stored[u], 8 * (n - u))
                nc.scalar.copy(y[u][:], ps_y[:, 0:DIM]).then_inc(y_ready, 1)

            def gate_of(n, u):
                act.wait_ge(g_done, n + 1)
                nc.scalar.activation(act_g[u][:], ps_g[u][:, :], ACT.Silu).then_inc(act_ready, 1)

            take_x(0, 0)
            gate_of(0, 0)
            take_x(1, 1)
            gate_of(1, 1)
            take_x(2, 0)
            take_y(0, 0, True)
            gate_of(2, 0)
            take_x(3, 1)
            take_y(1, 1, True)

            def turn_of(n, u):
                act.wait_ge(mid_ready, n - 1)
                gate_of(n, u)
                take_x(n + 1, 1 - u)
                take_y(n - 1, 1 - u, False)

            with act.Fori(2, MOE_TILES // 2) as i:
                turn_of(2 * i - 1, 1)
                turn_of(2 * i, 0)
            act.wait_ge(mid_ready, LAST - 1)
            gate_of(LAST, 1)
            take_y(LAST - 1, 0, False)
            take_y(LAST, 1, False)

        @block.vector
        def _(dve):
            def take_mid(n):
                dve.wait_ge(m_turned, n + 1)
                nc.vector.tensor_copy(midT[:].rearrange("p k n -> p (k n)"), ps_m[:, :]).then_inc(midT_ready, 1)

            def product(n, u):
                dve.wait_ge(act_ready, n + 1)
                dve.wait_ge(u_done, n + 1)
                nc.vector.tensor_tensor(mid[u][:], act_g[u][:], ps_u[u][:, :], ALU.mult).then_inc(mid_ready, 1)

            def turn_of(n, u, first, last):
                if not first:
                    take_mid(n - 1)
                product(n, u)

            pipelined(dve, MOE_TILES, turn_of)
            take_mid(LAST)

        @block.tensor
        def _(pe):
            def expert_of(n):
                return nc.tensor.value_load(tile_expert[0:1, bass.ds(n, 1)], min_val=0, max_val=EXPERTS)

            def turn_x(n, u, count):
                pe.wait_ge(xs_in[u], count)
                pe.wait_ge(xT_ready, n)
                for k in range(KT):
                    done = nc.tensor.transpose(ps_x[:, k * P:(k + 1) * P], xs[u][:, k * P:(k + 1) * P], ident[:, :])
                done.then_inc(x_turned, 1)

            def up(psum, half, e, u):
                for k in range(KT):
                    done = nc.tensor.matmul(psum[:, :], xT[u][:, k, :],
                                            gu[:, bass.ds(e, 1), k, half * FF:(half + 1) * FF].rearrange("p a n -> p (a n)"),
                                            start=(k == 0), stop=(k == KT - 1))
                return done

            def turn_mid(n, u):
                pe.wait_ge(mid_ready, n + 1)
                for c in range(FC):
                    done = nc.tensor.transpose(ps_m[:, c * P:(c + 1) * P], mid[u][:, c * P:(c + 1) * P], ident[:, :])
                done.then_inc(m_turned, 1)

            def down(n, e):
                pe.wait_ge(midT_ready, n + 1)
                for c in range(FC):
                    done = nc.tensor.matmul(ps_y[:, 0:DIM], midT[:, c, :],
                                            dn[:, bass.ds(e, 1), c, :].rearrange("p a n -> p (a n)"),
                                            start=(c == 0), stop=(c == FC - 1))
                done.then_inc(y_done, 1)

            def turn_of(n, u, e_before, e, first=False, last=False):
                pe.wait_ge(xT_ready, n + 1)
                if not first:
                    pe.wait_ge(act_ready, n)
                up(ps_g[u], 0, e, u).then_inc(g_done, 1)
                if not first:
                    turn_mid(n - 1, 1 - u)
                up(ps_u[u], 1, e, u).then_inc(u_done, 1)
                if not last:
                    turn_x(n + 1, 1 - u, 8 * (n + 1 - (1 - u)) + 16)
                if not first:
                    if not isinstance(n, int) or n > 1:
                        pe.wait_ge(y_ready, n - 1)
                    down(n - 1, e_before)

            def two_tiles(i):
                before, here, after = expert_of(2 * i - 2), expert_of(2 * i - 1), expert_of(2 * i)
                turn_of(2 * i - 1, 1, before, here)
                turn_of(2 * i, 0, here, after)

            pe.wait_ge(shared_in, 2 * 16)
            turn_x(0, 0, 16)
            turn_of(0, 0, None, EXPERTS, first=True)
            two_tiles(1)
            with pe.Fori(2, (TT + 1) // 2) as i:
                two_tiles(i)
            pe.wait_ge(experts_in, 16 * 2 * EXPERTS)
            with pe.Fori((TT + 1) // 2, MOE_TILES // 2) as i:
                two_tiles(i)
            before, here = expert_of(LAST - 1), expert_of(LAST)
            turn_of(LAST, 1, before, here, last=True)
            turn_mid(LAST, 1)
            pe.wait_ge(y_ready, LAST)
            down(LAST, here)


def combine(nc, moe_out, x1, weight, slot, gate, x2):
    with ExitStack() as ctx:
        def sb(name, shape, dt=F32):
            return ctx.enter_context(nc.sbuf_tensor("mix_" + name, shape, dt))

        def sem(name):
            return ctx.enter_context(nc.semaphore("mix_" + name))

        N = 5
        GROUPS = TILES // N
        pair = [[sb(f"pair{k}_{u}", [P, N, DIM]) for k in range(2)] for u in range(2)]
        shared = [sb(f"shared{u}", [P, N, DIM]) for u in range(2)]
        x = [sb(f"x_c{u}", [P, N, DIM]) for u in range(2)]
        rows_in = [sem(f"rows_in{u}") for u in range(2)]
        pair_in = [sem(f"pair_in{t}") for t in range(2 * N)]
        own, x2_ready = sem("combine_own"), sem("x2_ready")
        x2_stored = [sem(f"x2_stored{u}") for u in range(2)]
        block = ctx.enter_context(nc.Block())

        def group_of(dram, g, j):
            return dram.rearrange("b (g t j) d -> g j b t d", g=GROUPS, j=STEPS)[g, j]

        shared_rows = moe_out[0:TOKENS].rearrange("(b s) d -> b s d", b=B)

        @block.sync
        def _(sp):
            for g in range(GROUPS):
                u = g % 2
                if g >= 2:
                    sp.wait_ge(x2_stored[u], 16 * STEPS * (g // 2))
                for j in range(STEPS):
                    sp.dma_start(x[u][32 * j:32 * j + 32], group_of(x1, g, j)).then_inc(rows_in[u], 16)
                    sp.dma_start(shared[u][32 * j:32 * j + 32], group_of(shared_rows, g, j)).then_inc(rows_in[u], 16)

        @block.gpsimd
        def _(pool):
            for it in range(TILES):
                g, t = divmod(it, N)
                if g >= 2:
                    pool.wait_ge(x2_ready, it - 2 * N + 1)
                for k in range(2):
                    nc.gpsimd.indirect_dma_start(pair[g % 2][k][:, t, :], None, moe_out,
                                                 bass.IndirectOffsetOnAxis(ap=slot[:, it, k:k + 1], axis=0)).then_inc(pair_in[it % (2 * N)], 16)

        @block.vector
        def _(dve):
            chain = Chain(dve, own)
            for it in range(TILES):
                g, t = divmod(it, N)
                u = g % 2
                if t == 0:
                    dve.wait_ge(rows_in[u], 16 * 2 * STEPS * (g // 2 + 1))
                dve.wait_ge(pair_in[it % (2 * N)], 32 * (it // (2 * N) + 1))
                for k in range(2):
                    chain.step(nc.vector.scalar_tensor_tensor(shared[u][:, t, :], pair[u][k][:, t, :], weight[:, it, k:k + 1],
                                                              shared[u][:, t, :], ALU.mult, ALU.add))
                nc.vector.scalar_tensor_tensor(x[u][:, t, :], shared[u][:, t, :], gate[:, 0:1], x[u][:, t, :],
                                               ALU.mult, ALU.add).then_inc(x2_ready, 1)

        @block.scalar
        def _(act):
            for g in range(GROUPS):
                u = g % 2
                act.wait_ge(x2_ready, N * g + N)
                for j in range(STEPS):
                    act.dma_start(group_of(x2, g, j), x[u][32 * j:32 * j + 32]).then_inc(x2_stored[u], 16)
            for u in range(2):
                act.wait_ge(x2_stored[u], 16 * STEPS * len(range(u, GROUPS, 2)))


BANDS = 4
BAND = -(-KV // BANDS)
LAST_BAND = KV - (BANDS - 1) * BAND
DSTEPS = S + BANDS - 1
FAR = 1.0e30


def band(r):
    return slice(B * r, B * r + B)


def distances(nc, rows, mean, rstd, ctxT, table, ones, ident):
    AT_ONCE = 4
    with ExitStack() as ctx:
        def sb(name, shape, dt=F32):
            return ctx.enter_context(nc.sbuf_tensor("dist_" + name, shape, dt))

        def sem(name):
            return ctx.enter_context(nc.semaphore("dist_" + name))

        c_in = [sb(f"d_ctx{u}", [P, KT, KVP]) for u in range(AT_ONCE)]
        square = [sb(f"d_square{u}", [P, KT, KV]) for u in range(AT_ONCE)]
        xn = [sb(f"d_xn{u}", [S, DIM]) for u in range(AT_ONCE)]
        xx = [sb(f"d_xx{u}", [S, DIM]) for u in range(AT_ONCE)]
        norm = [sb(f"d_norm{u}", [S, 1]) for u in range(AT_ONCE)]
        xT = [sb(f"d_xT{u}", [P, KT, S]) for u in range(AT_ONCE)]
        dist = [sb(f"d_dist{u}", [S, KV]) for u in range(AT_ONCE)]
        ps_x = [ctx.enter_context(nc.psum_tensor(f"d_ps_x{u}", [P, 512], F32)) for u in range(AT_ONCE)]
        ps_d = [ctx.enter_context(nc.psum_tensor(f"d_ps_d{u}", [P, 512], F32)) for u in range(AT_ONCE)]
        ctx_in = [sem(f"d_ctx_in{u}") for u in range(AT_ONCE)]
        squared, xn_ready, turned, xT_ready = sem("d_squared"), sem("d_xn_ready"), sem("d_turned"), sem("d_xT_ready")
        norm_ready, summed, square_ready, dist_ready = sem("d_norm_ready"), sem("d_summed"), sem("d_square_ready"), sem("d_dist_ready")
        placed = [sem(f"d_placed{u}") for u in range(AT_ONCE)]
        cleared = sem("d_cleared")
        block = ctx.enter_context(nc.Block())

        @block.sync
        def _(sp):
            for b in range(B + AT_ONCE):
                before = b - AT_ONCE
                u = b % AT_ONCE
                if b < B:
                    if before >= 0:
                        sp.wait_ge(summed, before + 1)
                        sp.wait_ge(squared, before + 1)
                    sp.dma_start(c_in[u][:], ctxT[b]).then_inc(ctx_in[u], 16)
                if before >= 0:
                    if before == 0:
                        sp.wait_ge(cleared, 3)
                    sp.wait_ge(dist_ready, before + 1)
                    for r in range(BANDS):
                        n = BAND if r < BANDS - 1 else LAST_BAND
                        sp.dma_start(table[B * r + before:B * r + before + 1, r:r + S, 0:n],
                                     dist[u][:, r * BAND:r * BAND + n]).then_inc(placed[u], 16)
            for u in range(AT_ONCE):
                sp.wait_ge(placed[u], 16 * BANDS * (B // AT_ONCE))

        @block.gpsimd
        def _(pool):
            def turn_of(i):
                for u in range(AT_ONCE):
                    pool.wait_ge(ctx_in[u], 16 * i + 16)
                    reused(pool, summed, i, u, AT_ONCE)
                    nc.gpsimd.tensor_tensor(square[u][:], c_in[u][:, :, 0:KV], c_in[u][:, :, 0:KV], ALU.mult).then_inc(squared, 1)

            turn_of(0)
            nc.gpsimd.memset(table[:, 0:BANDS - 1, :], FAR).then_inc(cleared, 1)
            nc.gpsimd.memset(table[:, S:DSTEPS, :], FAR).then_inc(cleared, 1)
            nc.gpsimd.memset(table[:, BANDS - 1:S, LAST_BAND:BAND], FAR).then_inc(cleared, 1)
            with pool.Fori(1, B // AT_ONCE) as i:
                turn_of(i)

        @block.vector
        def _(dve):
            def turn_of(i):
                for u in range(AT_ONCE):
                    b = AT_ONCE * i + u
                    reused(dve, turned, i, u, AT_ONCE)
                    reused(dve, norm_ready, i, u, AT_ONCE)
                    normalize(nc, xn[u][:], rows[:, bass.ds(b, 1), :].rearrange("p a n -> p (a n)"), mean, rstd, b).then_inc(xn_ready, 1)
                for u in range(AT_ONCE):
                    b = AT_ONCE * i + u
                    dve.wait_ge(turned, b + 1)
                    nc.vector.tensor_scalar(xT[u][:].rearrange("p k s -> p (k s)"), ps_x[u][:, 0:KT * S], -2.0, None, ALU.mult).then_inc(xT_ready, 1)
                for u in range(AT_ONCE):
                    b = AT_ONCE * i + u
                    dve.wait_ge(summed, b + 1)
                    dve.wait_ge(norm_ready, b + 1)
                    dve.wait_ge(placed[u], 16 * BANDS * i)
                    nc.vector.tensor_scalar(dist[u][:], ps_d[u][0:S, 0:KV], norm[u][:, 0:1], 0.0, ALU.add, ALU.max).then_inc(square_ready, 1)

            repeat(dve, B // AT_ONCE, turn_of)

        @block.scalar
        def _(act):
            def turn_of(i):
                for u in range(AT_ONCE):
                    b = AT_ONCE * i + u
                    act.wait_ge(xn_ready, b + 1)
                    reused(act, square_ready, i, u, AT_ONCE)
                    nc.scalar.activation(xx[u][:], xn[u][:], ACT.Square, accum_out=norm[u][:, 0:1]).then_inc(norm_ready, 1)
                for u in range(AT_ONCE):
                    b = AT_ONCE * i + u
                    act.wait_ge(square_ready, b + 1)
                    nc.scalar.activation(dist[u][:], dist[u][:], ACT.Sqrt).then_inc(dist_ready, 1)

            repeat(act, B // AT_ONCE, turn_of)

        @block.tensor
        def _(pe):
            def turn_of(i):
                for u in range(AT_ONCE):
                    b = AT_ONCE * i + u
                    pe.wait_ge(xn_ready, b + 1)
                    reused(pe, xT_ready, i, u, AT_ONCE)
                    for k in range(KT):
                        last = nc.tensor.transpose(ps_x[u][:, k * S:(k + 1) * S], xn[u][:, k * P:(k + 1) * P], ident[0:S, 0:S])
                    last.then_inc(turned, 1)
                for u in range(AT_ONCE):
                    b = AT_ONCE * i + u
                    pe.wait_ge(squared, b + 1)
                    reused(pe, square_ready, i, u, AT_ONCE)
                    for k in range(KT):
                        nc.tensor.matmul(ps_d[u][0:S, 0:KV], ones[:, 0:S], square[u][:, k, :], start=(k == 0), stop=False)
                    pe.wait_ge(xT_ready, b + 1)
                    pe.wait_ge(ctx_in[u], 16 * i + 16)
                    for k in range(KT):
                        last = nc.tensor.matmul(ps_d[u][0:S, 0:KV], xT[u][:, k, :], c_in[u][:, k, 0:KV], start=False, stop=(k == KT - 1))
                    last.then_inc(summed, 1)

            repeat(pe, B // AT_ONCE, turn_of)


def align(nc, table, on_path, ident):
    with ExitStack() as ctx:
        def sb(name, shape, dt=F32):
            return ctx.enter_context(nc.sbuf_tensor("align_" + name, shape, dt))

        def sem(name):
            return ctx.enter_context(nc.semaphore("align_" + name))

        cost = sb("cost", [P, DSTEPS + 2, BAND + 1])
        least = sb("least", [P, BAND])
        back = sb("back", [P, 2, DSTEPS + 1, BAND + 1], BF16)
        up = sb("up", [P, DSTEPS + 1, BAND + 1], BF16)
        path_words = (DSTEPS + 1) * (BAND + 1)
        path = table[:].rearrange("p s n -> p (s n)").bitcast(BF16)[:, 0:path_words].rearrange("p (s n) -> p s n", n=BAND + 1)
        moved = sb("moved", [P, 2, BAND + 1], BF16)
        entry = sb("entry", [P, BAND], BF16)
        ident16 = sb("ident16", [P, P], BF16)
        ps_p = [ctx.enter_context(nc.psum_tensor(f"ps_p{u}", [P, 512], BF16)) for u in range(2)]
        set_up, own, edge = sem("a_set_up"), sem("align_own"), sem("align_edge")
        path_ready, path_turned, path_kept = sem("path_ready"), sem("path_turned"), sem("path_kept")
        block = ctx.enter_context(nc.Block())

        @block.gpsimd
        def _(pool):
            nc.gpsimd.memset(cost[:, 0:1, :], FAR).then_inc(set_up, 1)
            nc.gpsimd.memset(cost[:, 1:, 0:1], FAR).then_inc(set_up, 1)
            nc.gpsimd.memset(back[:, 0, 0:1, :], 0.0).then_inc(set_up, 1)
            nc.gpsimd.memset(back[:, 1, 0:1, :], 1.0).then_inc(set_up, 1)
            nc.gpsimd.memset(back[:, :, 1:, 0:1], 0.0).then_inc(set_up, 1)
            nc.gpsimd.memset(up[:, :, 0:1], 0.0).then_inc(set_up, 1)
            nc.gpsimd.tensor_copy(ident16[:], ident[:]).then_inc(set_up, 1)
            pool.wait_ge(set_up, 1)
            nc.gpsimd.memset(cost[0:B, 0:1, 0:1], 0.0).then_inc(set_up, 1)

        @block.vector
        def _(dve):
            v = nc.vector
            dve.wait_ge(set_up, 8)
            OWN, EDGE = 2, BANDS - 1

            def forward(s):
                dve.wait_ge(edge, EDGE * s)
                here, after = cost[:, bass.ds(s, 1), :], cost[:, bass.ds(s + 1, 1), :]
                v.tensor_tensor(least[:].unsqueeze(1), here[:, :, 0:BAND], here[:, :, 1:BAND + 1], ALU.min).then_inc(own, 1)
                dve.wait_ge(own, OWN * s + 1)
                v.tensor_tensor_scan(after[:, :, 1:BAND + 1].rearrange("p a n -> p (a n)"), least[:],
                                     table[:, bass.ds(s, 1), :].rearrange("p a n -> p (a n)"),
                                     after[:, :, 0:1].rearrange("p a n -> p (a n)"), ALU.min, ALU.add).then_inc(own, 1)
                dve.wait_ge(own, OWN * s + 2)
                for r in range(1, BANDS):
                    v.tensor_copy(cost[band(r), bass.ds(s + 2, 1), 0:1], after[band(r - 1), :, BAND:BAND + 1]).then_inc(edge, 1)

            for s in range(DSTEPS):
                forward(s)
            dve.wait_ge(edge, EDGE * DSTEPS)
            chain = Chain(dve, own, OWN * DSTEPS)
            before, at = cost[:, 0:DSTEPS, :], cost[:, 1:DSTEPS + 1, :]
            diagonal, above, left = before[:, :, 0:BAND], at[:, :, 0:BAND], before[:, :, 1:BAND + 1]
            is_diagonal, is_left, is_up = (m[:, 1:DSTEPS + 1, 1:BAND + 1][:, ::-1, ::-1] for m in (back[:, 0], back[:, 1], up))
            chain.step(v.tensor_tensor(table[:], above, left, ALU.min))
            chain.step(v.tensor_tensor(is_diagonal, diagonal, table[:], ALU.is_le))
            chain.step(v.tensor_tensor(is_up, above, left, ALU.is_le))
            chain.step(v.tensor_tensor(is_up, is_up, is_diagonal, ALU.is_gt))
            chain.step(v.tensor_tensor(is_left, is_up, is_diagonal, ALU.is_equal))
            for r in range(BANDS - 1):
                chain.step(v.tensor_copy(back[band(r), 0, 2:DSTEPS + 1, 0:1], back[band(r + 1), 0, 1:DSTEPS, BAND:BAND + 1]))
                chain.step(v.tensor_copy(up[band(r), 2:DSTEPS + 1, 0:1], up[band(r + 1), 1:DSTEPS, BAND:BAND + 1]))
            chain.step(v.memset(path[:, :, 0:1], 0.0))
            chain.step(v.memset(path[:, 0:1, :], 0.0))
            chain.step(v.memset(path[band(BANDS - 1), 0:1, BAND - LAST_BAND + 1:BAND - LAST_BAND + 2], 1.0))
            own_before = OWN * DSTEPS + 8 + 2 * (BANDS - 1)

            def backward(n, more=True):
                ahead, here = path[:, bass.ds(n, 1), :], path[:, bass.ds(n + 1, 1), :]
                dve.wait_ge(edge, EDGE * (n + DSTEPS))
                v.tensor_tensor(moved[:], ahead.to_broadcast([P, 2, BAND + 1]),
                                back[:, :, bass.ds(n, 1), :].rearrange("p k a n -> p k (a n)"), ALU.mult).then_inc(own, 1)
                dve.wait_ge(own, own_before + OWN * n + 1)
                v.tensor_tensor(entry[:], moved[:, 0, 0:BAND], moved[:, 1, 1:BAND + 1], ALU.add).then_inc(own, 1)
                dve.wait_ge(own, own_before + OWN * n + 2)
                v.tensor_tensor_scan(here[:, :, 1:BAND + 1].rearrange("p a n -> p (a n)"),
                                     up[:, bass.ds(n + 1, 1), 0:BAND].rearrange("p a n -> p (a n)"), entry[:],
                                     here[:, :, 0:1].rearrange("p a n -> p (a n)"), ALU.mult, ALU.add).then_inc(path_ready, 1)
                dve.wait_ge(path_ready, n + 1)
                if more:
                    for r in range(BANDS - 1):
                        v.tensor_copy(path[band(r), bass.ds(n + 2, 1), 0:1], here[band(r + 1), :, BAND:BAND + 1]).then_inc(edge, 1)

            for n in range(DSTEPS):
                backward(n, more=n + 1 < DSTEPS)

        @block.tensor
        def _(pe):
            pe.wait_ge(set_up, 8)

            def turn_of(i):
                for u in range(2):
                    n = 2 * i + u
                    pe.wait_ge(path_ready, n + 1)
                    reused(pe, path_kept, i, u, 2)
                    nc.tensor.matmul(ps_p[u][0:BAND, 0:P], path[:, bass.ds(n + 1, 1), 1:BAND + 1].rearrange("p a n -> p (a n)"),
                                     ident16[:, :], is_transpose=True, start=True, stop=True).then_inc(path_turned, 1)

            repeat(pe, DSTEPS // 2, turn_of)
            pe.wait_ge(path_ready, DSTEPS)
            pe.wait_ge(path_kept, DSTEPS - 1)
            nc.tensor.transpose(ps_p[0][0:BAND, 0:P], path[:, DSTEPS, 1:BAND + 1], ident16[:, :]).then_inc(path_turned, 1)

        @block.scalar
        def _(act):
            def turn_of(i):
                for u in range(2):
                    n = 2 * i + u
                    act.wait_ge(path_turned, n + 1)
                    nc.scalar.copy(on_path[:, bass.ds(DSTEPS - 1 - n, 1), :].rearrange("p a n -> p (a n)"), ps_p[u][0:BAND, 0:P]).then_inc(path_kept, 1)

            repeat(act, DSTEPS // 2, turn_of)
            act.wait_ge(path_turned, DSTEPS)
            nc.scalar.copy(on_path[:, 0, :], ps_p[0][0:BAND, 0:P]).then_inc(path_kept, 1)
            act.wait_ge(path_kept, DSTEPS)


def add_aligned(nc, rows, ctx_rows, on_path, g_xattn, gate):
    AHEAD = 4
    with ExitStack() as ctx:
        def sb(name, shape, dt=F32):
            return ctx.enter_context(nc.sbuf_tensor("add_" + name, shape, dt))

        def sem(name):
            return ctx.enter_context(nc.semaphore("add_" + name))

        c_rows = [sb(f"e_ctx{u}", [BAND, BANDS, DIM]) for u in range(AHEAD)]
        pick = [sb(f"pick{u}", [BAND, BANDS, S]) for u in range(AHEAD)]
        ps_e = [ctx.enter_context(nc.psum_tensor(f"e_ps{u}", [P, 512], F32)) for u in range(AHEAD)]
        ctx_in = [sem(f"e_ctx_in{u}") for u in range(AHEAD)]
        gate_in, gate_ready, pick_ready, summed, added = sem("e_gate_in"), sem("e_gate_ready"), sem("pick_ready"), sem("e_summed"), sem("e_added")
        block = ctx.enter_context(nc.Block())

        @block.sync
        def _(sp):
            sp.dma_start(gate[:, :], g_xattn.partition_broadcast(P)).then_inc(gate_in, 16)
            def turn_of(i):
                for u in range(AHEAD):
                    b = AHEAD * i + u
                    if not isinstance(i, int):
                        sp.wait_ge(summed, b - AHEAD + 1)
                    sp.dma_start(c_rows[u][:], ctx_rows[bass.ds(b, 1)].rearrange("a n r d -> (a n) r d")).then_inc(ctx_in[u], 16)

            repeat(sp, B // AHEAD, turn_of)

        @block.scalar
        def _(act):
            act.wait_ge(gate_in, 16)
            nc.scalar.activation(gate[:, :], gate[:, :], ACT.Tanh).then_inc(gate_ready, 1)
            def turn_of(i):
                for u in range(AHEAD):
                    b = AHEAD * i + u
                    if not isinstance(i, int):
                        act.wait_ge(summed, b - AHEAD + 1)
                    for r in range(BANDS):
                        nc.scalar.copy(pick[u][:, r, :], on_path[:, r:r + S, bass.ds(B * r + b, 1)].rearrange("p s a -> p (s a)")).then_inc(pick_ready, 1)

            repeat(act, B // AHEAD, turn_of)

        @block.tensor
        def _(pe):
            def turn_of(i):
                for u in range(AHEAD):
                    b = AHEAD * i + u
                    pe.wait_ge(pick_ready, BANDS * b + BANDS)
                    pe.wait_ge(ctx_in[u], 16 * i + 16)
                    if not isinstance(i, int):
                        pe.wait_ge(added, b - AHEAD + 1)
                    for r in range(BANDS):
                        last = nc.tensor.matmul(ps_e[u][0:S, 0:DIM], pick[u][:, r, :], c_rows[u][:, r, :],
                                                start=(r == 0), stop=(r == BANDS - 1))
                    last.then_inc(summed, 1)

            repeat(pe, B // AHEAD, turn_of)

        @block.vector
        def _(dve):
            dve.wait_ge(gate_ready, 1)
            def turn_of(i):
                for u in range(AHEAD):
                    b = AHEAD * i + u
                    dve.wait_ge(summed, b + 1)
                    x_b = rows[:, bass.ds(b, 1), :].rearrange("p a n -> p (a n)")
                    nc.vector.scalar_tensor_tensor(x_b, ps_e[u][0:S, 0:DIM], gate[0:S, 1:2], x_b, ALU.mult, ALU.add).then_inc(added, 1)

            repeat(dve, B // AHEAD, turn_of)
            dve.wait_ge(added, B)


F2 = 1024
F2C = F2 // P
CAPACITY = TOKENS // EXPERTS
CT = CAPACITY // S


def route_once(nc, rows, mean, rstd, router, below, ones, ident, iota_s, xn_all, slot_put, slot_get, keep_gate, gate):
    AT_ONCE = 4
    with ExitStack() as ctx:
        def sb(name, shape, dt=F32):
            return ctx.enter_context(nc.sbuf_tensor("once_" + name, shape, dt))

        def sem(name):
            return ctx.enter_context(nc.semaphore("once_" + name))

        x_now = [sb(f"r_x{u}", [S, DIM]) for u in range(AT_ONCE)]
        kept = sem("r_kept")
        wr = sb("wr", [P, KT, EXPERTS])
        xT = [sb(f"r_xT{u}", [P, KT, S]) for u in range(AT_ONCE)]
        logit = sb("logit", [S, B, EXPERTS])
        work = sb("r_work", [S, B, EXPERTS])
        hot = sb("r_hot", [S, B, EXPERTS])
        best = sb("r_best", [S, B])
        index = sb("r_index", [S, B])
        total = sb("r_total", [S, EXPERTS, B])
        upto = sb("r_upto", [S, EXPERTS, B])
        zeros = sb("r_zeros", [S, B])
        place = sb("r_place", [S, B])
        inside = sb("r_inside", [S, B])
        beyond = sb("r_beyond", [S, B])
        token_i = sb("token_i", [S, B], I32)
        token = sb("token", [S, B])
        ps_x = [ctx.enter_context(nc.psum_tensor(f"r_ps_x{u}", [P, 512], F32)) for u in range(AT_ONCE)]
        ps_l = ctx.enter_context(nc.psum_tensor("r_ps_l", [P, 512], F32))
        ps_rank = ctx.enter_context(nc.psum_tensor("r_ps_rank", [P, 512], F32))
        ps_total = ctx.enter_context(nc.psum_tensor("r_ps_total", [P, 512], F32))
        router_in, filled = sem("router_in"), sem("r_filled")
        xn_ready, turned, xT_ready, scored = sem("r_xn_ready"), sem("r_turned"), sem("r_xT_ready"), sem("scored")
        exp_in, exp_out, hot_ready, ranked, own = sem("r_exp_in"), sem("r_exp_out"), sem("r_hot_ready"), sem("r_ranked"), sem("r_own")
        block = ctx.enter_context(nc.Block())

        @block.sync
        def _(sp):
            sp.dma_start(wr[:], router).then_inc(router_in, 16)
            sp.wait_ge(router_in, 16)

        @block.gpsimd
        def _(pool):
            nc.gpsimd.iota(token_i[:], pattern=[[S, B]], base=TOKENS, channel_multiplier=1).then_inc(filled, 1)
            nc.gpsimd.memset(zeros[:], 0.0).then_inc(filled, 1)
            pool.wait_ge(filled, 2)
            nc.gpsimd.tensor_copy(token[:], token_i[:]).then_inc(filled, 1)

        @block.tensor
        def _(pe):
            pe.wait_ge(router_in, 16)
            def turn_of(i):
                for u in range(AT_ONCE):
                    b = AT_ONCE * i + u
                    pe.wait_ge(xn_ready, b + 1)
                    reused(pe, xT_ready, i, u, AT_ONCE)
                    for k in range(KT):
                        last = nc.tensor.transpose(ps_x[u][:, k * S:(k + 1) * S], x_now[u][:, k * P:(k + 1) * P], ident[0:S, 0:S])
                    last.then_inc(turned, 1)
                for u in range(AT_ONCE):
                    b = AT_ONCE * i + u
                    pe.wait_ge(xT_ready, b + 1)
                    for k in range(KT):
                        last = nc.tensor.matmul(ps_l[0:S, bass.ds(EXPERTS * b, EXPERTS)], xT[u][:, k, :], wr[:, k, :], start=(k == 0), stop=(k == KT - 1))
                    last.then_inc(scored, 1)

            repeat(pe, B // AT_ONCE, turn_of)
            pe.wait_ge(hot_ready, 1)
            flat = hot[:].rearrange("p b e -> p (b e)")
            nc.tensor.matmul(ps_rank[0:S, 0:B * EXPERTS], below[0:S, 0:S], flat, start=True, stop=True).then_inc(ranked, 1)
            nc.tensor.matmul(ps_total[0:S, 0:B * EXPERTS], ones[0:S, 0:S], flat, start=True, stop=True).then_inc(ranked, 1)

        @block.scalar
        def _(act):
            def turn_of(i):
                for u in range(AT_ONCE):
                    b = AT_ONCE * i + u
                    act.wait_ge(turned, b + 1)
                    reused(act, scored, i, u, AT_ONCE)
                    nc.scalar.copy(xT[u][:].rearrange("p k s -> p (k s)"), ps_x[u][:, 0:KT * S]).then_inc(xT_ready, 1)
                    nc.scalar.copy(xn_all[:, bass.ds(b, 1), :].rearrange("p a n -> p (a n)"), x_now[u][:]).then_inc(kept, 1)

            repeat(act, B // AT_ONCE, turn_of)
            act.wait_ge(exp_in, 1)
            nc.scalar.activation(logit[:], logit[:], ACT.Exp).then_inc(exp_out, 1)
            act.wait_ge(kept, B)

        @block.vector
        def _(dve):
            v = nc.vector
            chain = Chain(dve, own)
            def turn_of(i):
                for u in range(AT_ONCE):
                    b = AT_ONCE * i + u
                    reused(dve, turned, i, u, AT_ONCE)
                    reused(dve, kept, i, u, AT_ONCE)
                    normalize(nc, x_now[u][:], rows[:, bass.ds(b, 1), :].rearrange("p a n -> p (a n)"), mean, rstd, b).then_inc(xn_ready, 1)

            repeat(dve, B // AT_ONCE, turn_of)
            dve.wait_ge(scored, B)
            chain.step(v.tensor_copy(logit[:], ps_l[0:S, 0:B * EXPERTS].rearrange("p (b e) -> p b e", e=EXPERTS)))

            def every(a):
                return a[:].unsqueeze(2).to_broadcast([S, B, EXPERTS])

            chain.step(v.tensor_reduce(best[:], logit[:], AX.X, ALU.max))
            v.tensor_tensor(logit[:], logit[:], every(best), ALU.subtract).then_inc(exp_in, 1)
            dve.wait_ge(exp_out, 1)
            chain.step(v.tensor_reduce(inside[:], logit[:], AX.X, ALU.add))
            chain.step(v.reciprocal(keep_gate[:], inside[:]))
            chain.step(v.tensor_scalar(keep_gate[:], keep_gate[:], gate[0:S, 1:2], None, ALU.mult))
            chain.step(v.tensor_reduce(best[:], logit[:], AX.X, ALU.max))
            chain.step(v.tensor_tensor(work[:], logit[:], every(best), ALU.is_lt))
            chain.step(v.scalar_tensor_tensor(work[:], work[:], 2.0 * EXPERTS, iota_s[:], ALU.mult, ALU.add))
            chain.step(v.tensor_reduce(index[:], work[:], AX.X, ALU.min))
            v.tensor_tensor(hot[:], iota_s[:], every(index), ALU.is_equal).then_inc(hot_ready, 1)
            dve.wait_ge(ranked, 2)
            dve.wait_ge(filled, 3)
            chain.step(v.tensor_copy(total[:], ps_total[0:S, 0:B * EXPERTS].rearrange("p (b e) -> p e b", e=EXPERTS)))
            chain.together(*[v.tensor_tensor_scan(upto[:, e, :], zeros[:], total[:, e, :], 0.0, ALU.add, ALU.add)
                             for e in range(EXPERTS)])
            chain.step(v.tensor_tensor(upto[:], upto[:], total[:], ALU.subtract))
            chain.step(v.tensor_tensor(work[:], ps_rank[0:S, 0:B * EXPERTS].rearrange("p (b e) -> p b e", e=EXPERTS),
                                       upto[:].rearrange("p e b -> p b e"), ALU.add))
            chain.step(v.tensor_tensor(work[:], work[:], hot[:], ALU.mult))
            chain.step(v.tensor_reduce(place[:], work[:], AX.X, ALU.add))
            chain.step(v.tensor_scalar(inside[:], place[:], float(CAPACITY), None, ALU.is_le))
            chain.step(v.tensor_tensor(keep_gate[:], keep_gate[:], inside[:], ALU.mult))
            chain.step(v.scalar_tensor_tensor(place[:], index[:], float(CAPACITY), place[:], ALU.mult, ALU.add))
            chain.step(v.tensor_scalar(place[:], place[:], -1.0, None, ALU.add))
            chain.step(v.tensor_tensor(place[:], place[:], inside[:], ALU.mult))
            chain.step(v.tensor_copy(slot_get[:], place[:]))
            chain.step(v.tensor_scalar(beyond[:], inside[:], -1.0, 1.0, ALU.mult, ALU.add))
            chain.step(v.tensor_tensor(beyond[:], beyond[:], token[:], ALU.mult))
            chain.step(v.tensor_tensor(place[:], place[:], beyond[:], ALU.add))
            chain.step(v.tensor_copy(slot_put[:], place[:]))


def capacity_experts(nc, xn_all, slot_put, buffer, result, w1, b1, w2, b2, ident):
    with ExitStack() as ctx:
        def sb(name, shape, dt=F32):
            return ctx.enter_context(nc.sbuf_tensor("cap_" + name, shape, dt))

        def ps(name):
            return ctx.enter_context(nc.psum_tensor("cap_" + name, [P, 512], F32))

        def sem(name):
            return ctx.enter_context(nc.semaphore("cap_" + name))

        w1_sb = [sb(f"w1_{u}", [P, KT, F2]) for u in range(2)]
        w2_sb = [sb(f"w2_{u}", [P, F2C, DIM]) for u in range(2)]
        b2_sb = [sb(f"b2_{u}", [S, DIM]) for u in range(2)]
        b1_sb = sb("b1_sb", [P, EXPERTS, F2C])
        x = [sb(f"f_x{u}", [S, CT, DIM]) for u in range(2)]
        xT = sb("f_xT", [P, KT, CAPACITY])
        mid = sb("f_mid", [P, F2C, CAPACITY])
        y = [sb(f"f_y{u}", [S, CT, DIM]) for u in range(2)]
        ps_x = [ps(f"f_ps_x{u}") for u in range(KT)]
        ps_m = [ps(f"f_ps_m{u}") for u in range(2)]
        ps_y = [ps(f"f_ps_y{u}") for u in range(2)]
        bias_in = sem("f_bias_in")
        dispatched = sem("f_dispatched")
        x_in, loaded, stored = ([sem(f"f_{what}{u}") for u in range(2)] for what in ("x_in", "loaded", "stored"))
        turned, xT_ready, m_done, mid_ready, y_done, y_ready = (sem("f_turned"), sem("f_xT_ready"), sem("f_m_done"),
                                                               sem("f_mid_ready"), sem("f_y_done"), sem("f_y_ready"))
        block = ctx.enter_context(nc.Block())

        def one(dram, e):
            return dram[bass.ds(e, 1)]

        @block.sync
        def _(sp):
            sp.dma_start(b1_sb[:], b1).then_inc(bias_in, 16)

            def load_x(e, u):
                sp.dma_start(x[u][:], buffer[bass.ds(e * CAPACITY, CAPACITY), :].rearrange("(c s) d -> s c d", s=S)).then_inc(x_in[u], 16)

            def load_weights(e, u):
                sp.dma_start(w1_sb[u][:], one(w1, e).rearrange("a p k n -> (a p) k n")).then_inc(loaded[u], 16)
                sp.dma_start(w2_sb[u][:], one(w2, e).rearrange("a p k n -> (a p) k n")).then_inc(loaded[u], 16)
                sp.dma_start(b2_sb[u][:], one(b2, e).rearrange("a n -> (a n)").partition_broadcast(S)).then_inc(loaded[u], 16)

            for u in range(2):
                load_weights(u, u)
            sp.wait_ge(dispatched, 16 * B)
            for u in range(2):
                load_x(u, u)
            with sp.Fori(1, EXPERTS // 2) as i:
                for u in range(2):
                    sp.wait_ge(y_ready, CT * (2 * i + u - 1))
                    load_x(2 * i + u, u)
                    load_weights(2 * i + u, u)
            sp.wait_ge(bias_in, 16)

        @block.gpsimd
        def _(pool):
            for b in range(B):
                nc.gpsimd.indirect_dma_start(buffer, bass.IndirectOffsetOnAxis(ap=slot_put[:, b:b + 1], axis=0),
                                             xn_all[:, b, :], None).then_inc(dispatched, 16)
            pool.wait_ge(dispatched, 16 * B)

            def turn_of(i):
                for u in range(2):
                    e = 2 * i + u
                    pool.wait_ge(y_ready, CT * e + CT)
                    pool.dma_start(result[bass.ds(e * CAPACITY, CAPACITY), :].rearrange("(c s) d -> s c d", s=S), y[u][:]).then_inc(stored[u], 16)

            repeat(pool, EXPERTS // 2, turn_of)
            for u in range(2):
                pool.wait_ge(stored[u], 16 * (EXPERTS // 2))

        @block.tensor
        def _(pe):
            def turn_x(e, u):
                pe.wait_ge(x_in[u], 8 * (e - u) + 16)
                for k in range(KT):
                    for c in range(CT):
                        last = nc.tensor.transpose(ps_x[k][:, c * S:(c + 1) * S], x[u][:, c, k * P:(k + 1) * P], ident[0:S, 0:S])
                    last.then_inc(turned, 1)

            turn_x(0, 0)

            def turns_of(i, more=True):
                for u in range(2):
                    e = 2 * i + u
                    pe.wait_ge(loaded[u], 48 * i + 48)
                    pe.wait_ge(xT_ready, KT * e + KT)
                    for f in range(F2C):
                        n = F2C * e + f
                        if f >= 2:
                            pe.wait_ge(mid_ready, n - 1)
                        else:
                            pe.wait_ge(mid_ready, F2C * e)
                        for k in range(KT):
                            last = nc.tensor.matmul(ps_m[f % 2][:, 0:CAPACITY], w1_sb[u][:, k, f * P:(f + 1) * P], xT[:, k, :],
                                                    start=(k == 0), stop=(k == KT - 1))
                        last.then_inc(m_done, 1)
                    if u == 0 or more:
                        turn_x(e + 1, 1 - u)
                    pe.wait_ge(mid_ready, F2C * e + F2C)
                    for c in range(CT):
                        if c >= 2:
                            pe.wait_ge(y_ready, CT * e + c - 1)
                        else:
                            pe.wait_ge(y_ready, CT * e)
                        for f in range(F2C):
                            last = nc.tensor.matmul(ps_y[c % 2][0:S, 0:DIM], mid[:, f, c * S:(c + 1) * S], w2_sb[u][:, f, :],
                                                    start=(f == 0), stop=(f == F2C - 1))
                        last.then_inc(y_done, 1)

            repeat(pe, EXPERTS // 2 - 1, turns_of)
            turns_of(EXPERTS // 2 - 1, more=False)

        @block.scalar
        def _(act):
            act.wait_ge(bias_in, 16)
            def turn_of(i):
                for u in range(2):
                    e = 2 * i + u
                    act.wait_ge(y_done, CT * e)
                    for f in range(F2C):
                        act.wait_ge(m_done, F2C * e + f + 1)
                        nc.scalar.activation(mid[:, f, :], ps_m[f % 2][:, 0:CAPACITY], ACT.Relu,
                                             bias=b1_sb[:, bass.ds(e, 1), f:f + 1].rearrange("p a n -> p (a n)")).then_inc(mid_ready, 1)

            repeat(act, EXPERTS // 2, turn_of)

        @block.vector
        def _(dve):
            def take_x(e):
                for k in range(KT):
                    dve.wait_ge(turned, KT * e + k + 1)
                    nc.vector.tensor_copy(xT[:, k, :], ps_x[k][:, 0:CAPACITY]).then_inc(xT_ready, 1)

            take_x(0)

            def turns_of(i, more=True):
                for u in range(2):
                    e = 2 * i + u
                    if u == 0 or more:
                        dve.wait_ge(m_done, F2C * e + F2C)
                        take_x(e + 1)
                    dve.wait_ge(stored[u], 16 * i)
                    dve.wait_ge(loaded[u], 48 * i + 48)
                    for c in range(CT):
                        dve.wait_ge(y_done, CT * e + c + 1)
                        nc.vector.tensor_tensor(y[u][:, c, :], ps_y[c % 2][0:S, 0:DIM], b2_sb[u][:], ALU.add).then_inc(y_ready, 1)

            repeat(dve, EXPERTS // 2 - 1, turns_of)
            turns_of(EXPERTS // 2 - 1, more=False)


def finish(nc, rows, result, slot_get, keep_gate, out):
    with ExitStack() as ctx:
        N = 8
        got = [ctx.enter_context(nc.sbuf_tensor(f"got{u}", [S, DIM], F32)) for u in range(N)]
        got_in = [ctx.enter_context(nc.semaphore(f"got_in{u}")) for u in range(N)]
        out_ready = ctx.enter_context(nc.semaphore("out_ready"))
        out_stored = ctx.enter_context(nc.semaphore("out_stored"))
        block = ctx.enter_context(nc.Block())

        @block.gpsimd
        def _(pool):
            for b in range(B):
                if b >= N:
                    pool.wait_ge(out_ready, b - N + 1)
                nc.gpsimd.indirect_dma_start(got[b % N][:], None, result,
                                             bass.IndirectOffsetOnAxis(ap=slot_get[:, b:b + 1], axis=0)).then_inc(got_in[b % N], 16)

        @block.vector
        def _(dve):
            for b in range(B):
                dve.wait_ge(got_in[b % N], 16 * (b // N + 1))
                nc.vector.scalar_tensor_tensor(rows[:, b, :], got[b % N][:], keep_gate[:, b:b + 1], rows[:, b, :],
                                               ALU.mult, ALU.add).then_inc(out_ready, 1)

        @block.sync
        def _(sp):
            def turn_of(b):
                sp.wait_ge(out_ready, b + 1)
                sp.dma_start(out[bass.ds(b, 1)].rearrange("a s d -> (a s) d"),
                             rows[:, bass.ds(b, 1), :].rearrange("p a n -> p (a n)")).then_inc(out_stored, 16)

            repeat(sp, B, turn_of)
            sp.wait_ge(out_stored, 16 * B)


def constants_for_routing(nc, below, iota_e, iota_s):
    with ExitStack() as ctx:
        counted_e = ctx.enter_context(nc.sbuf_tensor("counted_e", [P, TILES, EXPERTS], I32))
        counted_s = ctx.enter_context(nc.sbuf_tensor("counted_s", [S, B, EXPERTS], I32))
        counted = ctx.enter_context(nc.semaphore("counted"))
        block = ctx.enter_context(nc.Block())

        @block.gpsimd
        def _(pool):
            nc.gpsimd.memset(below[:], 1.0).then_inc(counted, 1)
            nc.gpsimd.iota(counted_e[:], pattern=[[0, TILES], [1, EXPERTS]], base=0, channel_multiplier=0).then_inc(counted, 1)
            nc.gpsimd.iota(counted_s[:], pattern=[[0, B], [1, EXPERTS]], base=0, channel_multiplier=0).then_inc(counted, 1)
            pool.wait_ge(counted, 3)
            nc.gpsimd.affine_select(out=below[:], in_=below[:], compare_op=ALU.is_ge, fill=0.0, base=0,
                                    pattern=[[1, P]], channel_multiplier=-1).then_inc(counted, 1)
            nc.gpsimd.tensor_copy(iota_e[:], counted_e[:]).then_inc(counted, 1)
            nc.gpsimd.tensor_copy(iota_s[:], counted_s[:]).then_inc(counted, 1)
            pool.wait_ge(counted, 6)


def clear_semaphores(nc):
    numbers = sorted(nc.released_uncleared_semaphores)
    starts = [n for n in numbers if n - 1 not in numbers]
    with nc.Block() as block:

        @block.gpsimd
        def _(pool):
            for first in starts:
                stop = first
                while stop in numbers:
                    stop += 1
                pool.dma_reset(range(first, stop))
                pool.sem_clear(range(first, stop))


def build(nc, x, ctx_rows, ctxT, wqT, wkT, bqk, wvT, bv, woT, bo, g_xattn, g_ffn, whhT, wihT, wcT, ctx_b, weT, guT, dnT,
          router, w1, b1, w2, b2, out):
    def dram(name, shape):
        return nc.dram_tensor(name, shape, F32, kind="Internal").ap()

    x1 = dram("x1", (B, S, DIM))
    x2 = dram("x2", (B, S, DIM))
    states = dram("states", (TILES, STEPS, B, GD))
    moe_in = dram("moe_in", (MOE_TILES * P, DIM))
    moe_out = dram("moe_out", (MOE_TILES * P, DIM))
    buffer = dram("buffer", (2 * TOKENS, DIM))
    result = dram("result", (TOKENS, DIM))
    h_rows = moe_in[0:TOKENS].rearrange("(b s) d -> b s d", b=B)

    def pieces(rows, n):
        flat = rows.rearrange("r d -> (r d)").rearrange("(p c w) -> c p w", p=P, c=n)
        return [(flat[c], flat.shape[2]) for c in range(n)]

    to_clear = pieces(moe_in[TOKENS:MOE_TILES * P], 8) + pieces(buffer[0:TOKENS], 4)

    with ExitStack() as ctx:
        def sb(stack, name, shape, dt=F32, **more):
            return stack.enter_context(nc.sbuf_tensor(name, shape, dt, **more))

        ident = sb(ctx, "ident", [P, P])
        ones = sb(ctx, "ones", [P, P])
        gate = sb(ctx, "gate_ffn", [P, 2])
        gate_x = sb(ctx, "gate_x", [P, 2])
        below = sb(ctx, "below", [P, P])
        iota_e = sb(ctx, "iota_e", [P, TILES, EXPERTS])
        iota_s = sb(ctx, "iota_s", [S, B, EXPERTS])
        neg_ident = sb(ctx, "neg_ident", [P, P])
        whh_in = ctx.enter_context(nc.semaphore("whh_in"))
        cleared_rows = ctx.enter_context(nc.semaphore("cleared_rows"))
        shared_in = ctx.enter_context(nc.semaphore("shared_in"))
        h_in = ctx.enter_context(nc.semaphore("h_in"))
        constants(nc, ident, neg_ident, ones)
        constants_for_routing(nc, below, iota_e, iota_s)

        with ExitStack() as mixture:
            stat = sb(mixture, "stat", [P, TILES, NSTAT])
            with ExitStack() as recurrent:
                whh = sb(recurrent, "whh", [P, GC, 3 * GD])
                with ExitStack() as first:
                    rows = sb(first, "rows_x", [S, B, DIM], side="right")
                    mean = sb(first, "mean_x", [S, B], side="right")
                    rstd = sb(first, "rstd_x", [S, B], side="right")
                    load_rows(nc, "x", rows, x)
                    row_statistics(nc, "x", rows, mean[:], rstd[:])
                    attention(nc, rows, mean, rstd, ctxT, wqT, wkT, bqk, wvT, bv, woT, bo, g_xattn, x1, ident, neg_ident,
                              whh, whhT, whh_in, to_clear, cleared_rows)
                    row_statistics(nc, "x1", rows, mean[:], rstd[:])
                    hT = sb(recurrent, "hT", [P, KT, B, S])
                    normalized_rows_out(nc, rows, mean, rstd, h_rows, hT, ident)
                gru(nc, whh, whh_in, wihT, hT, wcT, ctx_b, weT, states, stat, ident)
            weight = sb(mixture, "weight", [P, TILES, 2])
            slot = sb(mixture, "slot", [P, TILES, 2], U32)
            tile_expert = sb(mixture, "tile_expert", [1, MOE_TILES], I32)
            with ExitStack() as experts:
                gu = sb(experts, "gu", [P, EXPERTS + 1, KT, 2 * FF])
                dn = sb(experts, "dn", [P, EXPERTS + 1, FC, DIM])
                h_all = sb(experts, "h_all", [P, TILES, DIM])
                routing(nc, stat, weight, slot, tile_expert, iota_e, below, ones, g_ffn, gate, gu, guT, dn, dnT, shared_in,
                        h_rows, h_all, h_in)
                expert_tiles(nc, moe_in, moe_out, gu, guT, dn, dnT, tile_expert, shared_in, ident, slot, h_all, h_in)
            combine(nc, moe_out, x1, weight, slot, gate, x2)

        clear_semaphores(nc)
        rows = sb(ctx, "rows", [S, B, DIM])
        mean = sb(ctx, "mean", [S, B])
        rstd = sb(ctx, "rstd", [S, B])
        load_rows(nc, "x2", rows, x2)
        row_statistics(nc, "x2", rows, mean[:], rstd[:])
        with ExitStack() as alignment:
            on_path = sb(alignment, "on_path", [BAND, DSTEPS, P], BF16)
            with ExitStack() as tables:
                table = sb(tables, "table", [P, DSTEPS, BAND])
                distances(nc, rows, mean, rstd, ctxT, table, ones, ident)
                align(nc, table, on_path, ident)
            add_aligned(nc, rows, ctx_rows, on_path, g_xattn, gate_x)
        row_statistics(nc, "x3", rows, mean[:], rstd[:])
        with ExitStack() as last:
            xn_all = sb(last, "xn_all", [S, B, DIM])
            slot_put = sb(last, "slot_put", [S, B], U32)
            slot_get = sb(last, "slot_get", [S, B], U32)
            keep_gate = sb(last, "keep_gate", [S, B])
            route_once(nc, rows, mean, rstd, router, below, ones, ident, iota_s, xn_all, slot_put, slot_get, keep_gate, gate)
            capacity_experts(nc, xn_all, slot_put, buffer, result, w1, b1, w2, b2, ident)
            finish(nc, rows, result, slot_get, keep_gate, out)


def layouts(i):
    import numpy as np

    def tiles(w):
        return w.T.reshape(-1, P, w.shape[0]).transpose(1, 0, 2)

    def pad_heads(w):
        out = np.zeros((P, KT, HG, 4, 32), w.dtype)
        out[..., 0:HD] = w.reshape(HG, 4, HD, KT, P).transpose(4, 3, 0, 1, 2)
        return out.reshape(P, KT, HG * P)

    att, ffn, moe = "L0_xattn_", "L0_ffn_", "L1_ffn_"
    ctxT = np.zeros((B, P, KT, KVP), i["ctx_1024"].dtype)
    ctxT[..., 0:KV] = i["ctx_1024"].reshape(B, KV, KT, P).transpose(0, 3, 2, 1)
    ctx_rows = np.zeros((B, BANDS * BAND, DIM), i["ctx_1024"].dtype)
    ctx_rows[:, 0:KV] = i["ctx_1024"]
    ctx_rows = ctx_rows.reshape(B, BANDS, BAND, DIM)[:, :, ::-1].transpose(0, 2, 1, 3)
    bqk = np.zeros((4, 32, 2, HG), i[att + "bq"].dtype)
    bqk[:, 0:HD, 0, :] = i[att + "bq"].reshape(HG, 4, HD).transpose(1, 2, 0)
    bqk[:, 0:HD, 1, :] = i[att + "bk"].reshape(HG, 4, HD).transpose(1, 2, 0)
    bqk[:, HD, 1, :] = 1

    def with_shared(name):
        return np.concatenate([i[ffn + name], i[ffn + "shared_" + name][None]])

    gate_up = np.concatenate([with_shared("gate_w"), with_shared("up_w")], 1)
    return {
        "x": i["x"], "ctx_rows": ctx_rows, "ctxT": ctxT,
        "wqT": pad_heads(i[att + "Wq"]), "wkT": pad_heads(i[att + "Wk"]), "bqk": bqk.reshape(P, 2, HG),
        "wvT": tiles(i[att + "Wv"]), "bv": i[att + "bv"], "woT": tiles(i[att + "Wo"]), "bo": i[att + "bo"],
        "g_xattn": i["g_xattn"], "g_ffn": i["g_ffn"],
        "whhT": tiles(i[ffn + "gru_w_hh"]), "wihT": tiles(i[ffn + "gru_w_ih"]), "wcT": tiles(i[ffn + "ctx_w"]),
        "ctx_b": i[ffn + "ctx_b"], "weT": tiles(i[ffn + "expr_w"]),
        "guT": gate_up.reshape(EXPERTS + 1, 2 * FF, KT, P).transpose(3, 0, 2, 1),
        "dnT": with_shared("down_w").reshape(EXPERTS + 1, DIM, FC, P).transpose(3, 0, 2, 1),
        "router": i[moe + "router_w"].reshape(KT, P, EXPERTS).transpose(1, 0, 2),
        "w1": i[moe + "w1"].reshape(EXPERTS, KT, P, F2).transpose(0, 2, 1, 3),
        "b1": i[moe + "b1"].reshape(EXPERTS, F2C, P).transpose(2, 0, 1),
        "w2": i[moe + "w2"].reshape(EXPERTS, F2C, P, DIM).transpose(0, 2, 1, 3),
        "b2": i[moe + "b2"],
    }


def kernel(**inputs):
    import numpy as np
    import concourse.bacc as bacc
    from concourse.bass_utils import run_bass_kernel_spmd

    nc = bacc.Bacc("TRN2", target_bir_lowering=False, num_devices=1)
    arrays, args = {}, []
    for name, a in layouts({k: np.asarray(v) for k, v in inputs.items()}).items():
        a = np.ascontiguousarray(a)
        arrays[f"in_{name}"] = a
        args.append(nc.dram_tensor(f"in_{name}", a.shape, mybir.dt.from_np(a.dtype), kind="ExternalInput").ap())
    args.append(nc.dram_tensor("out_x", (B, S, DIM), F32, kind="ExternalOutput").ap())
    build(nc, *args)
    result = run_bass_kernel_spmd(nc, [arrays], core_ids=[0])
    return result.results[0]["out_x"]
```

```python
from contextlib import ExitStack

import concourse.bass as bass
from concourse import mybir

F32 = mybir.dt.float32
BF16 = mybir.dt.bfloat16
I32 = mybir.dt.int32
U32 = mybir.dt.uint32
ALU = mybir.AluOpType
ACT = mybir.ActivationFunctionType
AX = mybir.AxisListType

P = 128
B, S, DIM = 32, 100, 256
KV, KC = 361, 121
KVP = 3 * KC
KLAST = KV - 2 * KC
KT = DIM // P
HEADS, HD = 16, 16
HG = HEADS // 4
LN_EPS = 1e-5


class Chain:

    def __init__(self, engine, semaphore, start=0):
        self.engine, self.semaphore, self.value = engine, semaphore, start

    def step(self, instruction):
        self.value = self.value + 1
        instruction.then_inc(self.semaphore, 1)
        self.engine.wait_ge(self.semaphore, self.value)

    def together(self, *instructions):
        for instruction in instructions:
            instruction.then_inc(self.semaphore, 1)
        self.value = self.value + len(instructions)
        self.engine.wait_ge(self.semaphore, self.value)


def repeat(engine, count, turn_of):
    turn_of(0)
    with engine.Fori(1, count) as i:
        turn_of(i)


def reused(engine, semaphore, i, u, of, per=1):
    if not isinstance(i, int):
        engine.wait_ge(semaphore, per * (of * (i - 1) + u + 1))


def row_statistics(nc, stage, rows, mean, rstd, source=None, on_sync=None, on_gpsimd=None):
    with ExitStack() as ctx:
        GROUP = 8
        rows_in = [ctx.enter_context(nc.semaphore(f"rows_in_{stage}_{g}")) for g in range(B // GROUP)]
        stats = ctx.enter_context(nc.sbuf_tensor(f"stats_{stage}", [S, GROUP, 6], F32))
        mean_var = ctx.enter_context(nc.sbuf_tensor(f"mean_var_{stage}", [S, GROUP, 2], F32))
        stats_done = ctx.enter_context(nc.semaphore(f"stats_done_{stage}"))
        aggregated = ctx.enter_context(nc.semaphore(f"aggregated_{stage}"))
        taken = ctx.enter_context(nc.semaphore(f"taken_{stage}"))
        root_ready = ctx.enter_context(nc.semaphore(f"root_ready_{stage}"))
        block = ctx.enter_context(nc.Block())

        if source is not None:

            @block.sync
            def _(sp):
                for g in range(B // GROUP):
                    some = slice(g * GROUP, (g + 1) * GROUP)
                    sp.dma_start(rows[:, some, :], source[some].rearrange("b s d -> s b d")).then_inc(rows_in[g], 16)
                if on_sync:
                    on_sync(sp)

        if on_gpsimd:

            @block.gpsimd
            def _(pool):
                on_gpsimd(pool)

        @block.vector
        def _(dve):
            for g in range(B // GROUP):
                if source is not None:
                    dve.wait_ge(rows_in[g], 16)
                for u in range(GROUP):
                    nc.vector.bn_stats(stats[:, u, :], rows[:, GROUP * g + u, :]).then_inc(stats_done, 1)
                dve.wait_ge(taken, 2 * g)
                for u in range(GROUP):
                    dve.wait_ge(stats_done, GROUP * g + u + 1)
                    nc.vector.bn_aggr(mean_var[:, u, :], stats[:, u, :]).then_inc(aggregated, 1)
                dve.wait_ge(aggregated, GROUP * g + GROUP)
                group = slice(GROUP * g, GROUP * g + GROUP)
                nc.vector.tensor_copy(mean[:, group], mean_var[:, :, 0]).then_inc(taken, 1)
                nc.vector.tensor_scalar(rstd[:, group], mean_var[:, :, 1], LN_EPS, None, ALU.add).then_inc(taken, 1)
            dve.wait_ge(taken, 2 * (B // GROUP) - 1)
            dve.wait_ge(root_ready, 1)
            nc.vector.reciprocal(rstd, rstd).then_inc(aggregated, 1)
            dve.wait_ge(aggregated, B + 1)

        @block.scalar
        def _(act):
            act.wait_ge(taken, 2 * (B // GROUP))
            nc.scalar.activation(rstd, rstd, ACT.Sqrt).then_inc(root_ready, 1)


def normalize(nc, out, rows, mean, rstd, b):
    return nc.vector.tensor_scalar(out, rows, mean[:, bass.ds(b, 1)], rstd[:, bass.ds(b, 1)], ALU.subtract, ALU.mult)


def normalized_rows_out(nc, rows, mean, rstd, h_rows, hT, ident):
    AT_ONCE = 4
    with ExitStack() as ctx:
        h = [ctx.enter_context(nc.sbuf_tensor(f"h{u}", [S, DIM], F32)) for u in range(AT_ONCE)]
        turned = [ctx.enter_context(nc.psum_tensor(f"turned{u}", [P, 512], F32)) for u in range(AT_ONCE)]
        h_ready = ctx.enter_context(nc.semaphore("h_ready"))
        h_stored = [ctx.enter_context(nc.semaphore(f"h_stored{u}")) for u in range(AT_ONCE)]
        h_turned = ctx.enter_context(nc.semaphore("h_turned"))
        hT_ready = ctx.enter_context(nc.semaphore("hT_ready"))
        block = ctx.enter_context(nc.Block())

        @block.vector
        def _(dve):
            def turn_of(i):
                for u in range(AT_ONCE):
                    b = AT_ONCE * i + u
                    dve.wait_ge(h_stored[u], 16 * i)
                    reused(dve, h_turned, i, u, AT_ONCE)
                    normalize(nc, h[u][:], rows[:, bass.ds(b, 1), :].rearrange("p a n -> p (a n)"), mean, rstd, b).then_inc(h_ready, 1)

            repeat(dve, B // AT_ONCE, turn_of)

        @block.tensor
        def _(pe):
            def turn_of(i):
                for u in range(AT_ONCE):
                    b = AT_ONCE * i + u
                    pe.wait_ge(h_ready, b + 1)
                    reused(pe, hT_ready, i, u, AT_ONCE)
                    for k in range(KT):
                        last = nc.tensor.transpose(turned[u][:, k * S:(k + 1) * S], h[u][:, k * P:(k + 1) * P], ident[0:S, 0:S])
                    last.then_inc(h_turned, 1)

            repeat(pe, B // AT_ONCE, turn_of)

        @block.scalar
        def _(act):
            def turn_of(i):
                for u in range(AT_ONCE):
                    b = AT_ONCE * i + u
                    act.wait_ge(h_turned, b + 1)
                    nc.scalar.copy(hT[:, :, bass.ds(b, 1), :].rearrange("p k a s -> p k (a s)"),
                                   turned[u][:, 0:KT * S].rearrange("p (k s) -> p k s", k=KT)).then_inc(hT_ready, 1)

            repeat(act, B // AT_ONCE, turn_of)
            act.wait_ge(hT_ready, B)

        @block.sync
        def _(sp):
            def turn_of(i):
                for u in range(AT_ONCE):
                    b = AT_ONCE * i + u
                    sp.wait_ge(h_ready, b + 1)
                    sp.dma_start(h_rows[bass.ds(b, 1)].rearrange("a s d -> (a s) d"), h[u][:]).then_inc(h_stored[u], 16)

            repeat(sp, B // AT_ONCE, turn_of)
            for u in range(AT_ONCE):
                sp.wait_ge(h_stored[u], 16 * (B // AT_ONCE))


def constants(nc, pool, filled, ident, one_row):
    nc.gpsimd.memset(ident[:, :], 0.0).then_inc(filled, 1)
    nc.gpsimd.memset(one_row[:, :], 1.0).then_inc(filled, 1)
    pool.wait_ge(filled, 2)
    nc.gpsimd.affine_select(out=ident[:, :], in_=ident[:, :], compare_op=ALU.not_equal, fill=1.0,
                            base=0, pattern=[[-1, P]], channel_multiplier=1).then_inc(filled, 1)
    pool.wait_ge(filled, 3)


def pipelined(engine, count, turn_of):
    turn_of(0, 0, True, False)
    with engine.Fori(1, count // 2) as i:
        turn_of(2 * i - 1, 1, False, False)
        turn_of(2 * i, 0, False, False)
    turn_of(count - 1, (count - 1) % 2, False, True)


def at_least(engine, semaphore, value):
    if not isinstance(value, int) or value > 0:
        engine.wait_ge(semaphore, value)


def attention_weights(nc, ctx, wqT, wkT, bqk, wvT, bv, woT, bo, head_mask, g_xattn):
    def sb(name, shape):
        return ctx.enter_context(nc.sbuf_tensor("att_" + name, shape, F32))

    tiles = [sb(name, [P, KT, DIM]) for name in ("wq", "wk", "wv", "wo")]
    tiles += [sb("bq_bk", [P, 2, KT]), sb("head_mask", [P, P // HD]), sb("bv_all", [P, DIM]), sb("bo_gated", [P, DIM]),
              sb("gate", [P, 2])]
    sources = [wqT, wkT, wvT, woT, bqk, head_mask] + [row.partition_broadcast(P) for row in (bv, bo, g_xattn)]
    return tiles, sources


def attention(nc, rows, mean, rstd, ctxT, weights, weights_in, x1, ident,
              whh, whhT, whh_in, to_clear, cleared_rows):
    with ExitStack() as ctx:
        def sb(name, shape, dt=F32):
            return ctx.enter_context(nc.sbuf_tensor("att_" + name, shape, dt))

        def ps(name):
            return ctx.enter_context(nc.psum_tensor("att_" + name, [P, 512], F32))

        def sem(name):
            return ctx.enter_context(nc.semaphore("att_" + name))

        AHEAD, BANKS = 3, 4
        HT = HEADS // KT
        LAST_VALUES, LAST_OUTPUTS, TURN_X, BACK, TURN_ATTN, OUTPUT, QUERIES = 0, 1, 1, 3, 5, 7, 9
        KEYS, VALUES = (2, 10), (12, 14)
        OUTPUTS = {6: 0, 11: 1, 13: 2}
        wq, wk, wv, wo, bq_bk, mask_sb, bv_all, bo_gated, gate = weights
        c_in = [sb(f"c_in{u}", [P, KT, KVP]) for u in range(2)]
        xn = sb("xn", [S, DIM])
        xnT = sb("xnT", [P, KT, S])
        q_all = sb("q_all", [P, KT, S])
        qT = [sb(f"qT{u}", [P, HT, KT, S]) for u in range(2)]
        kT = [sb(f"kT{u}", [P, KT, KVP]) for u in range(2)]
        v = [sb(f"v{u}", [KC, 3, HEADS, 32]) for u in range(2)]
        zero_rows = sb("zero_rows", [P, max(dram.shape[2] for dram in to_clear)])
        neg_max = sb("neg_max", [S, BANKS])
        probs = [sb(f"probs{n}", [S, KVP]) for n in range(BANKS)]
        probsT = [sb(f"probsT{n}", [KC, 4, 3 * S]) for n in range(2)]
        att = sb("att", [P, HG, S])
        inverse = sb("inverse", [S, HEADS])
        attn = sb("attn", [S, HEADS, HD])
        attnT = sb("attnT", [P, KT, S])

        score = [ps(f"score{n}") for n in range(BANKS)]
        turned = ps("turned")
        outs = ps("outs")
        proj = ps("proj")
        misc = ps("misc")

        ctx_arrived = [sem(f"ctx_arrived{u}") for u in range(2)]
        stored = sem("x1_stored")
        gate_ready, cleared, bias_ready = sem("gate_ready"), sem("cleared"), sem("bias_ready")
        xn_ready, bias_added = sem("xn_ready"), sem("bias_added")
        xnT_psum, xnT_ready = sem("xnT_psum"), sem("xnT_ready")
        q_psum, q_copied, q_ready = sem("q_psum"), sem("q_copied"), sem("q_ready")
        k_psum, k_ready = sem("k_psum"), sem("k_ready")
        v_psum, v_ready = sem("v_psum"), sem("v_ready")
        s_psum, max_ready, p_ready = sem("s_psum"), sem("max_ready"), sem("p_ready")
        t_psum, even_ready, odd_ready = sem("t_psum"), sem("even_ready"), sem("odd_ready")
        o_psum, att_ready = sem("o_psum"), sem("att_ready")
        back_psum, inverse_ready, attn_ready = sem("back_psum"), sem("inverse_ready"), sem("attn_ready")
        attnT_psum, attnT_ready = sem("attnT_psum"), sem("attnT_ready")
        y_psum, x1_ready = sem("y_psum"), sem("x1_ready")
        block = ctx.enter_context(nc.Block())

        def rows_of(b):
            return rows[:, bass.ds(b, 1), :].rearrange("p a n -> p (a n)")

        def ahead_of(b, u, h, last):
            if h + AHEAD < HEADS:
                return b, u, h + AHEAD
            return None if last else (b + 1, 1 - u, h + AHEAD - HEADS)

        @block.sync
        def _(sp):
            def turn_of(i):
                for u in range(2):
                    b = 2 * i + u
                    if not isinstance(i, int):
                        sp.wait_ge(v_ready, 3 * (b - 1))
                    sp.dma_start(c_in[u][:], ctxT[bass.ds(b, 1)].rearrange("a p k n -> (a p) k n")).then_inc(ctx_arrived[u], 16)

            repeat(sp, B // 2, turn_of)

        @block.gpsimd
        def _(pool):
            for u in range(2):
                nc.gpsimd.memset(v[u][:], 0.0).then_inc(cleared, 1)
            for n in range(BANKS):
                nc.gpsimd.memset(probs[n][:, KV:KVP], 0.0).then_inc(cleared, 1)
            nc.gpsimd.memset(zero_rows[:], 0.0).then_inc(cleared, 1)
            pool.wait_ge(cleared, BANKS + 3)
            for u in range(2):
                nc.gpsimd.memset(v[u][:, :, :, HD:HD + 1], 1.0).then_inc(cleared, 1)
            pool.wait_ge(weights_in, 9 * 16)
            for k in range(whh.shape[1]):
                pool.dma_start(whh[:, k, :], whhT[:, k, :]).then_inc(whh_in, 16)
            pool.wait_ge(bias_ready, 1)

            def store(b):
                pool.wait_ge(x1_ready, b + 1)
                pool.dma_start(x1[bass.ds(b, 1)].rearrange("a s d -> (a s) d"), rows_of(b)).then_inc(stored, 16)

            def mask_queries(b, u):
                pool.wait_ge(q_copied, b + 1)
                nc.gpsimd.tensor_tensor(qT[u][:].rearrange("p h g s -> p h (g s)"),
                                        q_all[:].rearrange("p g s -> p (g s)").unsqueeze(1).to_broadcast([P, HT, KT * S]),
                                        mask_sb[:].unsqueeze(2).to_broadcast([P, HT, KT * S]), ALU.mult).then_inc(q_ready, 1)

            mask_queries(0, 0)

            def turn_of(b, u, first, last):
                pool.wait_ge(xn_ready, b + 1)
                nc.gpsimd.tensor_tensor(rows_of(b), rows_of(b), bo_gated[0:S, :], ALU.add).then_inc(bias_added, 1)
                for dram in to_clear:
                    pool.dma_start(dram[bass.ds(b, 1)].rearrange("a p w -> (a p) w"),
                                   zero_rows[:, 0:dram.shape[2]]).then_inc(cleared_rows, 16)
                if not first:
                    store(b - 1)
                if not last:
                    mask_queries(b + 1, 1 - u)

            pipelined(pool, B, turn_of)
            store(B - 1)
            pool.wait_ge(stored, 16 * B)
            pool.wait_ge(cleared_rows, 16 * B * len(to_clear))

        @block.scalar
        def _(act):
            def exponential(b, u, h):
                act.wait_ge(max_ready, HEADS * b + h + 1)
                at_least(act, t_psum, HEADS * b + h + 1 - BANKS)
                nc.scalar.activation(probs[h % BANKS][:, 0:KV], score[h % BANKS][0:S, 0:KV], ACT.Exp,
                                     bias=neg_max[:, h % BANKS:h % BANKS + 1], scale=-1.0).then_inc(p_ready, 1)

            def keys_out(b, u, g):
                act.wait_ge(k_psum, KT * b + g + 1)
                nc.scalar.activation(kT[u][:, g, :], misc[:, 0:KVP], ACT.Identity, bias=bq_bk[:, 1, g:g + 1]).then_inc(k_ready, 1)

            def xnT_out(b):
                act.wait_ge(xnT_psum, b + 1)
                nc.scalar.copy(xnT[:].rearrange("p k s -> p (k s)"), proj[:, 0:KT * S]).then_inc(xnT_ready, 1)

            def att_out(b):
                act.wait_ge(o_psum, HG * b + HG)
                nc.scalar.copy(att[:].rearrange("p c s -> p (c s)"), outs[:, 0:HG * S]).then_inc(att_ready, 1)

            def attnT_out(b):
                act.wait_ge(attnT_psum, b + 1)
                nc.scalar.copy(attnT[:].rearrange("p k s -> p (k s)"), misc[:, 0:KT * S]).then_inc(attnT_ready, 1)

            act.wait_ge(weights_in, 9 * 16)
            nc.scalar.activation(gate[:, 0:1], gate[:, 0:1], ACT.Tanh).then_inc(gate_ready, 1)
            xnT_out(0)
            for g in range(KT):
                keys_out(0, 0, g)
            act.wait_ge(cleared, BANKS + 5)
            for h in range(AHEAD):
                exponential(0, 0, h)

            def turn_of(b, u, first, last):
                for h in range(HEADS):
                    if h % 2 == 1:
                        act.wait_ge(t_psum, HEADS * b + h + 1)
                        at_least(act, o_psum, HG * b + h // 4 - 1)
                        nc.scalar.copy(probsT[h // 4 % 2][:, h % 4, :], turned[0:KC, 0:3 * S]).then_inc(odd_ready, 1)
                    ahead = ahead_of(b, u, h, last)
                    if ahead:
                        exponential(*ahead)
                    if h == LAST_OUTPUTS and not first:
                        att_out(b - 1)
                    if h == TURN_X and not last:
                        xnT_out(b + 1)
                    if h == TURN_ATTN and not first:
                        attnT_out(b - 1)
                    if h in KEYS and not last:
                        keys_out(b + 1, 1 - u, KEYS.index(h))

            pipelined(act, B, turn_of)
            att_out(B - 1)
            attnT_out(B - 1)

        @block.vector
        def _(dve):
            def normalized(b):
                at_least(dve, xnT_psum, b)
                normalize(nc, xn[:], rows_of(b), mean, rstd, b).then_inc(xn_ready, 1)

            def queries_out(b):
                dve.wait_ge(q_psum, b + 1)
                at_least(dve, q_ready, b)
                nc.vector.tensor_tensor(q_all[:], proj[:, 0:KT * S].rearrange("p (g s) -> p g s", g=KT),
                                        bq_bk[:, 0, :].unsqueeze(2).to_broadcast([P, KT, S]), ALU.add).then_inc(q_copied, 1)

            def values_out(b, u, m):
                dve.wait_ge(v_psum, 3 * b + m + 1)
                at_least(dve, o_psum, HG * b - HG)
                nc.vector.tensor_tensor(v[u][:, m, :, 0:HD], proj[0:KC, 0:DIM].rearrange("p (h d) -> p h d", h=HEADS),
                                        bv_all[0:KC, :].rearrange("p (h d) -> p h d", h=HEADS), ALU.add).then_inc(v_ready, 1)

            def maximum(b, u, h):
                dve.wait_ge(s_psum, HEADS * b + h + 1)
                at_least(dve, p_ready, HEADS * b + h + 1 - BANKS)
                nc.vector.tensor_reduce(neg_max[:, h % BANKS:h % BANKS + 1], score[h % BANKS][0:S, 0:KV], AX.X, ALU.min).then_inc(max_ready, 1)

            def divide(b):
                dve.wait_ge(back_psum, b + 1)
                heads = misc[0:S, :].rearrange("p (h j) -> p h j", h=HEADS)
                nc.vector.reciprocal(inverse[:], heads[:, :, HD]).then_inc(inverse_ready, 1)
                dve.wait_ge(inverse_ready, b + 1)
                nc.vector.tensor_tensor(attn[:], heads[:, :, 0:HD], inverse[:].unsqueeze(2).to_broadcast([S, HEADS, HD]),
                                        ALU.mult).then_inc(attn_ready, 1)

            def add_output(b):
                dve.wait_ge(bias_added, b + 1)
                dve.wait_ge(y_psum, b + 1)
                nc.vector.scalar_tensor_tensor(rows_of(b), proj[0:S, 0:DIM], gate[0:S, 0:1], rows_of(b),
                                               ALU.mult, ALU.add).then_inc(x1_ready, 1)

            normalized(0)
            dve.wait_ge(gate_ready, 1)
            nc.vector.tensor_scalar(bo_gated[:], bo_gated[:], gate[:, 0:1], None, ALU.mult).then_inc(bias_ready, 1)
            dve.wait_ge(cleared, BANKS + 5)
            queries_out(0)
            for m in range(3):
                values_out(0, 0, m)
            for h in range(AHEAD):
                maximum(0, 0, h)

            def turn_of(b, u, first, last):
                for h in range(HEADS):
                    if h % 2 == 0:
                        dve.wait_ge(t_psum, HEADS * b + h + 1)
                        at_least(dve, o_psum, HG * b + h // 4 - 1)
                        nc.vector.tensor_copy(probsT[h // 4 % 2][:, h % 4, :], turned[0:KC, 0:3 * S]).then_inc(even_ready, 1)
                    ahead = ahead_of(b, u, h, last)
                    if ahead:
                        maximum(*ahead)
                    if h == TURN_X - 1 and not last:
                        normalized(b + 1)
                    if h == LAST_VALUES and not first:
                        values_out(b, u, 2)
                    if h == BACK and not first:
                        divide(b - 1)
                    if h in VALUES and not last:
                        values_out(b + 1, 1 - u, VALUES.index(h))
                    if h == OUTPUT and not first:
                        add_output(b - 1)
                    if h == QUERIES and not last:
                        queries_out(b + 1)

            pipelined(dve, B, turn_of)
            divide(B - 1)
            add_output(B - 1)
            dve.wait_ge(x1_ready, B)

        @block.tensor
        def _(pe):
            def turn_x(b):
                pe.wait_ge(xn_ready, b + 1)
                at_least(pe, v_ready, 3 * b)
                for k in range(KT):
                    done = nc.tensor.transpose(proj[:, k * S:(k + 1) * S], xn[:, k * P:(k + 1) * P], ident[0:S, 0:S])
                done.then_inc(xnT_psum, 1)

            def project_keys(b, u, g):
                at_least(pe, k_ready, KT * b + g)
                if g == 1:
                    at_least(pe, attnT_ready, b - 1)
                for k in range(KT):
                    done = nc.tensor.matmul(misc[:, 0:KVP], wk[:, k, g * P:(g + 1) * P], c_in[u][:, k, :],
                                            start=(k == 0), stop=(k == KT - 1))
                done.then_inc(k_psum, 1)

            def project_queries(b):
                pe.wait_ge(xnT_ready, b + 1)
                at_least(pe, x1_ready, b - 1)
                for g in range(KT):
                    for k in range(KT):
                        done = nc.tensor.matmul(proj[:, g * S:(g + 1) * S], wq[:, k, g * P:(g + 1) * P], xnT[:, k, :],
                                                start=(k == 0), stop=(k == KT - 1))
                done.then_inc(q_psum, 1)

            def project_values(b, u, m):
                at_least(pe, q_copied, b + 1)
                at_least(pe, v_ready, 3 * b + m)
                for k in range(KT):
                    done = nc.tensor.matmul(proj[0:KC, 0:DIM], c_in[u][:, k, m * KC:(m + 1) * KC], wv[:, k, :],
                                            start=(k == 0), stop=(k == KT - 1))
                done.then_inc(v_psum, 1)

            def scores(b, u, h):
                if h == 0:
                    pe.wait_ge(q_ready, b + 1)
                    pe.wait_ge(k_ready, KT * (b + 1))
                at_least(pe, p_ready, HEADS * b + h + 1 - BANKS)
                nc.tensor.matmul(score[h % BANKS][0:S, 0:KV], qT[u][:, h % HT, h // HT, :], kT[u][:, h // HT, 0:KV],
                                 start=True, stop=True).then_inc(s_psum, 1)

            def turn_probs(b, h):
                pe.wait_ge(p_ready, HEADS * b + h + 1)
                if h % 2 == 1:
                    pe.wait_ge(even_ready, HEADS // 2 * b + (h + 1) // 2)
                else:
                    at_least(pe, odd_ready, HEADS // 2 * b + h // 2)
                for m in range(3):
                    done = nc.tensor.transpose(turned[0:KC, m * S:(m + 1) * S], probs[h % BANKS][:, m * KC:(m + 1) * KC], ident[0:S, 0:S])
                done.then_inc(t_psum, 1)

            def outputs(b, u, c):
                if c == 0:
                    pe.wait_ge(v_ready, 3 * b + 3)
                    at_least(pe, att_ready, b)
                pe.wait_ge(even_ready, HEADS // 2 * b + 2 * c + 2)
                pe.wait_ge(odd_ready, HEADS // 2 * b + 2 * c + 2)
                for m in range(3):
                    n = KC if m < 2 else KLAST
                    for r in range(4):
                        done = nc.tensor.matmul(outs[32 * r:32 * r + 32, c * S:(c + 1) * S], v[u][0:n, m, 4 * c + r, :],
                                                probsT[c % 2][0:n, r, m * S:(m + 1) * S], start=(m == 0), stop=(m == 2))
                done.then_inc(o_psum, 1)

            def turn_back(b, keys_done):
                pe.wait_ge(att_ready, b + 1)
                pe.wait_ge(k_ready, keys_done)
                for c in range(HG):
                    done = nc.tensor.transpose(misc[0:S, c * P:(c + 1) * P], att[:, c, :], ident[:, :])
                done.then_inc(back_psum, 1)

            def turn_attn(b):
                pe.wait_ge(attn_ready, b + 1)
                for k in range(KT):
                    done = nc.tensor.transpose(misc[:, k * S:(k + 1) * S],
                                               attn[:].rearrange("p h d -> p (h d)")[:, k * P:(k + 1) * P], ident[0:S, 0:S])
                done.then_inc(attnT_psum, 1)

            def project_output(b):
                pe.wait_ge(attnT_ready, b + 1)
                for k in range(KT):
                    done = nc.tensor.matmul(proj[0:S, 0:DIM], attnT[:, k, :], wo[:, k, :], start=(k == 0), stop=(k == KT - 1))
                done.then_inc(y_psum, 1)

            pe.wait_ge(weights_in, 9 * 16)
            turn_x(0)
            pe.wait_ge(ctx_arrived[0], 16)
            project_keys(0, 0, 0)
            project_queries(0)
            project_keys(0, 0, 1)
            for m in range(3):
                project_values(0, 0, m)
            for h in range(AHEAD):
                scores(0, 0, h)

            def turn_of(b, u, first, last):
                for h in range(HEADS):
                    ahead = ahead_of(b, u, h, last)
                    if ahead:
                        scores(*ahead)
                    turn_probs(b, h)
                    if h == LAST_VALUES and not first:
                        project_values(b, u, 2)
                    if h == LAST_OUTPUTS and not first:
                        outputs(b - 1, 1 - u, HG - 1)
                    if h == TURN_X and not last:
                        turn_x(b + 1)
                    if h in KEYS and not last:
                        if h == KEYS[0]:
                            pe.wait_ge(ctx_arrived[1 - u], 8 * (b + 1 - (1 - u)) + 16)
                        project_keys(b + 1, 1 - u, KEYS.index(h))
                    if h == BACK and not first:
                        turn_back(b - 1, KT * (b + 1) + (0 if last else 1))
                    if h == TURN_ATTN and not first:
                        turn_attn(b - 1)
                    if h == OUTPUT and not first:
                        pe.wait_ge(v_ready, 3 * b + 3)
                        if not last:
                            pe.wait_ge(xnT_ready, b + 2)
                        project_output(b - 1)
                    if h in VALUES and not last:
                        project_values(b + 1, 1 - u, VALUES.index(h))
                    if h == QUERIES and not last:
                        project_queries(b + 1)
                    if h in OUTPUTS:
                        outputs(b, u, OUTPUTS[h])

            pipelined(pe, B, turn_of)
            outputs(B - 1, 1, HG - 1)
            turn_back(B - 1, KT * B)
            turn_attn(B - 1)
            project_output(B - 1)
            pe.wait_ge(x1_ready, B)


GD = 1024
EXPERTS, RD = 8, 128
GQ = GD // 4
GC = GD // P
STEPS = 4
TILES = S // STEPS
SHIFTS = ((0, 3), (1, 2), (4, 5, 6, 7))
ROWS = [sum(EXPERTS - s for s in g) for g in SHIFTS] + [2 * EXPERTS]
NSTAT = sum(ROWS)


def gru(nc, whh, whh_in, wihT, hT, wcT, ctx_b, weT, states, stat, ident):
    with ExitStack() as ctx:
        def sb(name, shape, dt=F32):
            return ctx.enter_context(nc.sbuf_tensor("gru_" + name, shape, dt))

        def ps(name):
            return ctx.enter_context(nc.psum_tensor("gru_" + name, [P, 512], F32))

        def sem(name):
            return ctx.enter_context(nc.semaphore("gru_" + name))

        wih = sb("wih", [P, KT, 3 * GD])
        we = sb("we", [P, KT, GD])
        xt = [sb(f"xt{u}", [P, KT, STEPS, B]) for u in range(2)]
        h = [sb(f"state{u}", [P, GQ]) for u in range(2)]
        stateT = [sb(f"stateT{t}", [P, P]) for t in range(2)]
        rz = sb("rz", [P, 2, GQ])
        one_z = sb("one_z", [P, GQ])
        zh = sb("zh", [P, GQ])
        cand = sb("cand", [P, GQ])
        cand_n = sb("cand_n", [P, GQ])
        routed = sb("routed", [P, EXPERTS, RD])
        expr = sb("expr", [P, EXPERTS, RD])
        prod = sb("prod", [P, max(ROWS), RD])
        x_mean = sb("x_mean", [P, KT, B])

        ps_rz, ps_n, ps_x = ps("ps_rz"), ps("ps_n"), ps("ps_x")
        ps_t = [ps("ps_t0"), ps("ps_t1")]
        ps_e = [ps("ps_e0"), ps("ps_e1")]

        small_in, inputs_in = sem("small_in"), sem("inputs_in")
        mean_ready, h0_psum = sem("mean_ready"), sem("h0_psum")
        xt_ready, gates_ready, rz_done, n_done = sem("xt_ready"), sem("gates_ready"), sem("rz_done"), sem("n_done")
        cand_ready, tanh_ready, h_ready = sem("cand_ready"), sem("tanh_ready"), sem("state_ready")
        turned, stateT_ready = sem("state_turned"), [sem("stateT0_ready"), sem("stateT1_ready")]
        stored = [sem("state_stored0"), sem("state_stored1")]
        e_done, e_copied = sem("e_done"), sem("e_copied")
        routed_in, prod_ready, prod_used = sem("routed_in"), sem("prod_ready"), sem("prod_used")
        dve_own = sem("gru_dve_own")

        with ExitStack() as first:
            wc = first.enter_context(nc.sbuf_tensor("wc", [P, KT, GD], F32))
            cb = first.enter_context(nc.sbuf_tensor("cb", [P, GQ], F32))
            block = first.enter_context(nc.Block())

            @block.sync
            def _(sp):
                sp.dma_start(wc[:], wcT).then_inc(small_in, 16)
                for q in range(4):
                    sp.dma_start(cb[32 * q:32 * q + 32, :], ctx_b[q * GQ:(q + 1) * GQ].partition_broadcast(32)).then_inc(small_in, 16)
                sp.dma_start(wih[:], wihT).then_inc(inputs_in, 16)
                sp.dma_start(we[:], weT).then_inc(inputs_in, 16)
                sp.wait_ge(small_in, 5 * 16)
                sp.wait_ge(inputs_in, 2 * 16)

            @block.vector
            def _(dve):
                nc.vector.tensor_reduce(x_mean[:], hT[:], AX.X, ALU.add).then_inc(dve_own, 1)
                dve.wait_ge(dve_own, 1)
                nc.vector.tensor_scalar(x_mean[:], x_mean[:], 1.0 / S, None, ALU.mult).then_inc(mean_ready, 1)
                dve.wait_ge(small_in, 5 * 16)
                dve.wait_ge(h0_psum, 1)
                nc.vector.tensor_tensor(h[0][:], ps_n[:, 0:GQ], cb[:], ALU.add).then_inc(h_ready, 1)
                dve.wait_ge(h_ready, 1)

            @block.tensor
            def _(pe):
                pe.wait_ge(small_in, 5 * 16)
                pe.wait_ge(mean_ready, 1)
                for q in range(4):
                    for k in range(KT):
                        last = nc.tensor.matmul(ps_n[32 * q:32 * q + 32, 0:GQ], x_mean[:, k, :], wc[:, k, q * GQ:(q + 1) * GQ],
                                                start=(k == 0), stop=(k == KT - 1))
                last.then_inc(h0_psum, 1)

        block = ctx.enter_context(nc.Block())

        def quarter(q):
            return slice(32 * q, 32 * q + 32)

        def rz_columns(w, k, q):
            return w[:, k, 0:2 * GD].rearrange("p (g n) -> p g n", g=2)[:, :, q * GQ:(q + 1) * GQ]

        def n_columns(w, k, q):
            return w[:, k, 2 * GD + q * GQ:2 * GD + (q + 1) * GQ]

        @block.sync
        def _(sp):
            def turn_of(it):
                for j in range(STEPS):
                    u = (j + 1) % 2
                    sp.wait_ge(h_ready, STEPS * it + j + 2)
                    sp.dma_start(states[bass.ds(it, 1), j].rearrange("a b (q n) -> (a q) b n", q=4), h[u][:]).then_inc(stored[u], 16)
                for u in range(2):
                    sp.wait_ge(stored[u], 16 * 2 * it + 32)
                sp.wait_ge(prod_ready, 4 * it)
                sp.dma_start(routed[:].rearrange("p e d -> p (e d)"),
                             states[bass.ds(it, 1)].rearrange("a j b n -> (a j b) n")).then_inc(routed_in, 16)

            repeat(sp, TILES, turn_of)

        @block.gpsimd
        def _(pool):
            def take_inputs(it, u):
                nc.gpsimd.tensor_copy(xt[u][:], hT[:, :, :, bass.ds(STEPS * it, STEPS)].rearrange("p k b j -> p k j b")).then_inc(xt_ready, 1)

            def products(it):
                pool.wait_ge(routed_in, 16 * it + 16)
                pool.wait_ge(e_copied, 2 * it + 2)
                groups = [[(routed[:, 0:EXPERTS - s, :], routed[:, s:EXPERTS, :]) for s in g] for g in SHIFTS]
                groups.insert(0, [(expr[:], routed[:]), (expr[:], expr[:])])
                for n, group in enumerate(groups):
                    pool.wait_ge(prod_used, 4 * it + n)
                    row = 0
                    for a, b in group:
                        rows = a.shape[1]
                        last = nc.gpsimd.tensor_tensor(prod[:, row:row + rows, :], a, b, ALU.mult)
                        row += rows
                    last.then_inc(prod_ready, 1)

            take_inputs(0, 0)
            def turn_of(i):
                for u in range(2):
                    it = 2 * i + u
                    pool.wait_ge(gates_ready, 2 * STEPS * it)
                    pool.wait_ge(e_done, STEPS * it)
                    take_inputs(it + 1, 1 - u)
                    products(it)

            repeat(pool, TILES // 2, turn_of)
            products(TILES - 1)
            pool.wait_ge(prod_ready, 4 * TILES)

        def sum_group(dve, it, n):
            at = sum((ROWS[-1:] + ROWS[:-1])[:n])
            rows = (ROWS[-1:] + ROWS[:-1])[n]
            dve.wait_ge(prod_ready, 4 * it + n + 1)
            nc.vector.tensor_reduce(stat[:, bass.ds(it, 1), at:at + rows].rearrange("p a n -> p (a n)"),
                                    prod[:, 0:rows, :], AX.X, ALU.add).then_inc(prod_used, 1)

        @block.vector
        def _(dve):
            def steps(it, first):
                for j in range(STEPS):
                    t = STEPS * it + j
                    old, new = h[j % 2], h[(j + 1) % 2]
                    dve.wait_ge(turned, 2 * t + 1)
                    nc.vector.tensor_copy(stateT[0][:], ps_t[0][:, 0:P]).then_inc(stateT_ready[0], 1)
                    if not first:
                        sum_group(dve, it - 1, j)
                    dve.wait_ge(gates_ready, 2 * t + 1)
                    nc.vector.tensor_tensor(zh[:], rz[:, 1, :], old[:], ALU.mult).then_inc(dve_own, 1)
                    dve.wait_ge(n_done, t + 1)
                    nc.vector.tensor_tensor(cand[:], rz[:, 0, :], ps_n[:, 0:GQ], ALU.mult).then_inc(dve_own, 1)
                    dve.wait_ge(dve_own, 3 * t + 3)
                    nc.vector.tensor_tensor(cand[:], cand[:], ps_x[:, 0:GQ], ALU.add).then_inc(cand_ready, 1)
                    dve.wait_ge(gates_ready, 2 * t + 2)
                    dve.wait_ge(tanh_ready, t + 1)
                    nc.vector.tensor_tensor(cand_n[:], cand_n[:], one_z[:], ALU.mult).then_inc(dve_own, 1)
                    dve.wait_ge(dve_own, 3 * t + 4)
                    dve.wait_ge(stored[(j + 1) % 2], 16 * (2 * it + j // 2))
                    nc.vector.tensor_tensor(new[:], cand_n[:], zh[:], ALU.add).then_inc(h_ready, 1)

            steps(0, True)
            with dve.Fori(1, TILES) as it:
                steps(it, False)
            for n in range(4):
                sum_group(dve, TILES - 1, n)
            dve.wait_ge(prod_used, 4 * TILES)

        @block.scalar
        def _(act):
            def turn_of(it):
                for j in range(STEPS):
                    t = STEPS * it + j
                    act.wait_ge(turned, 2 * t + 2)
                    nc.scalar.copy(stateT[1][:], ps_t[1][:, 0:P]).then_inc(stateT_ready[1], 1)
                    if j >= 2:
                        act.wait_ge(e_done, STEPS * it + 2 * (j - 1))
                        act.wait_ge(prod_ready, 4 * it)
                        nc.scalar.copy(expr[:].rearrange("p e d -> p (e d)")[:, (j - 2) * 512:(j - 1) * 512], ps_e[j - 2][:, :]).then_inc(e_copied, 1)
                    act.wait_ge(rz_done, t + 1)
                    nc.scalar.activation(rz[:].rearrange("p g n -> p (g n)"), ps_rz[:, :], ACT.Sigmoid).then_inc(gates_ready, 1)
                    nc.scalar.activation(one_z[:], ps_rz[:, GQ:2 * GQ], ACT.Sigmoid, scale=-1.0).then_inc(gates_ready, 1)
                    act.wait_ge(cand_ready, t + 1)
                    nc.scalar.activation(cand_n[:], cand[:], ACT.Tanh).then_inc(tanh_ready, 1)

            repeat(act, TILES, turn_of)

        @block.tensor
        def _(pe):
            pe.wait_ge(whh_in, 16 * GC)

            def steps(it, u):
                pe.wait_ge(xt_ready, it + 1)
                for j in range(STEPS):
                    t = STEPS * it + j
                    pe.wait_ge(gates_ready, 2 * t)
                    for k in range(KT):
                        for q in range(4):
                            nc.tensor.matmul(ps_rz[quarter(q), :], xt[u][:, k, j, :], rz_columns(wih, k, q),
                                             start=(k == 0), stop=False)
                    pe.wait_ge(cand_ready, t)
                    for k in range(KT):
                        for q in range(4):
                            nc.tensor.matmul(ps_x[quarter(q), 0:GQ], xt[u][:, k, j, :], n_columns(wih, k, q),
                                             start=(k == 0), stop=(k == KT - 1))
                    pe.wait_ge(h_ready, t + 1)
                    for half in range(2):
                        nc.tensor.transpose(ps_t[half][:, 0:P], h[j % 2][:, half * P:(half + 1) * P], ident[:, :]).then_inc(turned, 1)
                    if j % 2 == 0:
                        pe.wait_ge(e_copied, 2 * it)
                    for k in range(KT):
                        last = nc.tensor.matmul(ps_e[j // 2][:, (j % 2) * GQ:(j % 2 + 1) * GQ], xt[u][:, k, :, :].rearrange("p j b -> p (j b)"),
                                                we[:, k, j * GQ:(j + 1) * GQ], start=(k == 0), stop=(k == KT - 1))
                    last.then_inc(e_done, 1)
                    for half in range(2):
                        pe.wait_ge(stateT_ready[half], t + 1)
                    for c in range(GC):
                        for q in range(4):
                            last = nc.tensor.matmul(ps_rz[quarter(q), :], stateT[c % 2][:, quarter(c // 2)], rz_columns(whh, c, q),
                                                    start=False, stop=(c == GC - 1))
                    last.then_inc(rz_done, 1)
                    for c in range(GC):
                        for q in range(4):
                            last = nc.tensor.matmul(ps_n[quarter(q), 0:GQ], stateT[c % 2][:, quarter(c // 2)], n_columns(whh, c, q),
                                                    start=(c == 0), stop=(c == GC - 1))
                    last.then_inc(n_done, 1)

            def turn_of(i):
                for u in range(2):
                    steps(2 * i + u, u)

            repeat(pe, TILES // 2, turn_of)
            steps(TILES - 1, 0)


FF = 512
TOKENS = B * S
TT = TOKENS // P
SLOT_TILES = (2 * TOKENS + EXPERTS * (P - 1)) // P
MOE_TILES = TT + SLOT_TILES
FC = FF // P
TINY_NORM, TINY_COS = 1e-12, 1e-8
HUGE = 3.0e38


def routing(nc, stat, weight, slot, tile_expert, iota_e, below, ones, g_ffn, gate, gu, guT, dn, dnT, shared_in,
            h_rows, h_all, h_in):
    with ExitStack() as ctx:
        def sb(name, shape, dt=F32):
            return ctx.enter_context(nc.sbuf_tensor("route_" + name, shape, dt))

        def sem(name):
            return ctx.enter_context(nc.semaphore("route_" + name))

        inv = sb("inv", [P, TILES, EXPERTS])
        pair = sb("pair", [P, EXPERTS, TILES, EXPERTS])
        row2_too = sb("row2_too", [P, TILES, EXPERTS])
        row2 = sb("row2", [P, TILES, EXPERTS])
        root = sb("root", [P, TILES, EXPERTS])
        en = sb("en", [P, TILES, EXPERTS])
        score = sb("score", [P, TILES, EXPERTS])
        work = sb("work", [P, TILES, EXPERTS])
        hot = [sb(f"hot{k}", [P, TILES, EXPERTS]) for k in range(2)]
        chosen = sb("chosen", [P, TILES, EXPERTS])
        best = [sb(f"best{k}", [P, TILES]) for k in range(2)]
        index = sb("index", [P, TILES])
        ratio = sb("ratio", [P, TILES])
        share = sb("share", [P, TILES])
        pen = sb("pen", [P, 1])
        total = sb("total", [P, EXPERTS, TILES])
        upto = sb("upto", [P, EXPERTS, TILES])
        zeros = sb("zeros_r", [P, TILES])
        row_of = sb("row_of", [P, TILES, EXPERTS])
        steps_i = sb("steps_i", [P, EXPERTS, TILES], I32)
        steps_f = sb("steps_f", [P, EXPERTS, TILES])
        need = sb("need", [P, EXPERTS])
        end = sb("end", [P, EXPERTS])
        base = sb("base", [P, EXPERTS])
        slot_f = sb("slot_f", [P, TILES])
        tile_i = sb("tile_i", [1, MOE_TILES, EXPERTS], I32)
        tile_f = sb("tile_f", [1, MOE_TILES, EXPERTS])
        tile_e = sb("tile_e", [1, MOE_TILES])
        ps_pen = ctx.enter_context(nc.psum_tensor("ps_pen", [P, 512], F32))
        ps_rank = ctx.enter_context(nc.psum_tensor("ps_rank", [P, 512], F32))
        ps_total = ctx.enter_context(nc.psum_tensor("ps_total", [P, 512], F32))

        own, filled = sem("route_own"), sem("route_filled")
        root_in, root_out, exp_in, exp_out = sem("root_in"), sem("root_out"), sem("exp_in"), sem("exp_out")
        pen_in, pen_out, chosen_ready, ranked = sem("pen_in"), sem("pen_out"), sem("chosen_ready"), sem("ranked")
        gate_in, gate_ready = sem("ffn_gate_in"), sem("ffn_gate_ready")
        block = ctx.enter_context(nc.Block())

        @block.sync
        def _(sp):
            sp.dma_start(gate[:, :], g_ffn.partition_broadcast(P)).then_inc(gate_in, 16)
            sp.dma_start(gu[:, EXPERTS], guT[:, EXPERTS]).then_inc(shared_in, 16)
            sp.dma_start(dn[:, EXPERTS], dnT[:, EXPERTS]).then_inc(shared_in, 16)
            h_view = h_rows.rearrange("b (t j) d -> j b t d", j=STEPS)
            for j in range(STEPS):
                sp.dma_start(h_all[32 * j:32 * j + 32, :, :], h_view[j]).then_inc(h_in, 16)
            sp.wait_ge(gate_in, 16)

        @block.gpsimd
        def _(pool):
            nc.gpsimd.iota(steps_i[:], pattern=[[0, EXPERTS], [P, TILES]], base=0, channel_multiplier=0).then_inc(filled, 1)
            nc.gpsimd.iota(tile_i[:], pattern=[[1, MOE_TILES], [0, EXPERTS]], base=-TT, channel_multiplier=0).then_inc(filled, 1)
            nc.gpsimd.memset(zeros[:], 0.0).then_inc(filled, 1)
            pool.wait_ge(filled, 3)
            nc.gpsimd.tensor_copy(steps_f[:], steps_i[:]).then_inc(filled, 1)
            nc.gpsimd.tensor_copy(tile_f[:], tile_i[:]).then_inc(filled, 1)

        @block.scalar
        def _(act):
            act.wait_ge(gate_in, 16)
            nc.scalar.activation(gate[:, :], gate[:, :], ACT.Tanh).then_inc(gate_ready, 1)
            act.wait_ge(gate_ready, 1)
            for n, (a, b) in enumerate(((inv, stat[:, :, 16:24]), (en, stat[:, :, 8:16]), (root, root), (work, row2))):
                act.wait_ge(root_in, n + 1)
                nc.scalar.activation(a[:], b if n < 2 else b[:], ACT.Sqrt).then_inc(root_out, 1)
            act.wait_ge(exp_in, 1)
            nc.scalar.activation(ratio[:], ratio[:], ACT.Exp).then_inc(exp_out, 1)

        @block.tensor
        def _(pe):
            pe.wait_ge(pen_in, 1)
            nc.tensor.matmul(ps_pen[:, 0:1], ones[:, :], pen[:, :], start=True, stop=True).then_inc(pen_out, 1)
            pe.wait_ge(chosen_ready, 1)
            flat = chosen[:].rearrange("p t e -> p (t e)")
            nc.tensor.matmul(ps_rank[:, 0:TILES * EXPERTS], below[:, :], flat, start=True, stop=True).then_inc(ranked, 1)
            nc.tensor.matmul(ps_total[:, 0:TILES * EXPERTS], ones[:, :], flat, start=True, stop=True).then_inc(ranked, 1)

        @block.vector
        def _(dve):
            v = nc.vector
            chain = Chain(dve, own)

            def every(a):
                return a[:].unsqueeze(2).to_broadcast([P, TILES, EXPERTS])

            v.tensor_copy(pen[:], stat[:, 0, 0:1]).then_inc(root_in, 2)
            dve.wait_ge(root_out, 2)
            chain.step(v.tensor_scalar(inv[:], inv[:], TINY_NORM, None, ALU.max))
            chain.step(v.reciprocal(inv[:], inv[:]))
            chain.step(v.tensor_tensor(root[:], stat[:, :, 16:24], inv[:], ALU.mult))
            chain.step(v.tensor_tensor(root[:], root[:], inv[:], ALU.mult))
            chain.step(v.tensor_scalar(row2[:], root[:], -1.0, None, ALU.add))
            v.tensor_tensor(row2[:], row2[:], row2[:], ALU.mult).then_inc(root_in, 1)
            dve.wait_ge(root_in, 3)
            at, pairs = 2 * EXPERTS, []
            for s in (s for group in SHIFTS for s in group):
                n = EXPERTS - s
                if s:
                    pairs.append((s, n, pair[:, s, :, 0:n], stat[:, :, at:at + n]))
                at += n
            chain.together(*[v.tensor_tensor(p, raw, inv[:, :, 0:n], ALU.mult) for s, n, p, raw in pairs],
                           v.memset(row2_too[:], 0.0))
            chain.together(*[v.tensor_tensor(p, p, inv[:, :, s:EXPERTS], ALU.mult) for s, n, p, raw in pairs])
            chain.together(*[v.tensor_tensor(p, p, p, ALU.mult) for s, n, p, raw in pairs])
            for s, n, p, raw in pairs:
                chain.together(v.tensor_tensor(row2[:, :, 0:n], row2[:, :, 0:n], p, ALU.add),
                               v.tensor_tensor(row2_too[:, :, s:EXPERTS], row2_too[:, :, s:EXPERTS], p, ALU.add))
            chain.step(v.tensor_tensor(row2[:], row2[:], row2_too[:], ALU.add))
            v.tensor_scalar(pen[:], pen[:], 0.0, None, ALU.mult).then_inc(root_in, 1)
            dve.wait_ge(root_out, 3)
            chain.together(v.tensor_scalar(root[:], root[:], TINY_COS, None, ALU.max),
                           v.tensor_scalar(en[:], en[:], TINY_COS, None, ALU.max),
                           v.tensor_tensor(score[:], stat[:, :, 0:EXPERTS], inv[:], ALU.mult))
            chain.step(v.tensor_tensor(en[:], en[:], root[:], ALU.mult))
            chain.step(v.reciprocal(en[:], en[:]))
            chain.step(v.tensor_tensor(score[:], score[:], en[:], ALU.mult))
            chain.step(v.tensor_scalar(score[:], score[:], -1.0, 1.0, ALU.mult, ALU.add))
            dve.wait_ge(root_out, 4)
            chain.step(v.tensor_scalar(work[:], work[:], TINY_NORM, None, ALU.max))
            chain.step(v.reciprocal(work[:], work[:]))
            chain.step(v.tensor_tensor(row2[:], row2[:], work[:], ALU.mult))
            chain.step(v.tensor_tensor(row2[:], row2[:], work[:], ALU.mult))
            v.tensor_reduce(pen[:], row2[:], AX.XY, ALU.add).then_inc(pen_in, 1)
            dve.wait_ge(pen_out, 1)
            chain.step(v.tensor_scalar(pen[:], ps_pen[:, 0:1], 1.0 / TOKENS, 1.0, ALU.mult, ALU.add))
            chain.step(v.tensor_scalar(score[:], score[:], pen[:, 0:1], None, ALU.mult))
            for k in range(2):
                chain.step(v.tensor_reduce(best[k][:], score[:], AX.X, ALU.max))
                chain.step(v.tensor_tensor(work[:], score[:], every(best[k]), ALU.is_lt))
                chain.step(v.scalar_tensor_tensor(work[:], work[:], 2.0 * EXPERTS, iota_e[:], ALU.mult, ALU.add))
                chain.step(v.tensor_reduce(index[:], work[:], AX.X, ALU.min))
                chain.step(v.tensor_tensor(hot[k][:], iota_e[:], every(index), ALU.is_equal))
                if k == 0:
                    chain.step(v.scalar_tensor_tensor(score[:], hot[0][:], -HUGE, score[:], ALU.mult, ALU.add))
            v.tensor_tensor(chosen[:], hot[0][:], hot[1][:], ALU.add).then_inc(chosen_ready, 1)
            v.tensor_tensor(ratio[:], best[1][:], best[0][:], ALU.subtract).then_inc(exp_in, 1)
            dve.wait_ge(exp_out, 1)
            chain.step(v.tensor_scalar(share[:], ratio[:], 1.0, None, ALU.add))
            chain.step(v.reciprocal(weight[:, :, 0], share[:]))
            chain.step(v.tensor_tensor(weight[:, :, 1], weight[:, :, 0], ratio[:], ALU.mult))
            dve.wait_ge(ranked, 2)
            dve.wait_ge(filled, 5)
            chain.step(v.tensor_copy(total[:], ps_total[:, 0:TILES * EXPERTS].rearrange("p (t e) -> p e t", e=EXPERTS)))
            chain.together(*[v.tensor_tensor_scan(upto[:, e, :], zeros[:], total[:, e, :], 0.0, ALU.add, ALU.add)
                             for e in range(EXPERTS)])
            chain.step(v.tensor_tensor(steps_f[:], steps_f[:], upto[:, :, TILES - 1:TILES].to_broadcast([P, EXPERTS, TILES]), ALU.is_lt))
            chain.step(v.tensor_reduce(need[:], steps_f[:], AX.X, ALU.add))
            chain.step(v.tensor_tensor_scan(end[:], zeros[:, 0:EXPERTS], need[:], 0.0, ALU.add, ALU.add))
            chain.step(v.tensor_tensor(base[:], end[:], need[:], ALU.subtract))
            chain.step(v.tensor_scalar(base[:], base[:], float(P), float(TOKENS - 1), ALU.mult, ALU.add))
            chain.step(v.tensor_tensor(upto[:], upto[:], total[:], ALU.subtract))
            chain.step(v.tensor_tensor(upto[:], upto[:], base[:].unsqueeze(2).to_broadcast([P, EXPERTS, TILES]), ALU.add))
            chain.step(v.tensor_tensor(row_of[:], ps_rank[:, 0:TILES * EXPERTS].rearrange("p (t e) -> p t e", e=EXPERTS),
                                       upto[:].rearrange("p e t -> p t e"), ALU.add))
            for k in range(2):
                chain.step(v.tensor_tensor(work[:], hot[k][:], row_of[:], ALU.mult))
                chain.step(v.tensor_reduce(slot_f[:], work[:], AX.X, ALU.add))
                chain.step(v.tensor_copy(slot[:, :, k], slot_f[:]))
            chain.step(v.tensor_tensor(tile_f[:], tile_f[:], end[0:1, :].unsqueeze(1).to_broadcast([1, MOE_TILES, EXPERTS]), ALU.is_ge))
            chain.step(v.tensor_reduce(tile_e[:], tile_f[:], AX.X, ALU.add))
            chain.step(v.tensor_scalar(tile_e[:], tile_e[:], float(EXPERTS - 1), None, ALU.min))
            chain.step(v.memset(tile_e[:, 0:TT], float(EXPERTS)))
            chain.step(v.tensor_copy(tile_expert[:], tile_e[:]))


def expert_tiles(nc, moe_in, moe_out, gu, guT, dn, dnT, tile_expert, shared_in, ident, slot, h_all, h_in):
    with ExitStack() as ctx:
        def sb(name, shape, dt=F32):
            return ctx.enter_context(nc.sbuf_tensor("moe_" + name, shape, dt))

        def ps(name):
            return ctx.enter_context(nc.psum_tensor("moe_" + name, [P, 512], F32))

        def sem(name):
            return ctx.enter_context(nc.semaphore("moe_" + name))

        xs = [sb(f"xs{u}", [P, DIM]) for u in range(2)]
        xT = [sb(f"xT{u}", [P, KT, P]) for u in range(2)]
        act_g = [sb(f"act_g{u}", [P, FF]) for u in range(2)]
        mid = [sb(f"mid{u}", [P, FF]) for u in range(2)]
        midT = sb("midT", [P, FC, P])
        y = [sb(f"y{u}", [P, DIM]) for u in range(2)]
        ps_x, ps_m, ps_y = ps("ps_x"), ps("ps_m"), ps("ps_y")
        ps_g = [ps(f"ps_g{u}") for u in range(2)]
        ps_u = [ps(f"ps_u{u}") for u in range(2)]
        scattered, experts_in = sem("scattered"), sem("experts_in")
        xs_in, x_turned, xT_ready = [sem("xs_in0"), sem("xs_in1")], sem("x_turned"), sem("xT_ready")
        g_done, u_done, act_ready, mid_ready = sem("g_done"), sem("u_done"), sem("act_ready"), sem("mid_ready")
        m_turned, midT_ready, y_done, y_ready = sem("m_turned"), sem("midT_ready"), sem("y_done"), sem("y_ready")
        y_stored = [sem("y_stored0"), sem("y_stored1")]
        block = ctx.enter_context(nc.Block())
        LAST = MOE_TILES - 1
        assert TT % 2 == 1 and MOE_TILES % 2 == 0

        def rows(dram, n):
            return dram.rearrange("(t p) d -> t p d", p=P)[bass.ds(n, 1)].rearrange("a p d -> (a p) d")

        @block.sync
        def _(sp):
            def load(n, u):
                sp.dma_start(xs[u][:], rows(moe_in, n)).then_inc(xs_in[u], 16)

            def store(n, u):
                sp.wait_ge(y_ready, n + 1)
                sp.dma_start(rows(moe_out, n), y[u][:]).then_inc(y_stored[u], 16)

            def turn_of(n, u):
                sp.wait_ge(x_turned, n + 1)
                load(n + 2, u)
                store(n - 1, 1 - u)

            load(0, 0)
            load(1, 1)
            sp.wait_ge(x_turned, 1)
            load(2, 0)
            with sp.Fori(1, EXPERTS + 1) as i:
                turn_of(2 * i - 1, 1)
                e = bass.ds(i - 1, 1)
                sp.dma_start(gu[:, e].rearrange("p a k n -> p (a k n)"), guT[:, e].rearrange("p a k n -> p (a k n)")).then_inc(experts_in, 16)
                sp.dma_start(dn[:, e].rearrange("p a k n -> p (a k n)"), dnT[:, e].rearrange("p a k n -> p (a k n)")).then_inc(experts_in, 16)
                turn_of(2 * i, 0)
            with sp.Fori(EXPERTS + 1, (TT - 1) // 2) as i:
                turn_of(2 * i - 1, 1)
                turn_of(2 * i, 0)
            sp.wait_ge(scattered, 16 * 2 * TILES)
            with sp.Fori((TT - 1) // 2, MOE_TILES // 2 - 1) as i:
                turn_of(2 * i - 1, 1)
                turn_of(2 * i, 0)
            turn_of(LAST - 2, 1)
            store(LAST - 2, 1)
            store(LAST - 1, 0)
            store(LAST, 1)
            for u in range(2):
                sp.wait_ge(y_stored[u], 16 * (MOE_TILES // 2))

        @block.gpsimd
        def _(pool):
            pool.wait_ge(h_in, 16 * STEPS)
            for it in range(TILES):
                for k in range(2):
                    nc.gpsimd.indirect_dma_start(moe_in, bass.IndirectOffsetOnAxis(ap=slot[:, it, k:k + 1], axis=0),
                                                 h_all[:, it, :], None).then_inc(scattered, 16)
            pool.wait_ge(scattered, 16 * 2 * TILES)

        @block.scalar
        def _(act):
            def take_x(n, u):
                act.wait_ge(x_turned, n + 1)
                nc.scalar.copy(xT[u][:].rearrange("p k n -> p (k n)"), ps_x[:, 0:KT * P]).then_inc(xT_ready, 1)

            def take_y(n, u, first):
                act.wait_ge(y_done, n + 1)
                if not first:
                    act.wait_ge(y_stored[u], 8 * (n - u))
                nc.scalar.copy(y[u][:], ps_y[:, 0:DIM]).then_inc(y_ready, 1)

            def gate_of(n, u):
                act.wait_ge(g_done, n + 1)
                nc.scalar.activation(act_g[u][:], ps_g[u][:, :], ACT.Silu).then_inc(act_ready, 1)

            take_x(0, 0)
            gate_of(0, 0)
            take_x(1, 1)
            gate_of(1, 1)
            take_x(2, 0)
            take_y(0, 0, True)
            gate_of(2, 0)
            take_x(3, 1)
            take_y(1, 1, True)

            def turn_of(n, u):
                act.wait_ge(mid_ready, n - 1)
                gate_of(n, u)
                take_x(n + 1, 1 - u)
                take_y(n - 1, 1 - u, False)

            with act.Fori(2, MOE_TILES // 2) as i:
                turn_of(2 * i - 1, 1)
                turn_of(2 * i, 0)
            act.wait_ge(mid_ready, LAST - 1)
            gate_of(LAST, 1)
            take_y(LAST - 1, 0, False)
            take_y(LAST, 1, False)

        @block.vector
        def _(dve):
            def take_mid(n):
                dve.wait_ge(m_turned, n + 1)
                nc.vector.tensor_copy(midT[:].rearrange("p k n -> p (k n)"), ps_m[:, :]).then_inc(midT_ready, 1)

            def product(n, u):
                dve.wait_ge(act_ready, n + 1)
                dve.wait_ge(u_done, n + 1)
                nc.vector.tensor_tensor(mid[u][:], act_g[u][:], ps_u[u][:, :], ALU.mult).then_inc(mid_ready, 1)

            def turn_of(n, u, first, last):
                if not first:
                    take_mid(n - 1)
                product(n, u)

            pipelined(dve, MOE_TILES, turn_of)
            take_mid(LAST)

        @block.tensor
        def _(pe):
            def expert_of(n):
                return nc.tensor.value_load(tile_expert[0:1, bass.ds(n, 1)], min_val=0, max_val=EXPERTS)

            def turn_x(n, u, count):
                pe.wait_ge(xs_in[u], count)
                pe.wait_ge(xT_ready, n)
                for k in range(KT):
                    done = nc.tensor.transpose(ps_x[:, k * P:(k + 1) * P], xs[u][:, k * P:(k + 1) * P], ident[:, :])
                done.then_inc(x_turned, 1)

            def up(psum, half, e, u):
                for k in range(KT):
                    done = nc.tensor.matmul(psum[:, :], xT[u][:, k, :],
                                            gu[:, bass.ds(e, 1), k, half * FF:(half + 1) * FF].rearrange("p a n -> p (a n)"),
                                            start=(k == 0), stop=(k == KT - 1))
                return done

            def turn_mid(n, u):
                pe.wait_ge(mid_ready, n + 1)
                for c in range(FC):
                    done = nc.tensor.transpose(ps_m[:, c * P:(c + 1) * P], mid[u][:, c * P:(c + 1) * P], ident[:, :])
                done.then_inc(m_turned, 1)

            def down(n, e):
                pe.wait_ge(midT_ready, n + 1)
                for c in range(FC):
                    done = nc.tensor.matmul(ps_y[:, 0:DIM], midT[:, c, :],
                                            dn[:, bass.ds(e, 1), c, :].rearrange("p a n -> p (a n)"),
                                            start=(c == 0), stop=(c == FC - 1))
                done.then_inc(y_done, 1)

            def turn_of(n, u, e_before, e, first=False, last=False):
                pe.wait_ge(xT_ready, n + 1)
                if not first:
                    pe.wait_ge(act_ready, n)
                up(ps_g[u], 0, e, u).then_inc(g_done, 1)
                if not first:
                    turn_mid(n - 1, 1 - u)
                up(ps_u[u], 1, e, u).then_inc(u_done, 1)
                if not last:
                    turn_x(n + 1, 1 - u, 8 * (n + 1 - (1 - u)) + 16)
                if not first:
                    if not isinstance(n, int) or n > 1:
                        pe.wait_ge(y_ready, n - 1)
                    down(n - 1, e_before)

            def two_tiles(i):
                before, here, after = expert_of(2 * i - 2), expert_of(2 * i - 1), expert_of(2 * i)
                turn_of(2 * i - 1, 1, before, here)
                turn_of(2 * i, 0, here, after)

            pe.wait_ge(shared_in, 2 * 16)
            turn_x(0, 0, 16)
            turn_of(0, 0, None, EXPERTS, first=True)
            two_tiles(1)
            with pe.Fori(2, (TT + 1) // 2) as i:
                two_tiles(i)
            pe.wait_ge(experts_in, 16 * 2 * EXPERTS)
            with pe.Fori((TT + 1) // 2, MOE_TILES // 2) as i:
                two_tiles(i)
            before, here = expert_of(LAST - 1), expert_of(LAST)
            turn_of(LAST, 1, before, here, last=True)
            turn_mid(LAST, 1)
            pe.wait_ge(y_ready, LAST)
            down(LAST, here)


def combine(nc, moe_out, x1, weight, slot, gate, x2):
    with ExitStack() as ctx:
        def sb(name, shape, dt=F32):
            return ctx.enter_context(nc.sbuf_tensor("mix_" + name, shape, dt))

        def sem(name):
            return ctx.enter_context(nc.semaphore("mix_" + name))

        N = 5
        GROUPS = TILES // N
        pair = [[sb(f"pair{k}_{u}", [P, N, DIM]) for k in range(2)] for u in range(2)]
        shared = [sb(f"shared{u}", [P, N, DIM]) for u in range(2)]
        x = [sb(f"x_c{u}", [P, N, DIM]) for u in range(2)]
        rows_in = [sem(f"rows_in{u}") for u in range(2)]
        pair_in = [sem(f"pair_in{t}") for t in range(2 * N)]
        own, x2_ready = sem("combine_own"), sem("x2_ready")
        x2_stored = [sem(f"x2_stored{u}") for u in range(2)]
        block = ctx.enter_context(nc.Block())

        def group_of(dram, g, j):
            return dram.rearrange("b (g t j) d -> g j b t d", g=GROUPS, j=STEPS)[g, j]

        shared_rows = moe_out[0:TOKENS].rearrange("(b s) d -> b s d", b=B)

        @block.sync
        def _(sp):
            for g in range(GROUPS):
                u = g % 2
                if g >= 2:
                    sp.wait_ge(x2_stored[u], 16 * STEPS * (g // 2))
                for j in range(STEPS):
                    sp.dma_start(x[u][32 * j:32 * j + 32], group_of(x1, g, j)).then_inc(rows_in[u], 16)
                    sp.dma_start(shared[u][32 * j:32 * j + 32], group_of(shared_rows, g, j)).then_inc(rows_in[u], 16)

        @block.gpsimd
        def _(pool):
            for it in range(TILES):
                g, t = divmod(it, N)
                if g >= 2:
                    pool.wait_ge(x2_ready, it - 2 * N + 1)
                for k in range(2):
                    nc.gpsimd.indirect_dma_start(pair[g % 2][k][:, t, :], None, moe_out,
                                                 bass.IndirectOffsetOnAxis(ap=slot[:, it, k:k + 1], axis=0)).then_inc(pair_in[it % (2 * N)], 16)

        @block.vector
        def _(dve):
            chain = Chain(dve, own)
            for it in range(TILES):
                g, t = divmod(it, N)
                u = g % 2
                if t == 0:
                    dve.wait_ge(rows_in[u], 16 * 2 * STEPS * (g // 2 + 1))
                dve.wait_ge(pair_in[it % (2 * N)], 32 * (it // (2 * N) + 1))
                for k in range(2):
                    chain.step(nc.vector.scalar_tensor_tensor(shared[u][:, t, :], pair[u][k][:, t, :], weight[:, it, k:k + 1],
                                                              shared[u][:, t, :], ALU.mult, ALU.add))
                nc.vector.scalar_tensor_tensor(x[u][:, t, :], shared[u][:, t, :], gate[:, 0:1], x[u][:, t, :],
                                               ALU.mult, ALU.add).then_inc(x2_ready, 1)

        @block.scalar
        def _(act):
            for g in range(GROUPS):
                u = g % 2
                act.wait_ge(x2_ready, N * g + N)
                for j in range(STEPS):
                    act.dma_start(group_of(x2, g, j), x[u][32 * j:32 * j + 32]).then_inc(x2_stored[u], 16)
            for u in range(2):
                act.wait_ge(x2_stored[u], 16 * STEPS * len(range(u, GROUPS, 2)))


BANDS = 4
BAND = -(-KV // BANDS)
LAST_BAND = KV - (BANDS - 1) * BAND
DSTEPS = S + BANDS - 1
FAR = 1.0e30


def band(r):
    return slice(B * r, B * r + B)


def distances(nc, rows, mean, rstd, ctxT, table, ones, ident):
    AT_ONCE = 4
    with ExitStack() as ctx:
        def sb(name, shape, dt=F32):
            return ctx.enter_context(nc.sbuf_tensor("dist_" + name, shape, dt))

        def sem(name):
            return ctx.enter_context(nc.semaphore("dist_" + name))

        c_in = [sb(f"d_ctx{u}", [P, KT, KVP]) for u in range(AT_ONCE)]
        square = [sb(f"d_square{u}", [P, KT, KV]) for u in range(AT_ONCE)]
        xn = [sb(f"d_xn{u}", [S, DIM]) for u in range(AT_ONCE)]
        xx = [sb(f"d_xx{u}", [S, DIM]) for u in range(AT_ONCE)]
        norm = [sb(f"d_norm{u}", [S, 1]) for u in range(AT_ONCE)]
        xT = [sb(f"d_xT{u}", [P, KT, S]) for u in range(AT_ONCE)]
        dist = [sb(f"d_dist{u}", [S, KV]) for u in range(AT_ONCE)]
        ps_x = [ctx.enter_context(nc.psum_tensor(f"d_ps_x{u}", [P, 512], F32)) for u in range(AT_ONCE)]
        ps_d = [ctx.enter_context(nc.psum_tensor(f"d_ps_d{u}", [P, 512], F32)) for u in range(AT_ONCE)]
        ctx_in = [sem(f"d_ctx_in{u}") for u in range(AT_ONCE)]
        squared, xn_ready, turned, xT_ready = sem("d_squared"), sem("d_xn_ready"), sem("d_turned"), sem("d_xT_ready")
        norm_ready, summed, square_ready, dist_ready = sem("d_norm_ready"), sem("d_summed"), sem("d_square_ready"), sem("d_dist_ready")
        placed = [sem(f"d_placed{u}") for u in range(AT_ONCE)]
        cleared = sem("d_cleared")
        block = ctx.enter_context(nc.Block())

        @block.sync
        def _(sp):
            for b in range(B + AT_ONCE):
                before = b - AT_ONCE
                u = b % AT_ONCE
                if b < B:
                    if before >= 0:
                        sp.wait_ge(summed, before + 1)
                        sp.wait_ge(squared, before + 1)
                    sp.dma_start(c_in[u][:], ctxT[b]).then_inc(ctx_in[u], 16)
                if before >= 0:
                    if before == 0:
                        sp.wait_ge(cleared, 3)
                    sp.wait_ge(dist_ready, before + 1)
                    for r in range(BANDS):
                        n = BAND if r < BANDS - 1 else LAST_BAND
                        sp.dma_start(table[B * r + before:B * r + before + 1, r:r + S, 0:n],
                                     dist[u][:, r * BAND:r * BAND + n]).then_inc(placed[u], 16)
            for u in range(AT_ONCE):
                sp.wait_ge(placed[u], 16 * BANDS * (B // AT_ONCE))

        @block.gpsimd
        def _(pool):
            def turn_of(i):
                for u in range(AT_ONCE):
                    pool.wait_ge(ctx_in[u], 16 * i + 16)
                    reused(pool, summed, i, u, AT_ONCE)
                    nc.gpsimd.tensor_tensor(square[u][:], c_in[u][:, :, 0:KV], c_in[u][:, :, 0:KV], ALU.mult).then_inc(squared, 1)

            turn_of(0)
            nc.gpsimd.memset(table[:, 0:BANDS - 1, :], FAR).then_inc(cleared, 1)
            nc.gpsimd.memset(table[:, S:DSTEPS, :], FAR).then_inc(cleared, 1)
            nc.gpsimd.memset(table[:, BANDS - 1:S, LAST_BAND:BAND], FAR).then_inc(cleared, 1)
            with pool.Fori(1, B // AT_ONCE) as i:
                turn_of(i)

        @block.vector
        def _(dve):
            def turn_of(i):
                for u in range(AT_ONCE):
                    b = AT_ONCE * i + u
                    reused(dve, turned, i, u, AT_ONCE)
                    reused(dve, norm_ready, i, u, AT_ONCE)
                    normalize(nc, xn[u][:], rows[:, bass.ds(b, 1), :].rearrange("p a n -> p (a n)"), mean, rstd, b).then_inc(xn_ready, 1)
                for u in range(AT_ONCE):
                    b = AT_ONCE * i + u
                    dve.wait_ge(turned, b + 1)
                    nc.vector.tensor_scalar(xT[u][:].rearrange("p k s -> p (k s)"), ps_x[u][:, 0:KT * S], -2.0, None, ALU.mult).then_inc(xT_ready, 1)
                for u in range(AT_ONCE):
                    b = AT_ONCE * i + u
                    dve.wait_ge(summed, b + 1)
                    dve.wait_ge(norm_ready, b + 1)
                    dve.wait_ge(placed[u], 16 * BANDS * i)
                    nc.vector.tensor_scalar(dist[u][:], ps_d[u][0:S, 0:KV], norm[u][:, 0:1], 0.0, ALU.add, ALU.max).then_inc(square_ready, 1)

            repeat(dve, B // AT_ONCE, turn_of)

        @block.scalar
        def _(act):
            def turn_of(i):
                for u in range(AT_ONCE):
                    b = AT_ONCE * i + u
                    act.wait_ge(xn_ready, b + 1)
                    reused(act, square_ready, i, u, AT_ONCE)
                    nc.scalar.activation(xx[u][:], xn[u][:], ACT.Square, accum_out=norm[u][:, 0:1]).then_inc(norm_ready, 1)
                for u in range(AT_ONCE):
                    b = AT_ONCE * i + u
                    act.wait_ge(square_ready, b + 1)
                    nc.scalar.activation(dist[u][:], dist[u][:], ACT.Sqrt).then_inc(dist_ready, 1)

            repeat(act, B // AT_ONCE, turn_of)

        @block.tensor
        def _(pe):
            def turn_of(i):
                for u in range(AT_ONCE):
                    b = AT_ONCE * i + u
                    pe.wait_ge(xn_ready, b + 1)
                    reused(pe, xT_ready, i, u, AT_ONCE)
                    for k in range(KT):
                        last = nc.tensor.transpose(ps_x[u][:, k * S:(k + 1) * S], xn[u][:, k * P:(k + 1) * P], ident[0:S, 0:S])
                    last.then_inc(turned, 1)
                for u in range(AT_ONCE):
                    b = AT_ONCE * i + u
                    pe.wait_ge(squared, b + 1)
                    reused(pe, square_ready, i, u, AT_ONCE)
                    for k in range(KT):
                        nc.tensor.matmul(ps_d[u][0:S, 0:KV], ones[:, 0:S], square[u][:, k, :], start=(k == 0), stop=False)
                    pe.wait_ge(xT_ready, b + 1)
                    pe.wait_ge(ctx_in[u], 16 * i + 16)
                    for k in range(KT):
                        last = nc.tensor.matmul(ps_d[u][0:S, 0:KV], xT[u][:, k, :], c_in[u][:, k, 0:KV], start=False, stop=(k == KT - 1))
                    last.then_inc(summed, 1)

            repeat(pe, B // AT_ONCE, turn_of)


def align(nc, table, on_path, ident):
    with ExitStack() as ctx:
        def sb(name, shape, dt=F32):
            return ctx.enter_context(nc.sbuf_tensor("align_" + name, shape, dt))

        def sem(name):
            return ctx.enter_context(nc.semaphore("align_" + name))

        cost = sb("cost", [P, DSTEPS + 2, BAND + 1])
        least = sb("least", [P, BAND])
        back = sb("back", [P, 2, DSTEPS + 1, BAND + 1], BF16)
        up = sb("up", [P, DSTEPS + 1, BAND + 1], BF16)
        path_words = (DSTEPS + 1) * (BAND + 1)
        path = table[:].rearrange("p s n -> p (s n)").bitcast(BF16)[:, 0:path_words].rearrange("p (s n) -> p s n", n=BAND + 1)
        moved = sb("moved", [P, 2, BAND + 1], BF16)
        entry = sb("entry", [P, BAND], BF16)
        ident16 = sb("ident16", [P, P], BF16)
        ps_p = [ctx.enter_context(nc.psum_tensor(f"ps_p{u}", [P, 512], BF16)) for u in range(2)]
        set_up, own, edge = sem("a_set_up"), sem("align_own"), sem("align_edge")
        path_ready, path_turned, path_kept = sem("path_ready"), sem("path_turned"), sem("path_kept")
        block = ctx.enter_context(nc.Block())

        @block.gpsimd
        def _(pool):
            nc.gpsimd.memset(cost[:, 0:1, :], FAR).then_inc(set_up, 1)
            nc.gpsimd.memset(cost[:, 1:, 0:1], FAR).then_inc(set_up, 1)
            nc.gpsimd.memset(back[:, 0, 0:1, :], 0.0).then_inc(set_up, 1)
            nc.gpsimd.memset(back[:, 1, 0:1, :], 1.0).then_inc(set_up, 1)
            nc.gpsimd.memset(back[:, :, 1:, 0:1], 0.0).then_inc(set_up, 1)
            nc.gpsimd.memset(up[:, :, 0:1], 0.0).then_inc(set_up, 1)
            nc.gpsimd.tensor_copy(ident16[:], ident[:]).then_inc(set_up, 1)
            pool.wait_ge(set_up, 1)
            nc.gpsimd.memset(cost[0:B, 0:1, 0:1], 0.0).then_inc(set_up, 1)

        @block.vector
        def _(dve):
            v = nc.vector
            dve.wait_ge(set_up, 8)
            OWN, EDGE = 2, BANDS - 1

            def least_of(s):
                here = cost[:, s, :]
                v.tensor_tensor(least[:], here[:, 0:BAND], here[:, 1:BAND + 1], ALU.min).then_inc(own, 1)

            least_of(0)
            for s in range(DSTEPS):
                after = cost[:, s + 1, :]
                dve.wait_ge(own, OWN * s + 1)
                at_least(dve, edge, EDGE * s)
                v.tensor_tensor_scan(after[:, 1:BAND + 1], least[:], table[:, s, :], after[:, 0:1], ALU.min, ALU.add).then_inc(own, 1)
                dve.wait_ge(own, OWN * s + 2)
                if s + 1 < DSTEPS:
                    least_of(s + 1)
                for r in range(1, BANDS):
                    v.tensor_copy(cost[band(r), s + 2, 0:1], after[band(r - 1), BAND:BAND + 1]).then_inc(edge, 1)
            dve.wait_ge(edge, EDGE * DSTEPS)
            chain = Chain(dve, own, OWN * DSTEPS)
            before, at = cost[:, 0:DSTEPS, :], cost[:, 1:DSTEPS + 1, :]
            diagonal, above, left = before[:, :, 0:BAND], at[:, :, 0:BAND], before[:, :, 1:BAND + 1]
            is_diagonal, is_left, is_up = (m[:, 1:DSTEPS + 1, 1:BAND + 1][:, ::-1, ::-1] for m in (back[:, 0], back[:, 1], up))
            chain.step(v.tensor_tensor(table[:], above, left, ALU.min))
            chain.step(v.tensor_tensor(is_diagonal, diagonal, table[:], ALU.is_le))
            chain.step(v.tensor_tensor(is_up, above, left, ALU.is_le))
            chain.step(v.tensor_tensor(is_up, is_up, is_diagonal, ALU.is_gt))
            chain.step(v.tensor_tensor(is_left, is_up, is_diagonal, ALU.is_equal))
            for r in range(BANDS - 1):
                chain.step(v.tensor_copy(back[band(r), 0, 2:DSTEPS + 1, 0:1], back[band(r + 1), 0, 1:DSTEPS, BAND:BAND + 1]))
                chain.step(v.tensor_copy(up[band(r), 2:DSTEPS + 1, 0:1], up[band(r + 1), 1:DSTEPS, BAND:BAND + 1]))
            chain.step(v.memset(path[:, :, 0:1], 0.0))
            chain.step(v.memset(path[:, 0:1, :], 0.0))
            chain.step(v.memset(path[band(BANDS - 1), 0:1, BAND - LAST_BAND + 1:BAND - LAST_BAND + 2], 1.0))
            own_before = OWN * DSTEPS + 8 + 2 * (BANDS - 1)

            def move(n):
                v.tensor_tensor(moved[:], path[:, n:n + 1, :].to_broadcast([P, 2, BAND + 1]), back[:, :, n, :], ALU.mult).then_inc(own, 1)

            move(0)
            for n in range(DSTEPS):
                here = path[:, n + 1, :]
                dve.wait_ge(own, own_before + OWN * n + 1)
                v.tensor_tensor(entry[:], moved[:, 0, 0:BAND], moved[:, 1, 1:BAND + 1], ALU.add).then_inc(own, 1)
                dve.wait_ge(own, own_before + OWN * n + 2)
                dve.wait_ge(edge, EDGE * (n + DSTEPS))
                v.tensor_tensor_scan(here[:, 1:BAND + 1], up[:, n + 1, 0:BAND], entry[:], here[:, 0:1], ALU.mult, ALU.add).then_inc(path_ready, 1)
                dve.wait_ge(path_ready, n + 1)
                if n + 1 < DSTEPS:
                    move(n + 1)
                    for r in range(BANDS - 1):
                        v.tensor_copy(path[band(r), n + 2, 0:1], here[band(r + 1), BAND:BAND + 1]).then_inc(edge, 1)

        @block.tensor
        def _(pe):
            pe.wait_ge(set_up, 8)

            def turn_of(i):
                for u in range(2):
                    n = 2 * i + u
                    pe.wait_ge(path_ready, n + 1)
                    reused(pe, path_kept, i, u, 2)
                    nc.tensor.matmul(ps_p[u][0:BAND, 0:P], path[:, bass.ds(n + 1, 1), 1:BAND + 1].rearrange("p a n -> p (a n)"),
                                     ident16[:, :], is_transpose=True, start=True, stop=True).then_inc(path_turned, 1)

            repeat(pe, DSTEPS // 2, turn_of)
            pe.wait_ge(path_ready, DSTEPS)
            pe.wait_ge(path_kept, DSTEPS - 1)
            nc.tensor.transpose(ps_p[0][0:BAND, 0:P], path[:, DSTEPS, 1:BAND + 1], ident16[:, :]).then_inc(path_turned, 1)

        @block.scalar
        def _(act):
            def turn_of(i):
                for u in range(2):
                    n = 2 * i + u
                    act.wait_ge(path_turned, n + 1)
                    nc.scalar.copy(on_path[:, bass.ds(DSTEPS - 1 - n, 1), :].rearrange("p a n -> p (a n)"), ps_p[u][0:BAND, 0:P]).then_inc(path_kept, 1)

            repeat(act, DSTEPS // 2, turn_of)
            act.wait_ge(path_turned, DSTEPS)
            nc.scalar.copy(on_path[:, 0, :], ps_p[0][0:BAND, 0:P]).then_inc(path_kept, 1)
            act.wait_ge(path_kept, DSTEPS)


def add_aligned(nc, rows, ctx_rows, on_path, g_xattn, gate):
    AHEAD = 4
    with ExitStack() as ctx:
        def sb(name, shape, dt=F32):
            return ctx.enter_context(nc.sbuf_tensor("add_" + name, shape, dt))

        def sem(name):
            return ctx.enter_context(nc.semaphore("add_" + name))

        c_rows = [sb(f"e_ctx{u}", [P, BANDS, DIM]) for u in range(AHEAD)]
        pick = [sb(f"pick{u}", [P, BANDS, S]) for u in range(AHEAD)]
        ps_e = [ctx.enter_context(nc.psum_tensor(f"e_ps{u}", [P, 512], F32)) for u in range(AHEAD)]
        ctx_in = [sem(f"e_ctx_in{u}") for u in range(AHEAD)]
        padded = sem("e_padded")
        gate_in, gate_ready, pick_ready, summed, added = sem("e_gate_in"), sem("e_gate_ready"), sem("pick_ready"), sem("e_summed"), sem("e_added")
        block = ctx.enter_context(nc.Block())

        @block.gpsimd
        def _(pool):
            for u in range(AHEAD):
                nc.gpsimd.memset(c_rows[u][:], 0.0).then_inc(padded, 1)
                nc.gpsimd.memset(pick[u][:], 0.0).then_inc(padded, 1)

        @block.sync
        def _(sp):
            sp.dma_start(gate[:, :], g_xattn.partition_broadcast(P)).then_inc(gate_in, 16)
            sp.wait_ge(padded, 2 * AHEAD)
            def turn_of(i):
                for u in range(AHEAD):
                    b = AHEAD * i + u
                    if not isinstance(i, int):
                        sp.wait_ge(summed, b - AHEAD + 1)
                    sp.dma_start(c_rows[u][0:BAND], ctx_rows[bass.ds(b, 1)].rearrange("a n r d -> (a n) r d")).then_inc(ctx_in[u], 16)

            repeat(sp, B // AHEAD, turn_of)

        @block.scalar
        def _(act):
            act.wait_ge(gate_in, 16)
            nc.scalar.activation(gate[:, :], gate[:, :], ACT.Tanh).then_inc(gate_ready, 1)
            act.wait_ge(padded, 2 * AHEAD)
            def turn_of(i):
                for u in range(AHEAD):
                    b = AHEAD * i + u
                    if not isinstance(i, int):
                        act.wait_ge(summed, b - AHEAD + 1)
                    for r in range(BANDS):
                        nc.scalar.copy(pick[u][0:BAND, r, :], on_path[:, r:r + S, bass.ds(B * r + b, 1)].rearrange("p s a -> p (s a)")).then_inc(pick_ready, 1)

            repeat(act, B // AHEAD, turn_of)

        @block.tensor
        def _(pe):
            def turn_of(i):
                for u in range(AHEAD):
                    b = AHEAD * i + u
                    pe.wait_ge(pick_ready, BANDS * b + BANDS)
                    pe.wait_ge(ctx_in[u], 16 * i + 16)
                    if not isinstance(i, int):
                        pe.wait_ge(added, b - AHEAD + 1)
                    for r in range(BANDS):
                        last = nc.tensor.matmul(ps_e[u][0:S, 0:DIM], pick[u][:, r, :], c_rows[u][:, r, :],
                                                start=(r == 0), stop=(r == BANDS - 1))
                    last.then_inc(summed, 1)

            repeat(pe, B // AHEAD, turn_of)

        @block.vector
        def _(dve):
            dve.wait_ge(gate_ready, 1)
            def turn_of(i):
                for u in range(AHEAD):
                    b = AHEAD * i + u
                    dve.wait_ge(summed, b + 1)
                    x_b = rows[:, bass.ds(b, 1), :].rearrange("p a n -> p (a n)")
                    nc.vector.scalar_tensor_tensor(x_b, ps_e[u][0:S, 0:DIM], gate[0:S, 1:2], x_b, ALU.mult, ALU.add).then_inc(added, 1)

            repeat(dve, B // AHEAD, turn_of)
            dve.wait_ge(added, B)


F2 = 1024
F2C = F2 // P
CAPACITY = TOKENS // EXPERTS
CT = CAPACITY // S


def route_once(nc, rows, mean, rstd, router, below, ones, ident, iota_s, xn_all, slot_put, slot_get, keep_gate, gate):
    AT_ONCE = 4
    with ExitStack() as ctx:
        def sb(name, shape, dt=F32):
            return ctx.enter_context(nc.sbuf_tensor("once_" + name, shape, dt))

        def sem(name):
            return ctx.enter_context(nc.semaphore("once_" + name))

        x_now = [sb(f"r_x{u}", [S, DIM]) for u in range(AT_ONCE)]
        kept = sem("r_kept")
        wr = sb("wr", [P, KT, EXPERTS])
        xT = [sb(f"r_xT{u}", [P, KT, S]) for u in range(AT_ONCE)]
        logit = sb("logit", [S, B, EXPERTS])
        work = sb("r_work", [S, B, EXPERTS])
        hot = sb("r_hot", [S, B, EXPERTS])
        best = sb("r_best", [S, B])
        index = sb("r_index", [S, B])
        total = sb("r_total", [S, EXPERTS, B])
        upto = sb("r_upto", [S, EXPERTS, B])
        zeros = sb("r_zeros", [S, B])
        place = sb("r_place", [S, B])
        inside = sb("r_inside", [S, B])
        beyond = sb("r_beyond", [S, B])
        token_i = sb("token_i", [S, B], I32)
        token = sb("token", [S, B])
        ps_x = [ctx.enter_context(nc.psum_tensor(f"r_ps_x{u}", [P, 512], F32)) for u in range(AT_ONCE)]
        ps_l = ctx.enter_context(nc.psum_tensor("r_ps_l", [P, 512], F32))
        ps_rank = ctx.enter_context(nc.psum_tensor("r_ps_rank", [P, 512], F32))
        ps_total = ctx.enter_context(nc.psum_tensor("r_ps_total", [P, 512], F32))
        router_in, filled = sem("router_in"), sem("r_filled")
        xn_ready, turned, xT_ready, scored = sem("r_xn_ready"), sem("r_turned"), sem("r_xT_ready"), sem("scored")
        exp_in, exp_out, hot_ready, ranked, own = sem("r_exp_in"), sem("r_exp_out"), sem("r_hot_ready"), sem("r_ranked"), sem("r_own")
        block = ctx.enter_context(nc.Block())

        @block.sync
        def _(sp):
            sp.dma_start(wr[:], router).then_inc(router_in, 16)
            sp.wait_ge(router_in, 16)

        @block.gpsimd
        def _(pool):
            nc.gpsimd.iota(token_i[:], pattern=[[S, B]], base=TOKENS, channel_multiplier=1).then_inc(filled, 1)
            nc.gpsimd.memset(zeros[:], 0.0).then_inc(filled, 1)
            pool.wait_ge(filled, 2)
            nc.gpsimd.tensor_copy(token[:], token_i[:]).then_inc(filled, 1)

        @block.tensor
        def _(pe):
            pe.wait_ge(router_in, 16)
            def turn_of(i):
                for u in range(AT_ONCE):
                    b = AT_ONCE * i + u
                    pe.wait_ge(xn_ready, b + 1)
                    reused(pe, xT_ready, i, u, AT_ONCE)
                    for k in range(KT):
                        last = nc.tensor.transpose(ps_x[u][:, k * S:(k + 1) * S], x_now[u][:, k * P:(k + 1) * P], ident[0:S, 0:S])
                    last.then_inc(turned, 1)
                for u in range(AT_ONCE):
                    b = AT_ONCE * i + u
                    pe.wait_ge(xT_ready, b + 1)
                    for k in range(KT):
                        last = nc.tensor.matmul(ps_l[0:S, bass.ds(EXPERTS * b, EXPERTS)], xT[u][:, k, :], wr[:, k, :], start=(k == 0), stop=(k == KT - 1))
                    last.then_inc(scored, 1)

            repeat(pe, B // AT_ONCE, turn_of)
            pe.wait_ge(hot_ready, 1)
            flat = hot[:].rearrange("p b e -> p (b e)")
            nc.tensor.matmul(ps_rank[0:S, 0:B * EXPERTS], below[0:S, 0:S], flat, start=True, stop=True).then_inc(ranked, 1)
            nc.tensor.matmul(ps_total[0:S, 0:B * EXPERTS], ones[0:S, 0:S], flat, start=True, stop=True).then_inc(ranked, 1)

        @block.scalar
        def _(act):
            def turn_of(i):
                for u in range(AT_ONCE):
                    b = AT_ONCE * i + u
                    act.wait_ge(turned, b + 1)
                    reused(act, scored, i, u, AT_ONCE)
                    nc.scalar.copy(xT[u][:].rearrange("p k s -> p (k s)"), ps_x[u][:, 0:KT * S]).then_inc(xT_ready, 1)
                    nc.scalar.copy(xn_all[:, bass.ds(b, 1), :].rearrange("p a n -> p (a n)"), x_now[u][:]).then_inc(kept, 1)

            repeat(act, B // AT_ONCE, turn_of)
            act.wait_ge(exp_in, 1)
            nc.scalar.activation(logit[:], logit[:], ACT.Exp).then_inc(exp_out, 1)
            act.wait_ge(kept, B)

        @block.vector
        def _(dve):
            v = nc.vector
            chain = Chain(dve, own)
            def turn_of(i):
                for u in range(AT_ONCE):
                    b = AT_ONCE * i + u
                    reused(dve, turned, i, u, AT_ONCE)
                    reused(dve, kept, i, u, AT_ONCE)
                    normalize(nc, x_now[u][:], rows[:, bass.ds(b, 1), :].rearrange("p a n -> p (a n)"), mean, rstd, b).then_inc(xn_ready, 1)

            repeat(dve, B // AT_ONCE, turn_of)
            dve.wait_ge(scored, B)
            chain.step(v.tensor_copy(logit[:], ps_l[0:S, 0:B * EXPERTS].rearrange("p (b e) -> p b e", e=EXPERTS)))

            def every(a):
                return a[:].unsqueeze(2).to_broadcast([S, B, EXPERTS])

            chain.step(v.tensor_reduce(best[:], logit[:], AX.X, ALU.max))
            v.tensor_tensor(logit[:], logit[:], every(best), ALU.subtract).then_inc(exp_in, 1)
            dve.wait_ge(exp_out, 1)
            chain.step(v.tensor_reduce(inside[:], logit[:], AX.X, ALU.add))
            chain.step(v.reciprocal(keep_gate[:], inside[:]))
            chain.step(v.tensor_scalar(keep_gate[:], keep_gate[:], gate[0:S, 1:2], None, ALU.mult))
            chain.step(v.tensor_reduce(best[:], logit[:], AX.X, ALU.max))
            chain.step(v.tensor_tensor(work[:], logit[:], every(best), ALU.is_lt))
            chain.step(v.scalar_tensor_tensor(work[:], work[:], 2.0 * EXPERTS, iota_s[:], ALU.mult, ALU.add))
            chain.step(v.tensor_reduce(index[:], work[:], AX.X, ALU.min))
            v.tensor_tensor(hot[:], iota_s[:], every(index), ALU.is_equal).then_inc(hot_ready, 1)
            dve.wait_ge(ranked, 2)
            dve.wait_ge(filled, 3)
            chain.step(v.tensor_copy(total[:], ps_total[0:S, 0:B * EXPERTS].rearrange("p (b e) -> p e b", e=EXPERTS)))
            chain.together(*[v.tensor_tensor_scan(upto[:, e, :], zeros[:], total[:, e, :], 0.0, ALU.add, ALU.add)
                             for e in range(EXPERTS)])
            chain.step(v.tensor_tensor(upto[:], upto[:], total[:], ALU.subtract))
            chain.step(v.tensor_tensor(work[:], ps_rank[0:S, 0:B * EXPERTS].rearrange("p (b e) -> p b e", e=EXPERTS),
                                       upto[:].rearrange("p e b -> p b e"), ALU.add))
            chain.step(v.tensor_tensor(work[:], work[:], hot[:], ALU.mult))
            chain.step(v.tensor_reduce(place[:], work[:], AX.X, ALU.add))
            chain.step(v.tensor_scalar(inside[:], place[:], float(CAPACITY), None, ALU.is_le))
            chain.step(v.tensor_tensor(keep_gate[:], keep_gate[:], inside[:], ALU.mult))
            chain.step(v.scalar_tensor_tensor(place[:], index[:], float(CAPACITY), place[:], ALU.mult, ALU.add))
            chain.step(v.tensor_scalar(place[:], place[:], -1.0, None, ALU.add))
            chain.step(v.tensor_tensor(place[:], place[:], inside[:], ALU.mult))
            chain.step(v.tensor_copy(slot_get[:], place[:]))
            chain.step(v.tensor_scalar(beyond[:], inside[:], -1.0, 1.0, ALU.mult, ALU.add))
            chain.step(v.tensor_tensor(beyond[:], beyond[:], token[:], ALU.mult))
            chain.step(v.tensor_tensor(place[:], place[:], beyond[:], ALU.add))
            chain.step(v.tensor_copy(slot_put[:], place[:]))


def capacity_experts(nc, xn_all, slot_put, buffer, result, w1, b1, w2, b2, ident):
    with ExitStack() as ctx:
        def sb(name, shape, dt=F32):
            return ctx.enter_context(nc.sbuf_tensor("cap_" + name, shape, dt))

        def ps(name):
            return ctx.enter_context(nc.psum_tensor("cap_" + name, [P, 512], F32))

        def sem(name):
            return ctx.enter_context(nc.semaphore("cap_" + name))

        w1_sb = [sb(f"w1_{u}", [P, KT, F2]) for u in range(2)]
        w2_sb = [sb(f"w2_{u}", [P, F2C, DIM]) for u in range(2)]
        b2_sb = [sb(f"b2_{u}", [S, DIM]) for u in range(2)]
        b1_sb = sb("b1_sb", [P, EXPERTS, F2C])
        x = [sb(f"f_x{u}", [S, CT, DIM]) for u in range(2)]
        xT = sb("f_xT", [P, KT, CAPACITY])
        mid = sb("f_mid", [P, F2C, CAPACITY])
        y = [sb(f"f_y{u}", [S, CT, DIM]) for u in range(2)]
        ps_x = [ps(f"f_ps_x{u}") for u in range(KT)]
        ps_m = [ps(f"f_ps_m{u}") for u in range(2)]
        ps_y = [ps(f"f_ps_y{u}") for u in range(2)]
        bias_in = sem("f_bias_in")
        dispatched = sem("f_dispatched")
        x_in, loaded, stored = ([sem(f"f_{what}{u}") for u in range(2)] for what in ("x_in", "loaded", "stored"))
        turned, xT_ready, m_done, mid_ready, y_done, y_ready = (sem("f_turned"), sem("f_xT_ready"), sem("f_m_done"),
                                                               sem("f_mid_ready"), sem("f_y_done"), sem("f_y_ready"))
        block = ctx.enter_context(nc.Block())

        def one(dram, e):
            return dram[bass.ds(e, 1)]

        @block.sync
        def _(sp):
            sp.dma_start(b1_sb[:], b1).then_inc(bias_in, 16)

            def load_x(e, u):
                sp.dma_start(x[u][:], buffer[bass.ds(e * CAPACITY, CAPACITY), :].rearrange("(c s) d -> s c d", s=S)).then_inc(x_in[u], 16)

            def load_weights(e, u):
                sp.dma_start(w1_sb[u][:], one(w1, e).rearrange("a p k n -> (a p) k n")).then_inc(loaded[u], 16)
                sp.dma_start(w2_sb[u][:], one(w2, e).rearrange("a p k n -> (a p) k n")).then_inc(loaded[u], 16)
                sp.dma_start(b2_sb[u][:], one(b2, e).rearrange("a n -> (a n)").partition_broadcast(S)).then_inc(loaded[u], 16)

            for u in range(2):
                load_weights(u, u)
            sp.wait_ge(dispatched, 16 * B)
            for u in range(2):
                load_x(u, u)
            with sp.Fori(1, EXPERTS // 2) as i:
                for u in range(2):
                    sp.wait_ge(y_ready, CT * (2 * i + u - 1))
                    load_x(2 * i + u, u)
                    load_weights(2 * i + u, u)
            sp.wait_ge(bias_in, 16)

        @block.gpsimd
        def _(pool):
            for b in range(B):
                nc.gpsimd.indirect_dma_start(buffer, bass.IndirectOffsetOnAxis(ap=slot_put[:, b:b + 1], axis=0),
                                             xn_all[:, b, :], None).then_inc(dispatched, 16)
            pool.wait_ge(dispatched, 16 * B)

            def turn_of(i):
                for u in range(2):
                    e = 2 * i + u
                    pool.wait_ge(y_ready, CT * e + CT)
                    pool.dma_start(result[bass.ds(e * CAPACITY, CAPACITY), :].rearrange("(c s) d -> s c d", s=S), y[u][:]).then_inc(stored[u], 16)

            repeat(pool, EXPERTS // 2, turn_of)
            for u in range(2):
                pool.wait_ge(stored[u], 16 * (EXPERTS // 2))

        @block.tensor
        def _(pe):
            def turn_x(e, u):
                pe.wait_ge(x_in[u], 8 * (e - u) + 16)
                for k in range(KT):
                    for c in range(CT):
                        last = nc.tensor.transpose(ps_x[k][:, c * S:(c + 1) * S], x[u][:, c, k * P:(k + 1) * P], ident[0:S, 0:S])
                    last.then_inc(turned, 1)

            turn_x(0, 0)

            def turns_of(i, more=True):
                for u in range(2):
                    e = 2 * i + u
                    pe.wait_ge(loaded[u], 48 * i + 48)
                    pe.wait_ge(xT_ready, KT * e + KT)
                    for f in range(F2C):
                        n = F2C * e + f
                        if f >= 2:
                            pe.wait_ge(mid_ready, n - 1)
                        else:
                            pe.wait_ge(mid_ready, F2C * e)
                        for k in range(KT):
                            last = nc.tensor.matmul(ps_m[f % 2][:, 0:CAPACITY], w1_sb[u][:, k, f * P:(f + 1) * P], xT[:, k, :],
                                                    start=(k == 0), stop=(k == KT - 1))
                        last.then_inc(m_done, 1)
                    if u == 0 or more:
                        turn_x(e + 1, 1 - u)
                    pe.wait_ge(mid_ready, F2C * e + F2C)
                    for c in range(CT):
                        if c >= 2:
                            pe.wait_ge(y_ready, CT * e + c - 1)
                        else:
                            pe.wait_ge(y_ready, CT * e)
                        for f in range(F2C):
                            last = nc.tensor.matmul(ps_y[c % 2][0:S, 0:DIM], mid[:, f, c * S:(c + 1) * S], w2_sb[u][:, f, :],
                                                    start=(f == 0), stop=(f == F2C - 1))
                        last.then_inc(y_done, 1)

            repeat(pe, EXPERTS // 2 - 1, turns_of)
            turns_of(EXPERTS // 2 - 1, more=False)

        @block.scalar
        def _(act):
            act.wait_ge(bias_in, 16)
            def turn_of(i):
                for u in range(2):
                    e = 2 * i + u
                    act.wait_ge(y_done, CT * e)
                    for f in range(F2C):
                        act.wait_ge(m_done, F2C * e + f + 1)
                        nc.scalar.activation(mid[:, f, :], ps_m[f % 2][:, 0:CAPACITY], ACT.Relu,
                                             bias=b1_sb[:, bass.ds(e, 1), f:f + 1].rearrange("p a n -> p (a n)")).then_inc(mid_ready, 1)

            repeat(act, EXPERTS // 2, turn_of)

        @block.vector
        def _(dve):
            def take_x(e):
                for k in range(KT):
                    dve.wait_ge(turned, KT * e + k + 1)
                    nc.vector.tensor_copy(xT[:, k, :], ps_x[k][:, 0:CAPACITY]).then_inc(xT_ready, 1)

            take_x(0)

            def turns_of(i, more=True):
                for u in range(2):
                    e = 2 * i + u
                    if u == 0 or more:
                        dve.wait_ge(m_done, F2C * e + F2C)
                        take_x(e + 1)
                    dve.wait_ge(stored[u], 16 * i)
                    dve.wait_ge(loaded[u], 48 * i + 48)
                    for c in range(CT):
                        dve.wait_ge(y_done, CT * e + c + 1)
                        nc.vector.tensor_tensor(y[u][:, c, :], ps_y[c % 2][0:S, 0:DIM], b2_sb[u][:], ALU.add).then_inc(y_ready, 1)

            repeat(dve, EXPERTS // 2 - 1, turns_of)
            turns_of(EXPERTS // 2 - 1, more=False)


def finish(nc, rows, result, slot_get, keep_gate, out):
    with ExitStack() as ctx:
        N = 8
        got = [ctx.enter_context(nc.sbuf_tensor(f"got{u}", [S, DIM], F32)) for u in range(N)]
        got_in = [ctx.enter_context(nc.semaphore(f"got_in{u}")) for u in range(N)]
        out_ready = ctx.enter_context(nc.semaphore("out_ready"))
        out_stored = ctx.enter_context(nc.semaphore("out_stored"))
        block = ctx.enter_context(nc.Block())

        @block.gpsimd
        def _(pool):
            for b in range(B):
                if b >= N:
                    pool.wait_ge(out_ready, b - N + 1)
                nc.gpsimd.indirect_dma_start(got[b % N][:], None, result,
                                             bass.IndirectOffsetOnAxis(ap=slot_get[:, b:b + 1], axis=0)).then_inc(got_in[b % N], 16)

        @block.vector
        def _(dve):
            for b in range(B):
                dve.wait_ge(got_in[b % N], 16 * (b // N + 1))
                nc.vector.scalar_tensor_tensor(rows[:, b, :], got[b % N][:], keep_gate[:, b:b + 1], rows[:, b, :],
                                               ALU.mult, ALU.add).then_inc(out_ready, 1)

        @block.sync
        def _(sp):
            def turn_of(b):
                sp.wait_ge(out_ready, b + 1)
                sp.dma_start(out[bass.ds(b, 1)].rearrange("a s d -> (a s) d"),
                             rows[:, bass.ds(b, 1), :].rearrange("p a n -> p (a n)")).then_inc(out_stored, 16)

            repeat(sp, B, turn_of)
            sp.wait_ge(out_stored, 16 * B)


def constants_for_routing(nc, pool, counted, below, iota_e, iota_s, counted_e, counted_s):
    nc.gpsimd.memset(below[:], 1.0).then_inc(counted, 1)
    nc.gpsimd.iota(counted_e[:], pattern=[[0, TILES], [1, EXPERTS]], base=0, channel_multiplier=0).then_inc(counted, 1)
    nc.gpsimd.iota(counted_s[:], pattern=[[0, B], [1, EXPERTS]], base=0, channel_multiplier=0).then_inc(counted, 1)
    pool.wait_ge(counted, 3)
    nc.gpsimd.affine_select(out=below[:], in_=below[:], compare_op=ALU.is_ge, fill=0.0, base=0,
                            pattern=[[1, P]], channel_multiplier=-1).then_inc(counted, 1)
    nc.gpsimd.tensor_copy(iota_e[:], counted_e[:]).then_inc(counted, 1)
    nc.gpsimd.tensor_copy(iota_s[:], counted_s[:]).then_inc(counted, 1)
    pool.wait_ge(counted, 6)


def clear_semaphores(nc):
    numbers = sorted(nc.released_uncleared_semaphores)
    starts = [n for n in numbers if n - 1 not in numbers]
    with nc.Block() as block:

        @block.gpsimd
        def _(pool):
            for first in starts:
                stop = first
                while stop in numbers:
                    stop += 1
                pool.dma_reset(range(first, stop))
                pool.sem_clear(range(first, stop))


def build(nc, x, ctx_rows, ctxT, wqT, wkT, bqk, wvT, bv, woT, bo, head_mask, g_xattn, g_ffn, whhT, wihT, wcT, ctx_b, weT, guT, dnT,
          router, w1, b1, w2, b2, out):
    def dram(name, shape):
        return nc.dram_tensor(name, shape, F32, kind="Internal").ap()

    x1 = dram("x1", (B, S, DIM))
    x2 = dram("x2", (B, S, DIM))
    states = dram("states", (TILES, STEPS, B, GD))
    moe_in = dram("moe_in", (MOE_TILES * P, DIM))
    moe_out = dram("moe_out", (MOE_TILES * P, DIM))
    buffer = dram("buffer", (2 * TOKENS, DIM))
    result = dram("result", (TOKENS, DIM))
    h_rows = moe_in[0:TOKENS].rearrange("(b s) d -> b s d", b=B)

    def pieces(rows):
        return rows.rearrange("r d -> (r d)").rearrange("(p c w) -> c p w", p=P, c=B)

    to_clear = [pieces(moe_in[TOKENS:MOE_TILES * P]), pieces(buffer[0:TOKENS])]

    with ExitStack() as ctx:
        def sb(stack, name, shape, dt=F32, **more):
            return stack.enter_context(nc.sbuf_tensor(name, shape, dt, **more))

        ident = sb(ctx, "ident", [P, P])
        ones = sb(ctx, "ones", [P, P])
        gate = sb(ctx, "gate_ffn", [P, 2])
        gate_x = sb(ctx, "gate_x", [P, 2])
        below = sb(ctx, "below", [P, P])
        iota_e = sb(ctx, "iota_e", [P, TILES, EXPERTS])
        iota_s = sb(ctx, "iota_s", [S, B, EXPERTS])
        whh_in = ctx.enter_context(nc.semaphore("whh_in"))
        cleared_rows = ctx.enter_context(nc.semaphore("cleared_rows"))
        shared_in = ctx.enter_context(nc.semaphore("shared_in"))
        h_in = ctx.enter_context(nc.semaphore("h_in"))
        weights_in = ctx.enter_context(nc.semaphore("att_weights_in"))
        filled = ctx.enter_context(nc.semaphore("const_filled"))
        counted = ctx.enter_context(nc.semaphore("counted"))

        with ExitStack() as mixture:
            stat = sb(mixture, "stat", [P, TILES, NSTAT])
            with ExitStack() as recurrent:
                whh = sb(recurrent, "whh", [P, GC, 3 * GD])
                with ExitStack() as first:
                    rows = sb(first, "rows_x", [S, B, DIM], side="right")
                    mean = sb(first, "mean_x", [S, B], side="right")
                    rstd = sb(first, "rstd_x", [S, B], side="right")
                    with ExitStack() as attending:
                        weights, sources = attention_weights(nc, attending, wqT, wkT, bqk, wvT, bv, woT, bo, head_mask, g_xattn)

                        def load_weights(sp):
                            for tile, source in zip(weights, sources):
                                sp.dma_start(tile[:], source).then_inc(weights_in, 16)

                        with ExitStack() as counting:
                            counted_e = sb(counting, "counted_e", [P, TILES, EXPERTS], I32)
                            counted_s = sb(counting, "counted_s", [S, B, EXPERTS], I32)

                            def make_constants(pool):
                                constants(nc, pool, filled, ident, ones)
                                constants_for_routing(nc, pool, counted, below, iota_e, iota_s, counted_e, counted_s)

                            row_statistics(nc, "x", rows, mean[:], rstd[:], source=x, on_sync=load_weights, on_gpsimd=make_constants)
                        attention(nc, rows, mean, rstd, ctxT, weights, weights_in, x1, ident,
                                  whh, whhT, whh_in, to_clear, cleared_rows)
                    row_statistics(nc, "x1", rows, mean[:], rstd[:])
                    hT = sb(recurrent, "hT", [P, KT, B, S])
                    normalized_rows_out(nc, rows, mean, rstd, h_rows, hT, ident)
                gru(nc, whh, whh_in, wihT, hT, wcT, ctx_b, weT, states, stat, ident)
            weight = sb(mixture, "weight", [P, TILES, 2])
            slot = sb(mixture, "slot", [P, TILES, 2], U32)
            tile_expert = sb(mixture, "tile_expert", [1, MOE_TILES], I32)
            with ExitStack() as experts:
                gu = sb(experts, "gu", [P, EXPERTS + 1, KT, 2 * FF])
                dn = sb(experts, "dn", [P, EXPERTS + 1, FC, DIM])
                h_all = sb(experts, "h_all", [P, TILES, DIM])
                routing(nc, stat, weight, slot, tile_expert, iota_e, below, ones, g_ffn, gate, gu, guT, dn, dnT, shared_in,
                        h_rows, h_all, h_in)
                expert_tiles(nc, moe_in, moe_out, gu, guT, dn, dnT, tile_expert, shared_in, ident, slot, h_all, h_in)
            combine(nc, moe_out, x1, weight, slot, gate, x2)

        clear_semaphores(nc)
        rows = sb(ctx, "rows", [S, B, DIM])
        mean = sb(ctx, "mean", [S, B])
        rstd = sb(ctx, "rstd", [S, B])
        row_statistics(nc, "x2", rows, mean[:], rstd[:], source=x2)
        with ExitStack() as alignment:
            on_path = sb(alignment, "on_path", [BAND, DSTEPS, P], BF16)
            with ExitStack() as tables:
                table = sb(tables, "table", [P, DSTEPS, BAND])
                distances(nc, rows, mean, rstd, ctxT, table, ones, ident)
                align(nc, table, on_path, ident)
            add_aligned(nc, rows, ctx_rows, on_path, g_xattn, gate_x)
        row_statistics(nc, "x3", rows, mean[:], rstd[:])
        with ExitStack() as last:
            xn_all = sb(last, "xn_all", [S, B, DIM])
            slot_put = sb(last, "slot_put", [S, B], U32)
            slot_get = sb(last, "slot_get", [S, B], U32)
            keep_gate = sb(last, "keep_gate", [S, B])
            route_once(nc, rows, mean, rstd, router, below, ones, ident, iota_s, xn_all, slot_put, slot_get, keep_gate, gate)
            capacity_experts(nc, xn_all, slot_put, buffer, result, w1, b1, w2, b2, ident)
            finish(nc, rows, result, slot_get, keep_gate, out)


def layouts(i):
    import numpy as np

    def tiles(w):
        return w.T.reshape(-1, P, w.shape[0]).transpose(1, 0, 2)

    att, ffn, moe = "L0_xattn_", "L0_ffn_", "L1_ffn_"
    ctxT = np.zeros((B, P, KT, KVP), i["ctx_1024"].dtype)
    ctxT[..., 0:KV] = i["ctx_1024"].reshape(B, KV, KT, P).transpose(0, 3, 2, 1)
    ctx_rows = np.zeros((B, BANDS * BAND, DIM), i["ctx_1024"].dtype)
    ctx_rows[:, 0:KV] = i["ctx_1024"]
    ctx_rows = ctx_rows.reshape(B, BANDS, BAND, DIM)[:, :, ::-1].transpose(0, 2, 1, 3)
    bqk = np.stack([i[att + "bq"], i[att + "bk"]]).reshape(2, KT, P).transpose(2, 0, 1)
    head_mask = np.repeat(np.eye(P // HD, dtype=np.float32) * -HD ** -0.5, HD, axis=0)

    def with_shared(name):
        return np.concatenate([i[ffn + name], i[ffn + "shared_" + name][None]])

    gate_up = np.concatenate([with_shared("gate_w"), with_shared("up_w")], 1)
    return {
        "x": i["x"], "ctx_rows": ctx_rows, "ctxT": ctxT,
        "wqT": tiles(i[att + "Wq"]), "wkT": tiles(i[att + "Wk"]), "bqk": bqk,
        "wvT": tiles(i[att + "Wv"]), "bv": i[att + "bv"], "woT": tiles(i[att + "Wo"]), "bo": i[att + "bo"],
        "head_mask": head_mask,
        "g_xattn": i["g_xattn"], "g_ffn": i["g_ffn"],
        "whhT": tiles(i[ffn + "gru_w_hh"]), "wihT": tiles(i[ffn + "gru_w_ih"]), "wcT": tiles(i[ffn + "ctx_w"]),
        "ctx_b": i[ffn + "ctx_b"], "weT": tiles(i[ffn + "expr_w"]),
        "guT": gate_up.reshape(EXPERTS + 1, 2 * FF, KT, P).transpose(3, 0, 2, 1),
        "dnT": with_shared("down_w").reshape(EXPERTS + 1, DIM, FC, P).transpose(3, 0, 2, 1),
        "router": i[moe + "router_w"].reshape(KT, P, EXPERTS).transpose(1, 0, 2),
        "w1": i[moe + "w1"].reshape(EXPERTS, KT, P, F2).transpose(0, 2, 1, 3),
        "b1": i[moe + "b1"].reshape(EXPERTS, F2C, P).transpose(2, 0, 1),
        "w2": i[moe + "w2"].reshape(EXPERTS, F2C, P, DIM).transpose(0, 2, 1, 3),
        "b2": i[moe + "b2"],
    }


def kernel(**inputs):
    import numpy as np
    import concourse.bacc as bacc
    from concourse.bass_utils import run_bass_kernel_spmd

    nc = bacc.Bacc("TRN2", target_bir_lowering=False, num_devices=1)
    arrays, args = {}, []
    for name, a in layouts({k: np.asarray(v) for k, v in inputs.items()}).items():
        a = np.ascontiguousarray(a)
        arrays[f"in_{name}"] = a
        args.append(nc.dram_tensor(f"in_{name}", a.shape, mybir.dt.from_np(a.dtype), kind="ExternalInput").ap())
    args.append(nc.dram_tensor("out_x", (B, S, DIM), F32, kind="ExternalOutput").ap())
    build(nc, *args)
    result = run_bass_kernel_spmd(nc, [arrays], core_ids=[0])
    return result.results[0]["out_x"]
```
